# Optimizing a Trainium2 kernel written in Bass

```python
import numpy as np
import jax
import jax.numpy as jnp

def _softmax(x, axis=-1):
    return jax.nn.softmax(x, axis=axis)

def _gelu(x):
    return jax.nn.gelu(x, approximate=True)

def _silu(x):
    return jax.nn.silu(x)

def _sigmoid(x):
    return jax.nn.sigmoid(x)

def _layernorm(x, axis=-1, eps=1e-05):
    m = jnp.mean(x, axis=axis, keepdims=True)
    v = jnp.var(x, axis=axis, keepdims=True)
    return (x - m) / jnp.sqrt(v + eps)

def _scatter_add(tgt, idx, src, axis=0):
    return tgt.at[idx].add(src)

def _segment_sum(src, seg, n):
    return jax.ops.segment_sum(src, seg, n)
kernel_name = 'mk_gnn_resnorm_d4_gnn_r64_c579d6'

def setup_inputs(seed: int=0):
    np.random.seed(seed)
    _w = jnp.asarray

    def _rec_inputs():
        import jax
        import jax.numpy as jnp
        _gk = jax.random.key(seed)
        x = -0.000202 + 1 * jax.random.normal(jax.random.fold_in(_gk, 1), (100000, 64), jnp.float32)
        src = jax.random.randint(jax.random.fold_in(_gk, 2), (25000,), 0, 100000, jnp.int32)
        dst = jnp.minimum((100000 * jax.random.uniform(jax.random.fold_in(_gk, 3), (25000,)) ** 2.0).astype(jnp.int32), 99999)
        _o = jnp.argsort(dst, stable=True)
        src = src[_o]
        dst = dst[_o]
        edge_attr_2 = -0.000414295 + 0.999828 * jax.random.normal(jax.random.fold_in(_gk, 12), (25000, 2), jnp.float32)
        return (x, src, dst, edge_attr_2)
    x, src, dst, edge_attr_2 = _rec_inputs()

    def _L0_gnn_setup():
        import jax, jax.numpy as jnp
        import numpy as np
        N_NODES = 100000
        N_EDGES = 15625
        DIM = 64
        key = jax.random.key(seed)
        k1, k2, k3, k4, k5, k6 = jax.random.split(key, 6)
        h = jax.random.normal(k1, (N_NODES, DIM), dtype=jnp.float32)
        proj_cosim = jax.random.normal(k2, (DIM, DIM), dtype=jnp.float32) * np.sqrt(2.0 / DIM)
        W_ffn = jax.random.normal(k3, (DIM, DIM), dtype=jnp.float32) * np.sqrt(1.0 / DIM)
        b_ffn = jax.random.normal(k4, (DIM,), dtype=jnp.float32) * 0.01
        src = jax.random.randint(k5, (N_EDGES,), 0, N_NODES, dtype=jnp.int32)
        dst = jax.random.randint(k6, (N_EDGES,), 0, N_NODES, dtype=jnp.int32)
        return {'h': h, 'proj_cosim': proj_cosim, 'W_ffn': W_ffn, 'b_ffn': b_ffn, 'src': src, 'dst': dst}
    _L0_gnn_all = _L0_gnn_setup()
    _L0_gnn_in = {k: v for k, v in _L0_gnn_all.items() if k in ('proj_cosim', 'W_ffn', 'b_ffn')}
    del _L0_gnn_all

    def _L1_gnn_setup():
        import jax, jax.numpy as jnp
        import numpy as np
        K = 3
        SLOPE = 0.01
        N_NODES = 50000
        N_EDGES = 12500
        D_IN = 64
        D_OUT = 64
        E_DIM = 2

        def _moments(z_e, Wm_list):
            moms = [z_e]
            mu = z_e.mean(axis=0, keepdims=True)
            for k in range(2, K + 1):
                mk = jnp.mean((z_e - mu) ** k, axis=0)
                mk = jnp.sign(mk) * jnp.abs(mk) ** (1.0 / k)
                moms.append(mk @ Wm_list[k - 2].T)
            return moms
        key = jax.random.key(seed)
        ks = jax.random.split(key, 10)
        s = 0.1
        return {'h': jax.random.normal(ks[0], (N_NODES, D_IN), dtype=jnp.float32), 'e': jax.random.normal(ks[1], (N_EDGES, E_DIM), dtype=jnp.float32), 'src': jax.random.randint(ks[2], (N_EDGES,), 0, N_NODES), 'dst': jax.random.randint(ks[3], (N_EDGES,), 0, N_NODES), 'W_fc': jax.random.normal(ks[4], (D_OUT, D_IN), dtype=jnp.float32) * s, 'W_attn': jax.random.normal(ks[5], (1, 2 * D_OUT * K + E_DIM), dtype=jnp.float32) * s, 'W_edge': jax.random.normal(ks[6], (E_DIM, E_DIM), dtype=jnp.float32) * s, 'W_e2n': jax.random.normal(ks[7], (D_OUT, E_DIM), dtype=jnp.float32) * s, 'W_m1': jax.random.normal(ks[8], (D_OUT, D_OUT), dtype=jnp.float32) * s, 'W_m2': jax.random.normal(ks[9], (D_OUT, D_OUT), dtype=jnp.float32) * s}
    _L1_gnn_all = _L1_gnn_setup()
    _L1_gnn_in = {k: v for k, v in _L1_gnn_all.items() if k in ('W_fc', 'W_attn', 'W_edge', 'W_e2n', 'W_m1', 'W_m2')}
    del _L1_gnn_all

    def _L2_gnn_setup():
        import jax, jax.numpy as jnp
        import numpy as np
        DIM = 64
        HEADS = 4
        N_NODES = 50000
        N_EDGES = 12500
        NEG_SLOPE = 0.2
        key = jax.random.key(seed)
        k1, k2, k3, k4, k5 = jax.random.split(key, 5)
        meta_x = jax.random.normal(k1, (N_NODES, DIM), dtype=jnp.float32)
        meta_edge_index = jax.random.randint(k2, (2, N_EDGES), 0, N_NODES, dtype=jnp.int64)
        glorot = float(np.sqrt(2.0 / (DIM + HEADS * DIM)))
        W = jax.random.normal(k3, (DIM, HEADS * DIM), dtype=jnp.float32) * glorot
        att_src = jax.random.normal(k4, (1, HEADS, DIM), dtype=jnp.float32) * glorot
        att_dst = jax.random.normal(k5, (1, HEADS, DIM), dtype=jnp.float32) * glorot
        bias = jnp.zeros((DIM,), dtype=jnp.float32)
        return {'meta_x': meta_x, 'meta_edge_index': meta_edge_index, 'W': W, 'att_src': att_src, 'att_dst': att_dst, 'bias': bias}
    _L2_gnn_all = _L2_gnn_setup()
    _L2_gnn_in = {k: v for k, v in _L2_gnn_all.items() if k in ('W', 'att_src', 'att_dst', 'bias')}
    del _L2_gnn_all

    def _L3_gnn_setup():
        import jax, jax.numpy as jnp
        import numpy as np
        N_NODES = 100000
        N_EDGES = 25000
        IN_CH = 64
        OUT_CH = 64
        key = jax.random.key(seed)
        ks = jax.random.split(key, 6)
        x = jax.random.normal(ks[0], (N_NODES, IN_CH), dtype=jnp.float32)
        edge_index = jax.random.randint(ks[1], (2, N_EDGES), 0, N_NODES, dtype=jnp.int64)
        W1 = jax.random.normal(ks[2], (2 * IN_CH, OUT_CH), dtype=jnp.float32) * (1.0 / np.sqrt(2 * IN_CH))
        b1 = jnp.zeros((OUT_CH,), dtype=jnp.float32)
        W2 = jax.random.normal(ks[3], (OUT_CH, OUT_CH), dtype=jnp.float32) * (1.0 / np.sqrt(OUT_CH))
        b2 = jnp.zeros((OUT_CH,), dtype=jnp.float32)
        return {'x': x, 'edge_index': edge_index, 'W1': W1, 'b1': b1, 'W2': W2, 'b2': b2}
    _L3_gnn_all = _L3_gnn_setup()
    _L3_gnn_in = {k: v for k, v in _L3_gnn_all.items() if k in ('W1', 'b1', 'W2', 'b2')}
    del _L3_gnn_all
    return {'x': x, 'src': src, 'dst': dst, 'edge_attr_2': edge_attr_2, 'L0_gnn_proj_cosim': _L0_gnn_in['proj_cosim'], 'L0_gnn_W_ffn': _L0_gnn_in['W_ffn'], 'L0_gnn_b_ffn': _L0_gnn_in['b_ffn'], 'L1_gnn_W_fc': _L1_gnn_in['W_fc'], 'L1_gnn_W_attn': _L1_gnn_in['W_attn'], 'L1_gnn_W_edge': _L1_gnn_in['W_edge'], 'L1_gnn_W_e2n': _L1_gnn_in['W_e2n'], 'L1_gnn_W_m1': _L1_gnn_in['W_m1'], 'L1_gnn_W_m2': _L1_gnn_in['W_m2'], 'L2_gnn_W': _L2_gnn_in['W'], 'L2_gnn_att_src': _L2_gnn_in['att_src'], 'L2_gnn_att_dst': _L2_gnn_in['att_dst'], 'L2_gnn_bias': _L2_gnn_in['bias'], 'L3_gnn_W1': _L3_gnn_in['W1'], 'L3_gnn_b1': _L3_gnn_in['b1'], 'L3_gnn_W2': _L3_gnn_in['W2'], 'L3_gnn_b2': _L3_gnn_in['b2']}

def reference(x, src, dst, edge_attr_2, L0_gnn_proj_cosim, L0_gnn_W_ffn, L0_gnn_b_ffn, L1_gnn_W_fc, L1_gnn_W_attn, L1_gnn_W_edge, L1_gnn_W_e2n, L1_gnn_W_m1, L1_gnn_W_m2, L2_gnn_W, L2_gnn_att_src, L2_gnn_att_dst, L2_gnn_bias, L3_gnn_W1, L3_gnn_b1, L3_gnn_W2, L3_gnn_b2):
    import jax
    import jax.numpy as jnp

    def _L0_gnn_ref(h, proj_cosim, W_ffn, b_ffn, src, dst):
        import jax, jax.numpy as jnp
        import numpy as np
        N_NODES = 100000
        N_EDGES = 15625
        DIM = 64
        n_nodes = h.shape[0]
        h_src = h[src]
        h_dst = h[dst]
        scale = jnp.linalg.norm(h_src) * jnp.linalg.norm(h_dst) + 1e-06
        cosim = h_src * h_dst / scale
        cosim = jax.nn.relu(cosim @ proj_cosim)
        gate = jnp.exp(jnp.clip(cosim.sum(-1, keepdims=True), -5.0, 5.0))
        src_diff = jax.ops.segment_sum(h_src - h_dst, dst, num_segments=n_nodes)
        h_diff = jax.ops.segment_sum(src_diff[src] * gate, dst, num_segments=n_nodes)
        out = jax.nn.relu(h_diff @ W_ffn.T + b_ffn)
        return out

    def _L1_gnn_ref(h, e, src, dst, W_fc, W_attn, W_edge, W_e2n, W_m1, W_m2):
        import jax, jax.numpy as jnp
        import numpy as np
        K = 3
        SLOPE = 0.01
        N_NODES = 50000
        N_EDGES = 12500
        D_IN = 64
        D_OUT = 64
        E_DIM = 2

        def _moments(z_e, Wm_list):
            moms = [z_e]
            mu = z_e.mean(axis=0, keepdims=True)
            for k in range(2, K + 1):
                mk = jnp.mean((z_e - mu) ** k, axis=0)
                mk = jnp.sign(mk) * jnp.abs(mk) ** (1.0 / k)
                moms.append(mk @ Wm_list[k - 2].T)
            return moms
        N = h.shape[0]
        D = W_fc.shape[0]
        z = h @ W_fc.T
        z_src = z[src]
        z_dst = z[dst]
        ex = e @ W_edge.T
        wm = [W_m1, W_m2]
        src_m = _moments(z_src, wm)
        dst_m = _moments(z_dst, wm)
        wa = W_attn[0]
        blk = [wa[i * D:(i + 1) * D] for i in range(2 * K)]
        w_e = wa[2 * K * D:]
        a = z_src @ blk[0] + z_dst @ blk[K] + ex @ w_e
        for k in range(1, K):
            a = a + src_m[k] @ blk[k] + dst_m[k] @ blk[K + k]
        att = jnp.where(a > 0, a, SLOPE * a)
        m = jax.ops.segment_max(att, dst, num_segments=N)
        expv = jnp.exp(att - m[dst])
        denom = jax.ops.segment_sum(expv, dst, num_segments=N)
        w = expv / denom[dst]
        ez = ex @ W_e2n.T
        msg = w[:, None] * (z_src + ez)
        return jax.ops.segment_sum(msg, dst, num_segments=N)

    def _L2_gnn_ref(meta_x, meta_edge_index, W, att_src, att_dst, bias):
        import jax, jax.numpy as jnp
        import numpy as np
        DIM = 64
        HEADS = 4
        N_NODES = 50000
        N_EDGES = 12500
        NEG_SLOPE = 0.2
        N = meta_x.shape[0]
        loops = jnp.arange(N, dtype=meta_edge_index.dtype)
        edge = jnp.concatenate([meta_edge_index, jnp.stack([loops, loops])], axis=1)
        src, dst = (edge[0], edge[1])
        x = (meta_x @ W).reshape(N, HEADS, DIM)
        a_src = jnp.sum(x * att_src, axis=-1)
        a_dst = jnp.sum(x * att_dst, axis=-1)
        logits = a_src[src] + a_dst[dst]
        logits = jax.nn.leaky_relu(logits, NEG_SLOPE)
        seg_max = jax.ops.segment_max(logits, dst, num_segments=N)
        ex = jnp.exp(logits - seg_max[dst])
        seg_sum = jax.ops.segment_sum(ex, dst, num_segments=N)
        alpha = ex / (seg_sum[dst] + 1e-16)
        msg = x[src] * alpha[:, :, None]
        out = jax.ops.segment_sum(msg, dst, num_segments=N)
        return out.mean(axis=1) + bias

    def _L3_gnn_ref(x, edge_index, W1, b1, W2, b2):
        import jax, jax.numpy as jnp
        import numpy as np
        N_NODES = 100000
        N_EDGES = 25000
        IN_CH = 64
        OUT_CH = 64
        src = edge_index[0]
        dst = edge_index[1]
        x_i = x[dst]
        x_j = x[src]
        edge_features = jnp.concatenate([x_i, x_j - x_i], axis=-1)
        h = jax.nn.relu(edge_features @ W1 + b1)
        edge_messages = h @ W2 + b2
        out = jax.ops.segment_max(edge_messages, dst, num_segments=x.shape[0])
        return jnp.where(jnp.isfinite(out), out, jnp.zeros_like(out))
    edge_index = jnp.stack([src, dst])
    x = _layernorm(x + _L0_gnn_ref(x, L0_gnn_proj_cosim, L0_gnn_W_ffn, L0_gnn_b_ffn, src, dst), axis=-1)
    x = _layernorm(x + _L1_gnn_ref(x, edge_attr_2, src, dst, L1_gnn_W_fc, L1_gnn_W_attn, L1_gnn_W_edge, L1_gnn_W_e2n, L1_gnn_W_m1, L1_gnn_W_m2), axis=-1)
    x = _layernorm(x + _L2_gnn_ref(x, edge_index, L2_gnn_W, L2_gnn_att_src, L2_gnn_att_dst, L2_gnn_bias), axis=-1)
    x = _layernorm(x + _L3_gnn_ref(x, edge_index, L3_gnn_W1, L3_gnn_b1, L3_gnn_W2, L3_gnn_b2), axis=-1)
    return x

_drawn_inputs = setup_inputs


def setup_inputs(seed=0):
    import zlib

    import numpy as np

    out = dict(_drawn_inputs(seed))
    spreads = {'L2_gnn_bias': (0.0, 0.1), 'L3_gnn_b1': (0.0, 0.31), 'L3_gnn_b2': (0.0, 0.1)}
    factors = {'edge_attr_2': 8.0,
     'L0_gnn_proj_cosim': 64.0,
     'L0_gnn_b_ffn': 8.0,
     'L1_gnn_W_attn': 3.453,
     'L1_gnn_W_edge': 8.0,
     'L1_gnn_W_e2n': 8.0,
     'L1_gnn_W_m1': 51.824,
     'L1_gnn_W_m2': 64.0,
     'L2_gnn_att_src': 3.618,
     'L2_gnn_att_dst': 21.873}
    for name, (base, spread) in spreads.items():
        noise = np.random.default_rng([zlib.crc32(name.encode()), seed]).standard_normal(out[name].shape)
        drawn = base * np.exp(spread * noise) if base else spread * noise
        out[name] = jnp.asarray(drawn.astype(out[name].dtype))
    for name, factor in factors.items():
        out[name] = (out[name] * factor).astype(out[name].dtype)
    return out
```

```python
import numpy as np
from contextlib import ExitStack
import concourse.bass as bass
from concourse import mybir

N, D, E = 100000, 64, 25000
SE = 1024
NS = (E + SE - 1) // SE
EP = NS * SE
LASTC = E - (NS - 1) * SE
HW = 512
NG = N // SE
RC = EP // 128
HEADS = 4
EPS = 1e-5
BIG = 3e38
FMAX = 3.4028234663852886e38
FAR = 1 << 20

F32, I32, BF16 = mybir.dt.float32, mybir.dt.int32, mybir.dt.bfloat16
A = mybir.AluOpType
ACT = mybir.ActivationFunctionType
AX = mybir.AxisListType.X


def supers(eng, body):
    with eng.Fori(0, NS // 2) as i:
        body(2 * i, 0, i + 1, 2 * i + 1)
        body(2 * i + 1, 1, i + 1, 2 * i + 2)
    body(NS - 1, 0, NS // 2 + 1, NS)


def settle(eng, sem):
    eng.sem_inc(sem, 1)


def per_row(t):
    return t.rearrange("p (j o) -> p j o", o=1).to_broadcast([128, 8, D])


def rows(t):
    return t.rearrange("p (j f) -> p j f", f=D)


def build(nc, a, out):
    ctx = ExitStack()
    with ctx:
        def sb(name, shape, dt=F32):
            return ctx.enter_context(nc.sbuf_tensor(name, shape, dt))

        def dram(name, shape, dt=F32):
            return nc.dram_tensor(name, shape, dt, kind="Internal").ap()

        class Sems:
            def __init__(self, prefix):
                self.prefix, self.made = prefix, {}

            def __call__(self, name):
                if name not in self.made:
                    self.made[name] = nc.alloc_semaphore(name=self.prefix + name)
                return self.made[name]

            def done(self):
                nc.clear_and_free_semaphores(list(self.made.values()))
                nc.all_engine_barrier()

        rank = dram("rank", [N, 1], I32)
        table = [dram(f"table{k}", [2 * EP, D]) for k in range(4)]
        logit1_d = dram("logit1_d", [EP])
        weight1_d = dram("weight1_d", [EP])
        logit2_d = dram("logit2_d", [2 * HEADS, EP])
        weight2_d = dram("weight2_d", [2 * HEADS, EP])

        XD = sb("XD", [128, NS * HW])
        XS = sb("XS", [128, NS * HW])
        SAME = sb("SAME", [128, NS * HW], BF16)
        MORE = sb("MORE", [128, NS * HW], BF16)
        src_i = sb("src_i", [128, 8 * NS], I32)
        dst_i = sb("dst_i", [128, 8 * NS], I32)
        seg_i = sb("seg_i", [128, 8 * NS], I32)
        row_i = sb("row_i", [128, 8 * NS], I32)
        look_i = sb("look_i", [128, 8 * NS], I32)
        t_i = sb("t_i", [128, 8 * NS], I32)
        win = sb("win", [128, 2, 16], I32)
        GA = sb("GA", [128, 2, HW])
        GB = sb("GB", [128, 2, HW])
        rank_t = sb("rank_t", [128, 8 * NS], I32)
        work = sb("work", [128, 8 * HW])
        wk = [work[:, i * HW:(i + 1) * HW] for i in range(8)]
        FS = sb("FS", [128, HW])
        junk = sb("junk", [128, HW])
        small = sb("small", [128, 64])
        car = sb("car", [128, 1])
        stat = sb("stat", [128, 8, NS])
        red = sb("red", [128, 32])

        ident = sb("ident", [128, 128])
        ones = sb("ones", [128, 128])
        center = sb("center", [128, 128])
        average = sb("average", [128, 128])
        total = sb("total", [128, 128])
        fold = sb("fold", [128, 128])
        proj = sb("proj", [128, 128])
        wffn = sb("wffn", [128, 128])
        wfc = sb("wfc", [128, 128])
        chain = sb("chain", [128, 128])
        wh = [sb(f"wh{h}", [128, 128]) for h in range(HEADS)]
        w1d = sb("w1d", [128, 128])
        w1s = sb("w1s", [128, 128])
        w2 = sb("w2", [128, 128])
        eprj = sb("eprj", [128, 128])
        one_l = sb("one_l", [128, 6])
        two_l = sb("two_l", [128, 32])
        vec = sb("vec", [128, 16])
        eat = sb("eat", [128, HW])
        P = [ctx.enter_context(nc.psum_tensor(f"P{i}", [128, HW], F32)) for i in range(8)]
        bff, relub, bias2, bias2c, b1, b2, eps_t, one_t = (vec[:, i:i + 1] for i in range(8))
        bias_row = sb("bias_row", [128, D])
        inv_scale, mu_s, mu_d, shift = (vec[:, i:i + 1] for i in range(8, 12))
        grad = sb("grad", [128, 4])
        row_same = sb("row_same", [128, RC])
        row_more = sb("row_more", [128, RC])
        row_neg = sb("row_neg", [128, RC])
        row_last = sb("row_last", [128, RC])
        ends = sb("ends", [128, 2 * HEADS])
        carry = sb("carry", [HEADS, 512])
        carry_in = sb("carry_in", [128, HEADS])

        S = Sems("su_")
        wl = GA[:, :, :].rearrange("p a c -> p (a c)")
        wl2 = GB[:, :, :].rearrange("p a c -> p (a c)")
        Wsb, Att, Wfc_n, Blk, Wed, We2, Wm, Asum = (wl[:, 0:256], wl[:, 256:768], wl[0:64, 768:896], wl[0:64, 900:906],
                                                    wl[0:2, 908:910], wl2[0:2, 0:64], wl2[:, 64:192], wl2[:, 192:320])
        Wmn = work[0:64, 2048:2304].rearrange("p (k c) -> p k c", k=2)
        W1a, IW, CW, we_t, Pr = wl2[:, 320:448], wl2[:, 448:576], wl2[:, 576:704], wl[0:2, 912:913], wl2[:, 704:960]

        with nc.Block() as block:
            blocks = [(proj, "proj"), (wffn, "wffnT"), (wfc, "wfcT"), (w1s, "w1b"), (w2, "w2"), (W1a, "w1a")]
            loads = [0]

            @block.sync
            def _(sp):
                def ld(dst, src):
                    sp.dma_start(dst, src).then_inc(S("load"), 16)
                    loads[0] += 16
                sp.wait_ge(S("zero"), 1)
                for h in range(2):
                    lo, hi = h * 64, h * 64 + 64
                    for t, name in blocks:
                        ld(t[lo:hi, lo:hi], a[name])
                    for k in range(HEADS):
                        ld(wh[k][lo:hi, lo:hi], a["w2l"][:, k * D:(k + 1) * D])
                    ld(Wsb[lo:hi, :], a["w2l"])
                    for i, name in enumerate(["b_ffn", "bias2", "b1", "b2"]):
                        ld(vec[lo:hi, (0, 2, 4, 5)[i]:(0, 2, 4, 5)[i] + 1], a[name].rearrange("(p o) -> p o", o=1))
                    ld(Wfc_n[:, h * 64:h * 64 + 64], a["wfc"])
                ld(Att, a["att"].rearrange("(o c) -> o c", o=1).to_broadcast([128, 512]))
                ld(bias_row[:, :], a["bias2"].rearrange("(o c) -> o c", o=1).to_broadcast([128, D]))
                ld(Blk, a["blkT"])
                ld(Wed, a["wedge"])
                ld(We2, a["we2nT"])
                ld(we_t, a["we"])
                for k in range(2):
                    for h in range(2):
                        ld(Wmn[:, k, h * 64:h * 64 + 64], a[f"wm{k + 1}"])
                for k, (t, off) in enumerate([(row_same, 0), (row_neg, 1), (row_more, 2)]):
                    ld(t[:, :].bitcast(I32), a["dst_pad"][off:off + EP].rearrange("(p c) -> p c", p=128))
                for i, t in enumerate([ident, center, average, total, fold, ones]):
                    ld(t[:, :], a["const"][:, i * 128:(i + 1) * 128])
                ld(src_i[:, :], a["src_l"])
                ld(dst_i[:, :], a["dst_l"])
                ld(seg_i[:, :], a["next_l"])
                sp.wait_ge(S("load"), loads[0])
                sp.sem_inc(S("loaded"), 1)
                sp.wait_ge(S("fill"), 2)
                sp.dma_start(rank.rearrange("(p c) o -> p (c o)", p=80), XS[0:80, 0:N // 80].bitcast(I32)).then_inc(S("init"), 16)
                sp.dma_start(table[0][EP:2 * EP, :].rearrange("(p c) f -> p (c f)", p=128), XD[:, :]).then_inc(S("init"), 16)
                sp.wait_ge(S("init"), 32)

            @block.gpsimd
            def _(pool):
                pool.iota(row_i[:, :].rearrange("p (s j) -> p s j", j=8), [[SE, NS], [1, 8]], base=0,
                          channel_multiplier=8).then_inc(S("iota"), 1)
                pool.memset(XS[0:80, 0:N // 80].bitcast(I32), -1).then_inc(S("fill"), 1)
                pool.memset(XD[:, :], 0.0).then_inc(S("fill"), 1)

            @block.vector
            def _(dve):
                step = [0]

                def link(ins):
                    step[0] += 1
                    ins.then_inc(S("dve"), 1)
                    dve.wait_ge(S("dve"), step[0])

                for t in [proj, wffn, wfc, w1s, w2, eprj, *wh]:
                    dve.memset(t[:, :], 0.0)
                for t in [one_l, two_l, car, eat]:
                    dve.memset(t[:, :], 0.0)
                dve.memset(stat[:, :, :], 0.0)
                dve.memset(W1a, 0.0)
                link(dve.memset(eps_t, EPS))
                link(dve.memset(one_t, 1.0))
                dve.nop().then_inc(S("zero"), 1)
                dve.wait_ge(S("loaded"), 1)
                dve.wait_ge(S("iota"), 1)
                link(dve.tensor_tensor(t_i[:, :], dst_i[:, :], seg_i[:, :], A.is_equal))
                link(dve.scalar_tensor_tensor(seg_i[:, :], t_i[:, :], float(FAR), dst_i[:, :], A.mult, A.add))
                link(dve.tensor_scalar(dst_i[:, :], dst_i[:, :], float(N - 1), None, A.min))
                for t in (row_same, row_more):
                    link(dve.tensor_tensor(t[:, :], t[:, :].bitcast(I32), row_neg[:, :].bitcast(I32), A.is_equal))
                link(dve.tensor_scalar(row_neg[:, :], row_same[:, :], -1.0, BIG, A.add, A.mult))
                link(dve.tensor_scalar(row_last[:, :], row_more[:, :], 0.0, None, A.is_equal))
                link(dve.tensor_scalar(relub, bff, 0.0, None, A.max))
                link(dve.tensor_tensor(Asum[:, 0:64], Wsb[:, 0:64], Wsb[:, 64:128], A.add))
                link(dve.tensor_tensor(Asum[:, 64:128], Wsb[:, 128:192], Wsb[:, 192:256], A.add))
                link(dve.memset(Wm, 0.0))
                link(dve.tensor_tensor(Wm[0:64, 0:64], Asum[0:64, 0:64], Asum[0:64, 64:128], A.add))
                link(dve.tensor_tensor(Wm[64:128, 64:128], Asum[64:128, 0:64], Asum[64:128, 64:128], A.add))
                link(dve.scalar_tensor_tensor(IW, Wm, 1.0 / HEADS, ident[:, :], A.mult, A.add))
                for side in range(2):
                    link(dve.tensor_tensor(Pr, Wsb, Att[:, side * 256:(side + 1) * 256], A.mult))
                    link(dve.tensor_reduce(small[:, side * 4:side * 4 + 4], Pr.rearrange("p (h d) -> p h d", h=HEADS), AX, A.add))
                link(dve.tensor_tensor(small[:, 8:12], small[:, 0:4], small[:, 4:8], A.add))
                for h in range(2):
                    lo, hi = h * 64, h * 64 + 64
                    cols = lambda base: two_l[lo:hi, base + h:base + h + 7:2]
                    link(dve.tensor_copy(cols(0), small[lo:hi, 0:4]))
                    link(dve.tensor_copy(cols(16), small[lo:hi, 4:8]))
                    link(dve.tensor_copy(cols(24), small[lo:hi, 8:12]))
                link(dve.tensor_tensor(w1d[:, :], W1a, w1s[:, :], A.subtract))
                dve.nop().then_inc(S("folded"), 1)
                dve.wait_ge(S("pe"), 1)
                link(dve.tensor_copy(CW, P[0][:, 0:128]))
                for h in range(2):
                    lo, hi = h * 64, h * 64 + 64
                    for c in range(2):
                        link(dve.tensor_copy(one_l[lo:hi, 2 * c + h:2 * c + h + 1], P[1][lo:hi, (0, 3)[c]:(0, 3)[c] + 1]))
                    link(dve.tensor_copy(eprj[lo:lo + 2, lo:hi], P[2][lo:lo + 2, 0:64]))
                    link(dve.tensor_copy(one_l[lo:lo + 2, 4 + h:5 + h], P[2][lo:lo + 2, 64:65]))
                link(dve.tensor_copy(bias2c, P[3][:, 0:1]))
                for k in range(2):
                    link(dve.tensor_copy(grad[:, k:k + 3:2], P[3][:, 4 + 2 * k:6 + 2 * k]))
                dve.nop().then_inc(S("cw"), 1)
                dve.wait_ge(S("pe"), 2)
                link(dve.tensor_copy(chain[:, :], P[4][:, 0:128]))
                link(dve.tensor_reduce(red[:, 0:1], bias_row[:, :], AX, A.add))
                link(dve.tensor_scalar(red[:, 1:2], red[:, 0:1], 1.0 / D, None, A.mult))
                link(dve.tensor_scalar(bias_row[:, :], bias_row[:, :], red[:, 1:2], None, A.subtract))

            @block.tensor
            def _(pe):
                pe.wait_ge(S("folded"), 1)
                pe.matmul(P[0][:, 0:128], center[:, :], IW, start=True, stop=True)
                pe.matmul(P[1][:, 0:6], Wfc_n, Blk, start=True, stop=True)
                for h in range(2):
                    pe.matmul(P[2][64 * h:64 * h + 2, 0:64], Wed, We2, start=True, stop=True)
                    pe.matmul(P[2][64 * h:64 * h + 2, 64:65], Wed, we_t, start=True, stop=True)
                pe.matmul(P[3][:, 0:1], center[:, :], bias2, start=True, stop=True)
                for k in range(2):
                    last = pe.matmul(P[3][:, 4 + 2 * k:6 + 2 * k], Wmn[:, k, :], Blk[:, 1 + k:5 + k:3], start=True, stop=True)
                last.then_inc(S("pe"), 1)
                pe.wait_ge(S("cw"), 1)
                pe.transpose(P[5][:, 0:128], CW, ident[:, :]).then_inc(S("pet"), 1)
                pe.wait_ge(S("cwt"), 1)
                pe.matmul(P[4][:, 0:128], wk[0][:, 0:128], center[:, :], start=True, stop=True).then_inc(S("pe"), 1)

            @block.scalar
            def _(act):
                act.wait_ge(S("pet"), 1)
                act.activation(wk[0][:, 0:128], P[5][:, 0:128], ACT.Copy).then_inc(S("cwt"), 1)

        S.done()

        M = Sems("mk_")
        with nc.Block() as block:
            cols = lambda par: work[:, par * 1024:par * 1024 + HW + 2].bitcast(I32)

            @block.sync
            def _(sp):
                def load(s, par, k, n):
                    sp.wait_ge(M(f"free{par}"), k)
                    for h in range(2):
                        sp.dma_start(cols(par)[64 * h:64 * h + 64, :],
                                     a["dst_pad"][bass.ds(s * SE + h * HW, HW + 2)].rearrange("(o c) -> o c", o=1)
                                     .to_broadcast([64, HW + 2])).then_inc(M(f"load{par}"), 16)
                supers(sp, load)

            @block.vector
            def _(dve):
                for par in range(2):
                    dve.nop().then_inc(M(f"free{par}"), 1)

                def masks(s, par, k, n):
                    dve.wait_ge(M(f"load{par}"), k * 32)
                    c = cols(par)
                    dve.tensor_tensor(SAME[:, bass.ds(s * HW, HW)], c[:, 1:HW + 1], c[:, 0:HW], A.is_equal).then_inc(M("one"), 1)
                    dve.tensor_tensor(MORE[:, bass.ds(s * HW, HW)], c[:, HW:0:-1], c[:, HW + 1:1:-1], A.is_equal).then_inc(M("two"), 1)
                    dve.wait_ge(M("one"), n)
                    dve.wait_ge(M("two"), n)
                    dve.nop().then_inc(M(f"free{par}"), 1)
                supers(dve, masks)

        M.done()

        def at(t, s):
            return t[:, bass.ds(s * HW, HW)]

        def gather_rounds(pool, S, buffers, looks, tables):
            def body(s, par, k, n):
                pool.wait_ge(S(f"slot_free{par}"), k)
                for b, look in enumerate(looks):
                    pool.tensor_copy(win[:, par, b * 8:b * 8 + 8], look[:, bass.ds(s * 8, 8)]).then_inc(S("window"), 1)
                pool.wait_ge(S("window"), n * len(looks))
                settle(pool, S("settled"))
                for b, (buf, t) in enumerate(zip(buffers, tables)):
                    for j in range(8):
                        pool.indirect_dma_start(buf[:, par, j * D:(j + 1) * D], None, t,
                                                bass.IndirectOffsetOnAxis(ap=win[:, par, b * 8 + j:b * 8 + j + 1], axis=0)
                                                ).then_inc(S(f"gathered{par}"), 16)
            supers(pool, body)

        def transpose4(pe, dst, src):
            for q in range(4):
                ins = pe.transpose(dst[:, q * 128:(q + 1) * 128], src[:, q * 128:(q + 1) * 128], ident[:, :])
            return ins

        def seg_scan(dve, S, n, V, F, m, op0, op1):
            dve.tensor_tensor_scan(F[0:64, :], m[0:64, :], V[0:64, :], car[0:64, :], op0, op1).then_inc(S("scan0"), 1)
            dve.wait_ge(S("scan0"), n)
            dve.tensor_copy(car[64:128, :], F[0:64, HW - 1:HW]).then_inc(S("mid_carry"), 1)
            dve.wait_ge(S("mid_carry"), n)
            dve.tensor_tensor_scan(F[64:128, :], m[64:128, :], V[64:128, :], car[64:128, :], op0, op1).then_inc(S("scan1"), 1)
            dve.wait_ge(S("scan1"), n)
            dve.tensor_copy(car[0:64, :], F[64:128, HW - 1:HW]).then_inc(S("next_carry"), 1)
            dve.wait_ge(S("next_carry"), n)

        U, SQ, DEV, X, EMB = wk[4], wk[5], wk[6], wk[7], wk[2]
        BACK = [wk[5], wk[6]]

        def norm_pe(pe, S, n):
            pe.wait_ge(S("u"), n)
            pe.matmul(P[2][:, :], center[:, :], U, start=True, stop=True).then_inc(S("centred"), 1)
            pe.wait_ge(S("square"), n)
            pe.matmul(P[3][:, :], average[:, :], SQ, start=True, stop=True).then_inc(S("variance"), 1)
            pe.wait_ge(S("x"), n)
            transpose4(pe, P[4], X).then_inc(S("x_em"), 1)

        def norm_act(act, S, n, emb=EMB):
            act.wait_ge(S("centred"), n)
            act.activation(SQ, P[2][:, :], ACT.Square).then_inc(S("square"), 1)
            act.wait_ge(S("variance"), n)
            act.activation(DEV, P[3][:, :], ACT.Sqrt, bias=eps_t).then_inc(S("deviation"), 1)
            act.wait_ge(S("x_em"), n)
            act.wait_ge(S("emb_free"), n)
            act.activation(emb, P[4][:, :], ACT.Copy).then_inc(S("emb"), 1)

        def norm_dve(dve, S, s, n, keep=True):
            dve.wait_ge(S("deviation"), n)
            dve.reciprocal(DEV, DEV).then_inc(S("rstd"), 1)
            dve.wait_ge(S("rstd"), n)
            dve.tensor_tensor(X, P[2][:, :], DEV, A.mult).then_inc(S("x"), 1)
            if keep:
                dve.wait_ge(S("x"), n)
                dve.scalar_tensor_tensor(at(XD, s), at(MORE, s), 0.0, X[:, ::-1], A.is_equal, A.mult).then_inc(S("kept"), 1)

        def store_tables(sp, S, table_k):
            sp.sem_inc(S("emb_free"), 1)

            def body(s, par, k, n):
                sp.wait_ge(S("emb"), n)
                sp.dma_start(table_k[bass.ds(s * SE, SE), :].rearrange("(p j) f -> p (j f)", p=128), EMB).then_inc(S("stored"), 16)
                sp.wait_ge(S("stored"), n * 16)
                sp.sem_inc(S("emb_free"), 1)
            supers(sp, body)

        def pass_back(dve, S):
            dve.memset(car[:, :], 0.0).then_inc(S("car0"), 1)
            dve.wait_ge(S("car0"), 1)
            for par in range(2):
                dve.sem_inc(S(f"back_free{par}"), 1)

            def body(s, par, k, n):
                dve.wait_ge(S(f"back_free{par}"), k)
                settle(dve, S("settled"))
                B = BACK[par]
                for h in (1, 0):
                    lo, hi = 64 * h, 64 * h + 64
                    other = slice(64 - lo, 128 - lo)
                    x, more = (at(t, (NS - 1) - s)[lo:hi, :] for t in (XD, MORE))
                    dve.tensor_tensor_scan(B[lo:hi, ::-1], more, x, car[lo:hi, :], A.mult, A.add).then_inc(S(f"back{h}"), 1)
                    dve.wait_ge(S(f"back{h}"), n)
                    dve.tensor_copy(car[other, :], B[lo:hi, 0:1]).then_inc(S(f"back_carry{h}"), 1)
                    dve.wait_ge(S(f"back_carry{h}"), n)
            supers(dve, body)

        def keep_back(act, S, s, par, n):
            act.wait_ge(S("back_carry0"), n)
            act.activation(at(XD, (NS - 1) - s), BACK[par], ACT.Copy).then_inc(S(f"back_free{par}"), 1)

        def dense_pe(pe, S, n):
            pe.wait_ge(S("vt"), n)
            for w, p in ((center, P[6]), (chain, P[7])):
                for q in range(4):
                    ins = pe.matmul(p[:, q * 128:(q + 1) * 128], VT[:, q * 128:(q + 1) * 128], w[:, :], start=True, stop=True)
                ins.then_inc(S("dense_mm"), 1)

        VT, DQ, Y, O1, O2, O3 = wk[0], wk[1], wk[3], wk[4], wk[5], wk[6]

        def sm(k):
            return small[:, k * 8:k * 8 + 8]

        def dense_act(act, S, n, nodes):
            act.wait_ge(S("dense_mm"), 2 * n)
            act.activation(DQ, P[6][:, :], ACT.Square).then_inc(S("sq1"), 1)
            act.wait_ge(S("ss1"), n)
            act.activation(sm(1), sm(0), ACT.Sqrt, scale=1.0 / D, bias=eps_t).then_inc(S("sd1"), 1)
            act.wait_ge(S("ss2"), n)
            act.activation(sm(3), sm(2), ACT.Sqrt, scale=1.0 / D, bias=eps_t).then_inc(S("sd2"), 1)
            act.wait_ge(S("y"), n)
            act.activation(DQ, Y, ACT.Square).then_inc(S("sq2"), 1)
            act.wait_ge(S("ss3"), n)
            act.activation(sm(5), sm(4), ACT.Sqrt, scale=1.0 / D, bias=eps_t).then_inc(S("sd3"), 1)
            if nodes:
                act.wait_ge(S("ss4"), n)
                act.activation(sm(7), sm(6), ACT.Sqrt, scale=1.0 / D, bias=eps_t).then_inc(S("sd4"), 1)

        def twice(dve, S, n, ss, sd, ss_next, names):
            dve.reciprocal(sd, sd).then_inc(S(names[0]), 1)
            dve.wait_ge(S(names[0]), n)
            dve.tensor_tensor(ss_next, ss, sd, A.mult).then_inc(S(names[1]), 1)
            dve.wait_ge(S(names[1]), n)
            dve.tensor_tensor(ss_next, ss_next, sd, A.mult).then_inc(S(names[2]), 1)

        def dense_dve(dve, S, n, nodes):
            dve.wait_ge(S("sq1"), n)
            dve.tensor_reduce(sm(0), rows(DQ), AX, A.add).then_inc(S("ss1"), 1)
            dve.wait_ge(S("sd1"), n)
            twice(dve, S, n, sm(0), sm(1), sm(2), ("r1", "t2", "ss2"))
            dve.wait_ge(S("sd2"), n)
            dve.reciprocal(sm(3), sm(3)).then_inc(S("r2"), 1)
            dve.wait_ge(S("r2"), n)
            dve.tensor_tensor(sm(3), sm(3), sm(1), A.mult).then_inc(S("r12"), 1)
            dve.wait_ge(S("r12"), n)
            dve.tensor_tensor(rows(Y), rows(P[7][:, :]), per_row(sm(3)), A.mult).then_inc(S("y0"), 1)
            if not nodes:
                dve.wait_ge(S("o_free"), n)
                dve.tensor_tensor(rows(O1), rows(P[6][:, :]), per_row(sm(1)), A.mult).then_inc(S("o1"), 1)
                dve.tensor_tensor(rows(O2), rows(P[6][:, :]), per_row(sm(3)), A.mult).then_inc(S("o2"), 1)
            dve.wait_ge(S("y0"), n)
            dve.tensor_tensor(rows(Y), rows(Y), bias_row[:, :].rearrange("p (o f) -> p o f", o=1).to_broadcast([128, 8, D]),
                              A.add).then_inc(S("y"), 1)
            dve.wait_ge(S("sq2"), n)
            dve.tensor_reduce(sm(4), rows(DQ), AX, A.add).then_inc(S("ss3"), 1)
            dve.wait_ge(S("sd3"), n)
            if not nodes:
                dve.reciprocal(sm(5), sm(5)).then_inc(S("r3"), 1)
                dve.wait_ge(S("r3"), n)
                dve.tensor_tensor(rows(O3), rows(Y), per_row(sm(5)), A.mult).then_inc(S("o3"), 1)
            else:
                twice(dve, S, n, sm(4), sm(5), sm(6), ("r3", "t4", "ss4"))
                dve.wait_ge(S("sd4"), n)
                dve.reciprocal(sm(7), sm(7)).then_inc(S("r4"), 1)
                dve.wait_ge(S("r4"), n)
                dve.tensor_tensor(sm(7), sm(7), sm(5), A.mult).then_inc(S("r34"), 1)
                dve.wait_ge(S("r34"), n)
                dve.wait_ge(S("o_free"), n)
                dve.tensor_tensor(rows(O1), rows(Y), per_row(sm(7)), A.mult).then_inc(S("o1"), 1)

        def gather_pe(pe, S):
            for par in range(2):
                pe.sem_inc(S(f"slot_free{par}"), 1)
            pe.sem_inc(S("fm_kept"), 1)

            def body(s, par, k, n):
                pe.wait_ge(S(f"gathered{par}"), k * 128)
                pe.wait_ge(S("fm_kept"), n)
                transpose4(pe, P[0], GA[:, par, :]).then_inc(S("fm"), 1)
                pe.wait_ge(S("fm"), n)
                pe.sem_inc(S(f"slot_free{par}"), 1)
            supers(pe, body)

        def load_attributes(sp, S, s):
            for h in range(2):
                sp.dma_start(eat[64 * h:64 * h + 2, :], a["attr"][:, bass.ds(s * SE + h * HW, HW)]).then_inc(S("eat"), 16)

        def load_weights(sp, S, w, t, s, name="weights"):
            for h in range(2):
                sp.dma_start(t[64 * h:64 * h + 64, :], w[bass.ds(s * SE + h * HW, HW)].rearrange("(o c) -> o c", o=1)
                             .to_broadcast([64, HW])).then_inc(S(name), 16)

        def softmax_rows(block, S, logits, weights, K, slope, own):
            view = lambda i: work[:, i * 1024:i * 1024 + K * RC].rearrange("p (h c) -> p h c", h=K)
            L, T, R, X = (view(i) for i in range(4))
            LO, XO = (g[:, :, :].rearrange("p a c -> p (a c)")[:, 0:K * RC].rearrange("p (h c) -> p h c", h=K) for g in (GA, GB))
            all_ = lambda m: m[:, :].rearrange("p (o c) -> p o c", o=1).to_broadcast([128, K, RC])

            @block.sync
            def _(sp):
                for t, lo in ((L, 0), (LO, K)) if own else ((L, 0),):
                    for h in range(K):
                        src = logits[lo + h, :] if own else logits
                        sp.dma_start(t[:, h, :], src.rearrange("(p c) -> p c", p=128)).then_inc(S("load"), 16)
                sp.wait_ge(S("weights"), 1)
                for t, lo in ((X, 0), (XO, K)) if own else ((X, 0),):
                    for h in range(K):
                        dst = weights[lo + h, :] if own else weights
                        sp.dma_start(dst.rearrange("(p c) -> p c", p=128), t[:, h, :]).then_inc(S("store"), 16)
                sp.wait_ge(S("store"), 16 * K * (1 + own))

            rounds = [0]

            @block.vector
            def _(dve):
                step = [0]

                def link(ins):
                    step[0] += 1
                    ins.then_inc(S("dve"), 1)
                    dve.wait_ge(S("dve"), step[0])

                def scan(src, dst, mask, op0, op1, start, down=False):
                    rounds[0] += 1
                    r = rounds[0]
                    d = (lambda x: x[:, ::-1]) if down else (lambda x: x)
                    for h in range(K):
                        link(dve.tensor_tensor_scan(d(dst[:, h, :]), d(mask[:, :]), d(src[:, h, :]), start, op0, op1))
                    edge = 0 if down else RC - 1
                    link(dve.tensor_copy(ends[:, 0:K], dst[:, :, edge]))
                    link(dve.tensor_reduce(red[:, 0:1], mask[:, :], AX, A.min))
                    link(dve.tensor_copy(ends[:, HEADS:HEADS + K], red[:, 0:1].to_broadcast([128, K])))
                    dve.nop().then_inc(S("ends"), 1)
                    dve.wait_ge(S("ends_row"), r)
                    link(dve.tensor_copy(carry[0:K, 0:256], P[0][0:K, 0:256]))
                    link(dve.memset(carry[0:K, 256:385], start))
                    into = carry[0:K, 256:384] if down else carry[0:K, 257:385]
                    link(dve.tensor_tensor_scan(d(into), d(carry[0:K, 128:256]), d(carry[0:K, 0:128]), start, op0, op1))
                    dve.nop().then_inc(S("carry"), 1)
                    dve.wait_ge(S("carry_in"), r)
                    link(dve.tensor_copy(carry_in[:, 0:K], P[1][:, 0:K]))
                    for h in range(K):
                        link(dve.tensor_tensor_scan(d(dst[:, h, :]), d(mask[:, :]), d(src[:, h, :]), carry_in[:, h:h + 1], op0, op1))

                def spread(t, dst):
                    link(dve.tensor_tensor(t, t, all_(row_last), A.mult))
                    scan(t, dst, row_more, A.mult, A.add, 0.0, down=True)

                dve.wait_ge(S("load"), 16 * K * (1 + own))
                if not own:
                    link(dve.tensor_scalar(L, L, shift, None, A.add))
                link(dve.scalar_tensor_tensor(L, L, slope, L, A.mult, A.max))
                scan(L, T, row_neg, A.add, A.max, -BIG)
                spread(T, R)
                if own:
                    link(dve.scalar_tensor_tensor(LO, LO, slope, LO, A.mult, A.max))
                    link(dve.tensor_tensor(R, R, LO, A.max))
                    link(dve.tensor_tensor(LO, LO, R, A.subtract))
                link(dve.tensor_tensor(L, L, R, A.subtract))
                dve.nop().then_inc(S("shifted"), 1)
                dve.wait_ge(S("exp"), 1 + own)
                scan(X, T, row_same, A.mult, A.add, 0.0)
                spread(T, R)
                if own:
                    link(dve.tensor_tensor(R, R, XO, A.add))
                    link(dve.tensor_scalar(R, R, 1e-16, float(HEADS), A.add, A.mult))
                link(dve.reciprocal(R, R))
                link(dve.tensor_tensor(X, X, R, A.mult))
                if own:
                    link(dve.tensor_tensor(XO, XO, R, A.mult))
                dve.nop().then_inc(S("weights"), 1)

            @block.scalar
            def _(act):
                act.wait_ge(S("shifted"), 1)
                act.activation(X, L, ACT.Exp).then_inc(S("exp"), 1)
                if own:
                    act.activation(XO, LO, ACT.Exp).then_inc(S("exp"), 1)

            @block.tensor
            def _(pe):
                for r, down in enumerate((False, True, False, True)):
                    pe.wait_ge(S("ends"), r + 1)
                    pe.transpose(P[0][0:K, 0:128], ends[:, 0:K], ident[:, :])
                    pe.transpose(P[0][0:K, 128:256], ends[:, HEADS:HEADS + K], ident[:, :]).then_inc(S("ends_row"), 1)
                    pe.wait_ge(S("carry"), r + 1)
                    src = carry[0:K, 257:385] if down else carry[0:K, 256:384]
                    pe.transpose(P[1][:, 0:K], src, ident[0:K, 0:K]).then_inc(S("carry_in"), 1)

        SA = Sems("a_")
        V_, F_ = wk[7], FS[:, :]
        with nc.Block() as block:
            @block.gpsimd
            def _(pool):
                gather_rounds(pool, SA, [GA, GB], [src_i, dst_i], [a["x"], a["x"]])

            @block.tensor
            def _(pe):
                for par in range(2):
                    pe.sem_inc(SA(f"slot_free{par}"), 1)

                def body(s, par, k, n):
                    pe.wait_ge(SA(f"gathered{par}"), k * 256)
                    transpose4(pe, P[0], GA[:, par, :])
                    transpose4(pe, P[1], GB[:, par, :]).then_inc(SA("ends_fm"), 1)
                    dense_pe(pe, SA, n)
                    pe.wait_ge(SA("ends_fm"), n)
                    pe.sem_inc(SA(f"slot_free{par}"), 1)
                    pe.wait_ge(SA("scan1"), n)
                    transpose4(pe, P[4], F_).then_inc(SA("x_em"), 1)
                    pe.wait_ge(SA("sum_d"), n)
                    pe.wait_ge(SA("o2"), n)
                    pe.wait_ge(SA("emb"), n)
                supers(pe, body)

            @block.scalar
            def _(act):
                def body(s, par, k, n):
                    act.wait_ge(SA("ends_fm"), n)
                    act.activation(at(XS, s), P[0][:, :], ACT.Copy).then_inc(SA("xs"), 1)
                    act.activation(at(XD, s), P[1][:, :], ACT.Copy).then_inc(SA("xd"), 1)
                    act.activation(VT, P[0][:, :], ACT.Identity, bias=relub).then_inc(SA("vt"), 1)
                    last = isinstance(s, int)
                    hi, c = (64, LASTC) if last else (128, HW)
                    act.activation(junk[0:hi, 0:c], P[0][0:hi, 0:c], ACT.Square,
                                   accum_out=stat[0:hi, 0, bass.ds(s, 1)]).then_inc(SA("sum_s"), 1)
                    act.wait_ge(SA("sum_s"), n)
                    act.activation(junk[0:hi, 0:c], P[1][0:hi, 0:c], ACT.Square,
                                   accum_out=stat[0:hi, 1, bass.ds(s, 1)]).then_inc(SA("sum_d"), 1)
                    dense_act(act, SA, n, False)
                    act.wait_ge(SA("x_em"), n)
                    act.wait_ge(SA("emb_free"), n)
                    act.activation(EMB, P[4][:, :], ACT.Copy).then_inc(SA("emb"), 1)
                supers(act, body)

            @block.vector
            def _(dve):
                def body(s, par, k, n):
                    dve.wait_ge(SA("xd"), n)
                    dve.tensor_tensor(V_, at(XS, s), at(XD, s), A.subtract).then_inc(SA("v"), 1)
                    dve.wait_ge(SA("v"), n)
                    seg_scan(dve, SA, n, V_, F_, at(SAME, s), A.mult, A.add)
                    dense_dve(dve, SA, n, False)
                supers(dve, body)

            @block.sync
            def _(sp):
                for name in ("emb_free", "o_free"):
                    sp.sem_inc(SA(name), 1)

                def body(s, par, k, n):
                    for name, t in (("o1", 1), ("o2", 2), ("o3", 3)):
                        sp.wait_ge(SA(name), n)
                        sp.dma_start(table[t][bass.ds(s * SE + EP, SE), :].rearrange("(p j) f -> p (j f)", p=128),
                                     (None, O1, O2, O3)[t]).then_inc(SA("stored_o"), 16)
                    sp.wait_ge(SA("emb"), n)
                    sp.dma_start(table[0][bass.ds(s * SE, SE), :].rearrange("(p j) f -> p (j f)", p=128), EMB).then_inc(SA("stored"), 16)
                    sp.wait_ge(SA("stored_o"), n * 48)
                    sp.sem_inc(SA("o_free"), 1)
                    sp.wait_ge(SA("stored"), n * 16)
                    sp.sem_inc(SA("emb_free"), 1)
                supers(sp, body)

        SA.done()

        SN = Sems("n_")
        XN = GB
        with nc.Block() as block:
            @block.gpsimd
            def _(pool):
                def scatter(s, par, k, n):
                    pool.tensor_copy(win[:, par, 0:8], seg_i[:, bass.ds(s * 8, 8)]).then_inc(SN("window"), 1)
                    pool.tensor_copy(win[:, par, 8:16], row_i[:, bass.ds(s * 8, 8)]).then_inc(SN("window"), 1)
                    pool.wait_ge(SN("window"), n * 2)
                    settle(pool, SN("settled"))
                    for j in range(8):
                        pool.indirect_dma_start(rank, bass.IndirectOffsetOnAxis(ap=win[:, par, j:j + 1], axis=0),
                                                win[:, par, 8 + j:9 + j], None, bounds_check=N - 1, oob_is_err=False
                                                ).then_inc(SN(f"scattered{par}"), 16)

                def scattered(par, k):
                    pool.wait_ge(SN(f"scattered{par}"), 128 * k)

                def look(s, par, k, n):
                    pool.tensor_copy(win[:, par, 0:8], src_i[:, bass.ds(s * 8, 8)]).then_inc(SN("window_look"), 1)
                    pool.wait_ge(SN("window_look"), n)
                    settle(pool, SN("settled"))
                    for j in range(8):
                        pool.indirect_dma_start(win[:, par, 8 + j:9 + j], None, rank,
                                                bass.IndirectOffsetOnAxis(ap=win[:, par, j:j + 1], axis=0)
                                                ).then_inc(SN(f"looked{par}"), 16)

                def looked(s, par, k, n):
                    pool.wait_ge(SN(f"looked{par}"), 128 * k)
                    pool.tensor_copy(rank_t[:, bass.ds(s * 8, 8)], win[:, par, 8:16]).then_inc(SN("rank_t"), 1)
                    pool.wait_ge(SN("rank_t"), n)

                with pool.Fori(0, NS // 2) as i:
                    scatter(2 * i, 0, i + 1, 2 * i + 1)
                    scatter(2 * i + 1, 1, i + 1, 2 * i + 2)
                    scattered(0, i + 1)
                    scattered(1, i + 1)
                scatter(NS - 1, 0, NS // 2 + 1, NS)
                scattered(0, NS // 2 + 1)
                with pool.Fori(0, NS // 2) as i:
                    look(2 * i, 0, i + 1, 2 * i + 1)
                    look(2 * i + 1, 1, i + 1, 2 * i + 2)
                    looked(2 * i, 0, i + 1, 2 * i + 1)
                    looked(2 * i + 1, 1, i + 1, 2 * i + 2)
                look(NS - 1, 0, NS // 2 + 1, NS)
                looked(NS - 1, 0, NS // 2 + 1, NS)

            @block.sync
            def _(sp):
                def load(par, k, at_row):
                    sp.wait_ge(SN(f"xn_free{par}"), k)
                    sp.dma_start(XN[:, par, :], a["x"][bass.ds(at_row, SE), :].rearrange("(p j) f -> p (j f)", p=128)
                                 ).then_inc(SN(f"xn{par}"), 16)

                def store(n, at_row):
                    sp.wait_ge(SN("o1"), n)
                    sp.dma_start(out[bass.ds(at_row, SE), :].rearrange("(p j) f -> p (j f)", p=128), O1).then_inc(SN("stored"), 16)
                    sp.wait_ge(SN("stored"), n * 16)
                    sp.sem_inc(SN("o_free"), 1)
                sp.sem_inc(SN("o_free"), 1)
                load(0, 1, 0)
                with sp.Fori(0, NG // 2) as i:
                    load(1, i + 1, (2 * i + 1) * SE)
                    store(2 * i + 1, 2 * i * SE)
                    load(0, i + 2, (2 * i + 2) * SE)
                    store(2 * i + 2, (2 * i + 1) * SE)
                load(1, NG // 2 + 1, N - SE)
                store(NG, (NG - 1) * SE)
                store(NG + 1, N - SE)

            def groups(eng, body):
                with eng.Fori(0, NG // 2) as i:
                    body(0, i + 1, 2 * i + 1)
                    body(1, i + 1, 2 * i + 2)
                body(0, NG // 2 + 1, NG)
                body(1, NG // 2 + 1, NG + 1)

            @block.tensor
            def _(pe):
                for par in range(2):
                    pe.sem_inc(SN(f"xn_free{par}"), 1)

                def body(par, k, n):
                    pe.wait_ge(SN(f"xn{par}"), k * 16)
                    transpose4(pe, P[0], XN[:, par, :]).then_inc(SN("xt"), 1)
                    dense_pe(pe, SN, n)
                    pe.wait_ge(SN("xt"), n)
                    pe.sem_inc(SN(f"xn_free{par}"), 1)
                    pe.wait_ge(SN("sq1"), n)
                    pe.wait_ge(SN("y0"), n)
                groups(pe, body)

            @block.scalar
            def _(act):
                def body(par, k, n):
                    act.wait_ge(SN("xt"), n)
                    act.activation(VT, P[0][:, :], ACT.Identity, bias=relub).then_inc(SN("vt"), 1)
                    dense_act(act, SN, n, True)
                groups(act, body)

            @block.vector
            def _(dve):
                groups(dve, lambda par, k, n: dense_dve(dve, SN, n, True))

        SN.done()

        SB = Sems("b_")
        with nc.Block() as block:
            @block.vector
            def _(dve):
                step = [0]

                def link(ins):
                    step[0] += 1
                    ins.then_inc(SB("dve"), 1)
                    dve.wait_ge(SB("dve"), step[0])

                link(dve.tensor_scalar(t_i[:, :], row_i[:, :], float(EP + 1), None, A.add))
                link(dve.scalar_tensor_tensor(look_i[:, :], rank_t[:, :], 0.0, t_i[:, :], A.is_lt, A.mult))
                link(dve.tensor_tensor(t_i[:, :], look_i[:, :], rank_t[:, :], A.add))
                link(dve.tensor_copy(look_i[:, :], t_i[:, :]))
                link(dve.tensor_reduce(red[:, 0:2], stat[:, 0:2, :], AX, A.add))
                dve.nop().then_inc(SB("sums"), 1)
                dve.wait_ge(SB("norms"), 1)
                link(dve.tensor_tensor(red[:, 4:5], red[:, 2:3], red[:, 3:4], A.mult))
                link(dve.tensor_scalar(red[:, 5:6], red[:, 4:5], 1e-6, None, A.add))
                link(dve.reciprocal(inv_scale, red[:, 5:6]))
                link(dve.memset(car[:, :], 0.0))

            @block.tensor
            def _(pe):
                pe.wait_ge(SB("sums"), 1)
                pe.matmul(P[0][:, 0:2], ones[:, :], red[:, 0:2], start=True, stop=True).then_inc(SB("all"), 1)

            @block.scalar
            def _(act):
                act.wait_ge(SB("all"), 1)
                act.activation(red[:, 2:4], P[0][:, 0:2], ACT.Sqrt).then_inc(SB("norms"), 1)

        SB.done()

        S0 = Sems("c_")
        PR, RL, GT, OUT0, V = wk[0], wk[1], wk[3], wk[1], wk[5]
        with nc.Block() as block:
            @block.gpsimd
            def _(pool):
                gather_rounds(pool, S0, [GA], [look_i], [table[0]])

            @block.vector
            def _(dve):
                def body(s, par, k, n):
                    dve.tensor_tensor(PR, at(XS, s), at(XD, s), A.mult).then_inc(S0("product"), 1)
                    dve.wait_ge(S0("logit"), n)
                    dve.tensor_scalar(GT, P[5][:, :], -5.0, 5.0, A.max, A.min).then_inc(S0("clipped"), 1)
                    dve.wait_ge(S0("gate"), n)
                    dve.wait_ge(S0("sums_fm"), n)
                    dve.tensor_tensor(V, P[0][:, :], GT, A.mult).then_inc(S0("v"), 1)
                    dve.wait_ge(S0("v"), n)
                    seg_scan(dve, S0, n, V, FS[:, :], at(SAME, s), A.mult, A.add)
                    dve.wait_ge(S0("ffn"), n)
                    dve.tensor_tensor(U, at(XD, s), OUT0, A.add).then_inc(S0("u"), 1)
                    norm_dve(dve, S0, s, n)
                supers(dve, body)

            @block.tensor
            def _(pe):
                for par in range(2):
                    pe.sem_inc(S0(f"slot_free{par}"), 1)

                def body(s, par, k, n):
                    pe.wait_ge(S0("product"), n)
                    pe.matmul(P[1][:, :], proj[:, :], PR, start=True, stop=True).then_inc(S0("cos"), 1)
                    pe.wait_ge(S0("relu"), n)
                    pe.matmul(P[5][:, :], total[:, :], RL, start=True, stop=True).then_inc(S0("logit"), 1)
                    pe.wait_ge(S0(f"gathered{par}"), k * 128)
                    transpose4(pe, P[0], GA[:, par, :]).then_inc(S0("sums_fm"), 1)
                    pe.wait_ge(S0("sums_fm"), n)
                    pe.sem_inc(S0(f"slot_free{par}"), 1)
                    pe.wait_ge(S0("scan1"), n)
                    pe.matmul(P[1][:, :], wffn[:, :], FS[:, :], start=True, stop=True).then_inc(S0("ffn_mm"), 1)
                    norm_pe(pe, S0, n)
                supers(pe, body)

            @block.scalar
            def _(act):
                def body(s, par, k, n):
                    act.wait_ge(S0("cos"), n)
                    act.activation(RL, P[1][:, :], ACT.Relu, scale=inv_scale).then_inc(S0("relu"), 1)
                    act.wait_ge(S0("clipped"), n)
                    act.activation(GT, GT, ACT.Exp).then_inc(S0("gate"), 1)
                    act.wait_ge(S0("ffn_mm"), n)
                    act.activation(OUT0, P[1][:, :], ACT.Relu, bias=bff).then_inc(S0("ffn"), 1)
                    norm_act(act, S0, n)
                supers(act, body)

            @block.sync
            def _(sp):
                store_tables(sp, S0, table[1])

        S0.done()

        S1 = Sems("d_")
        with nc.Block() as block:
            @block.gpsimd
            def _(pool):
                gather_rounds(pool, S1, [GA], [look_i], [table[1]])

            @block.vector
            def _(dve):
                pass_back(dve, S1)
                dve.wait_ge(S1("back_free0"), NS // 2 + 2)
                dve.wait_ge(S1("back_free1"), NS // 2 + 1)

                def sums(s, par, k, n):
                    hi, c = (64, LASTC) if isinstance(s, int) else (128, HW)
                    dve.tensor_reduce(stat[0:hi, 3, bass.ds(s, 1)], at(XD, s)[0:hi, 0:c], AX, A.add)
                supers(dve, sums)

            @block.tensor
            def _(pe):
                gather_pe(pe, S1)

            @block.scalar
            def _(act):
                def body(s, par, k, n):
                    keep_back(act, S1, s, par, n)
                    act.wait_ge(S1("fm"), n)
                    hi, c = (64, LASTC) if isinstance(s, int) else (128, HW)
                    act.activation(junk[0:hi, 0:c], P[0][0:hi, 0:c], ACT.Copy,
                                   accum_out=stat[0:hi, 2, bass.ds(s, 1)]).then_inc(S1("sum_s"), 1)
                    act.activation(at(XS, s), P[0][:, :], ACT.Copy).then_inc(S1("fm_kept"), 1)
                supers(act, body)

        S1.done()

        S2 = Sems("e_")
        with nc.Block() as block:
            @block.vector
            def _(dve):
                step = [0]

                def link(ins):
                    step[0] += 1
                    ins.then_inc(S2("dve"), 1)
                    dve.wait_ge(S2("dve"), step[0])

                link(dve.tensor_reduce(red[:, 0:2], stat[:, 2:4, :], AX, A.add))
                dve.nop().then_inc(S2("sums"), 1)
                dve.wait_ge(S2("folded"), 1)
                link(dve.tensor_copy(red[:, 2:4], P[0][:, 0:2]))
                dve.nop().then_inc(S2("means"), 1)
                dve.wait_ge(S2("mu"), 1)
                link(dve.tensor_scalar(vec[:, 9:11], P[1][:, 0:2], -1.0 / E, None, A.mult))
                dve.nop().then_inc(S2("mu_ready"), 1)

                def body(s, par, k, n):
                    hi, c = (64, LASTC) if isinstance(s, int) else (128, HW)
                    for side, (ps, mu) in enumerate(((P[2], mu_s), (P[3], mu_d))):
                        dve.wait_ge(S2(f"square{side}"), n)
                        dve.scalar_tensor_tensor(junk[0:hi, 0:c], ps[0:hi, 0:c], mu[0:hi, :], wk[side][0:hi, 0:c], A.add, A.mult,
                                                 accum_out=stat[0:hi, 5 + 2 * side, bass.ds(s, 1)]).then_inc(S2(f"cube{side}"), 1)
                        dve.wait_ge(S2(f"cube{side}"), n)
                supers(dve, body)
                dve.wait_ge(S2("squares"), 1)
                link(dve.tensor_reduce(red[:, 4:8], stat[:, 4:8, :], AX, A.add))
                dve.nop().then_inc(S2("moment_sums"), 1)
                dve.wait_ge(S2("moments"), 1)
                m = red[:, 8:12]
                link(dve.tensor_scalar(m, P[0][:, 4:8], 1.0 / E, None, A.mult))
                link(dve.scalar_tensor_tensor(red[:, 12:16], m, -1.0, m, A.mult, A.max))
                dve.nop().then_inc(S2("abs"), 1)
                link(dve.tensor_scalar(red[:, 16:20], m, 0.0, None, A.is_gt))
                link(dve.tensor_scalar(red[:, 20:24], m, 0.0, None, A.is_lt))
                link(dve.tensor_tensor(red[:, 16:20], red[:, 16:20], red[:, 20:24], A.subtract))
                dve.wait_ge(S2("root"), 1)
                link(dve.tensor_tensor(red[:, 16:20], red[:, 16:20], red[:, 24:28], A.mult))
                link(dve.tensor_tensor(red[:, 16:20], red[:, 16:20], grad[:, :], A.mult))
                link(dve.tensor_reduce(red[:, 28:29], red[:, 16:20], AX, A.add))
                dve.nop().then_inc(S2("weighted"), 1)
                dve.wait_ge(S2("shifted"), 1)
                link(dve.tensor_copy(shift, P[0][:, 8:9]))

            @block.gpsimd
            def _(pool):
                pool.memset(small[:, 0:4:2], 0.5).then_inc(S2("exponents"), 1)
                pool.memset(small[:, 1:4:2], 1.0 / 3.0).then_inc(S2("exponents"), 1)
                pool.wait_ge(S2("exponents"), 2)
                pool.wait_ge(S2("abs"), 1)
                pool.tensor_tensor(red[:, 24:28], red[:, 12:16], small[:, 0:4], A.pow).then_inc(S2("root"), 1)

            @block.tensor
            def _(pe):
                pe.wait_ge(S2("sums"), 1)
                pe.matmul(P[0][:, 0:2], fold[:, :], red[:, 0:2], start=True, stop=True).then_inc(S2("folded"), 1)
                pe.wait_ge(S2("means"), 1)
                pe.matmul(P[1][:, 0:2], wfc[:, :], red[:, 2:4], start=True, stop=True).then_inc(S2("mu"), 1)
                pe.wait_ge(S2("mu_ready"), 1)

                def body(s, par, k, n):
                    pe.matmul(P[2][:, :], wfc[:, :], at(XS, s), start=True, stop=True).then_inc(S2("z"), 1)
                    pe.matmul(P[3][:, :], wfc[:, :], at(XD, s), start=True, stop=True).then_inc(S2("z"), 1)
                    pe.matmul(P[4][0:2, :], one_l[:, 0:2], at(XS, s), start=True, stop=False)
                    pe.matmul(P[4][0:2, :], one_l[:, 2:4], at(XD, s), start=False, stop=False)
                    pe.wait_ge(S2("eat"), n * 32)
                    pe.matmul(P[4][0:2, :], one_l[:, 4:6], eat[:, :], start=False, stop=True).then_inc(S2("logit"), 1)
                    pe.wait_ge(S2("cube0"), n)
                    pe.wait_ge(S2("cube1"), n)
                    pe.wait_ge(S2("row"), n)
                supers(pe, body)
                pe.wait_ge(S2("moment_sums"), 1)
                pe.matmul(P[0][:, 4:8], fold[:, :], red[:, 4:8], start=True, stop=True).then_inc(S2("moments"), 1)
                pe.wait_ge(S2("weighted"), 1)
                pe.matmul(P[0][:, 8:9], total[:, :], red[:, 28:29], start=True, stop=True).then_inc(S2("shifted"), 1)

            @block.scalar
            def _(act):
                def body(s, par, k, n):
                    hi, c = (64, LASTC) if isinstance(s, int) else (128, HW)
                    act.wait_ge(S2("z"), 2 * n)
                    for side, (ps, mu) in enumerate(((P[2], mu_s), (P[3], mu_d))):
                        act.activation(wk[side][0:hi, 0:c], ps[0:hi, 0:c], ACT.Square, bias=mu[0:hi, :],
                                       accum_out=stat[0:hi, 4 + 2 * side, bass.ds(s, 1)]).then_inc(S2(f"square{side}"), 1)
                    act.wait_ge(S2("logit"), n)
                    act.wait_ge(S2("row_free"), n)
                    act.activation(wk[2][0:2, :], P[4][0:2, :], ACT.Copy).then_inc(S2("row"), 1)
                supers(act, body)
                act.wait_ge(S2("square1"), NS)
                act.nop().then_inc(S2("squares"), 1)

            @block.sync
            def _(sp):
                sp.sem_inc(S2("row_free"), 1)

                def body(s, par, k, n):
                    load_attributes(sp, S2, s)
                    sp.wait_ge(S2("row"), n)
                    sp.dma_start(logit1_d[bass.ds(s * SE, SE)].rearrange("(a c) -> a c", a=2), wk[2][0:2, :]).then_inc(S2("stored"), 16)
                    sp.wait_ge(S2("stored"), n * 16)
                    sp.sem_inc(S2("row_free"), 1)
                supers(sp, body)

        S2.done()

        SF = Sems("f_")
        with nc.Block() as block:
            softmax_rows(block, SF, logit1_d, weight1_d, 1, 0.01, False)
        SF.done()

        S3 = Sems("g_")
        with nc.Block() as block:
            @block.sync
            def _(sp):
                sp.sem_inc(S3("emb_free"), 1)

                def body(s, par, k, n):
                    load_attributes(sp, S3, s)
                    load_weights(sp, S3, weight1_d, wk[3], s)
                    sp.wait_ge(S3("emb"), n)
                    sp.dma_start(table[2][bass.ds(s * SE, SE), :].rearrange("(p j) f -> p (j f)", p=128), EMB).then_inc(S3("stored"), 16)
                    sp.wait_ge(S3("stored"), n * 16)
                    sp.sem_inc(S3("emb_free"), 1)
                supers(sp, body)

            @block.tensor
            def _(pe):
                def body(s, par, k, n):
                    pe.matmul(P[0][:, :], wfc[:, :], at(XS, s), start=True, stop=False)
                    pe.wait_ge(S3("eat"), n * 32)
                    pe.matmul(P[0][:, :], eprj[:, :], eat[:, :], start=False, stop=True).then_inc(S3("message"), 1)
                    norm_pe(pe, S3, n)
                supers(pe, body)

            @block.vector
            def _(dve):
                dve.memset(car[:, :], 0.0).then_inc(S3("car0"), 1)
                dve.wait_ge(S3("car0"), 1)

                def body(s, par, k, n):
                    dve.wait_ge(S3("message"), n)
                    dve.wait_ge(S3("weights"), n * 32)
                    dve.tensor_tensor(V, P[0][:, :], wk[3], A.mult).then_inc(S3("v"), 1)
                    dve.wait_ge(S3("v"), n)
                    seg_scan(dve, S3, n, V, FS[:, :], at(SAME, s), A.mult, A.add)
                    dve.tensor_tensor(U, at(XD, s), FS[:, :], A.add).then_inc(S3("u"), 1)
                    norm_dve(dve, S3, s, n)
                supers(dve, body)

            @block.scalar
            def _(act):
                supers(act, lambda s, par, k, n: norm_act(act, S3, n))

        S3.done()

        S4 = Sems("h_")
        with nc.Block() as block:
            @block.gpsimd
            def _(pool):
                gather_rounds(pool, S4, [GA], [look_i], [table[2]])

            @block.vector
            def _(dve):
                pass_back(dve, S4)
                dve.wait_ge(S4("back_free0"), NS // 2 + 2)
                dve.wait_ge(S4("back_free1"), NS // 2 + 1)
                dve.nop().then_inc(S4("back"), 1)

            @block.tensor
            def _(pe):
                def body(s, par, k, n):
                    pe.matmul(P[1][0:16, :], two_l[:, 0:16], at(XS, s), start=True, stop=False)
                    pe.matmul(P[1][0:16, :], two_l[:, 16:32], at(XD, s), start=False, stop=True).then_inc(S4("logit"), 1)
                    pe.wait_ge(S4("row"), n)
                gather_pe(pe, S4)
                pe.wait_ge(S4("fm_kept"), NS)
                pe.wait_ge(S4("back"), 1)
                supers(pe, body)

            @block.scalar
            def _(act):
                def keep(s, par, k, n):
                    keep_back(act, S4, s, par, n)
                    act.wait_ge(S4("fm"), n)
                    act.activation(at(XS, s), P[0][:, :], ACT.Copy).then_inc(S4("fm_kept"), 1)
                supers(act, keep)

                def row(s, par, k, n):
                    act.wait_ge(S4("logit"), n)
                    act.wait_ge(S4("row_free"), n)
                    act.activation(wk[2][0:16, :], P[1][0:16, :], ACT.Copy).then_inc(S4("row"), 1)
                supers(act, row)

            @block.sync
            def _(sp):
                sp.sem_inc(S4("row_free"), 1)

                def body(s, par, k, n):
                    sp.wait_ge(S4("row"), n)
                    for h in range(2):
                        sp.dma_start(logit2_d[:, bass.ds(s * SE + h * HW, HW)], wk[2][h:16:2, :]).then_inc(S4("stored"), 16)
                    sp.wait_ge(S4("stored"), n * 32)
                    sp.sem_inc(S4("row_free"), 1)
                supers(sp, body)

        S4.done()
        SI = Sems("i_")
        with nc.Block() as block:
            softmax_rows(block, SI, logit2_d, weight2_d, HEADS, 0.2, True)
        SI.done()


        S5 = Sems("j_")
        HB = [GA[:, 0, :], GA[:, 1, :]]
        with nc.Block() as block:
            @block.sync
            def _(sp):
                sp.sem_inc(S5("emb_free"), 1)

                def body(s, par, k, n):
                    for c in range(2 * HEADS):
                        b, t = c % 2, 4 * (n - 1) + c // 2 + 1
                        sp.wait_ge(S5(f"hw_free{b}"), t)
                        load_weights(sp, S5, weight2_d[c, :], HB[b], s, f"hw{b}")
                    sp.wait_ge(S5("emb"), n)
                    sp.dma_start(table[3][bass.ds(s * SE, SE), :].rearrange("(p j) f -> p (j f)", p=128), EMB).then_inc(S5("stored"), 16)
                    sp.wait_ge(S5("stored"), n * 16)
                    sp.sem_inc(S5("emb_free"), 1)
                supers(sp, body)

            @block.vector
            def _(dve):
                dve.memset(car[:, :], 0.0).then_inc(S5("car0"), 1)
                dve.wait_ge(S5("car0"), 1)
                for b in range(2):
                    dve.sem_inc(S5(f"hw_free{b}"), 1)
                    dve.sem_inc(S5(f"ya_free{b}"), 1)

                def body(s, par, k, n):
                    def heads(side, x):
                        for h in range(HEADS):
                            c = side * HEADS + h
                            b, t = c % 2, 4 * (n - 1) + c // 2 + 1
                            dve.wait_ge(S5(f"hw{b}"), 32 * t)
                            dve.wait_ge(S5(f"ya_free{b}"), t)
                            dve.tensor_tensor(wk[b], x, HB[b], A.mult).then_inc(S5(f"ya{b}"), 1)
                            dve.wait_ge(S5(f"ya{b}"), t)
                            dve.sem_inc(S5(f"hw_free{b}"), 1)
                    heads(0, at(XS, s))
                    heads(1, at(XD, s))
                    dve.wait_ge(S5("message"), n)
                    seg_scan(dve, S5, n, P[0], FS[:, :], at(SAME, s), A.mult, A.add)
                    dve.wait_ge(S5("self"), n)
                    dve.scalar_tensor_tensor(V, P[1][:, :], bias2, FS[:, :], A.add, A.add).then_inc(S5("v"), 1)
                    dve.wait_ge(S5("v"), n)
                    dve.tensor_tensor(U, V, at(XD, s), A.add).then_inc(S5("u"), 1)
                    norm_dve(dve, S5, s, n)
                supers(dve, body)

            @block.tensor
            def _(pe):
                def body(s, par, k, n):
                    for side, name in ((0, "message"), (1, "self")):
                        for h in range(HEADS):
                            c = side * HEADS + h
                            b, t = c % 2, 4 * (n - 1) + c // 2 + 1
                            pe.wait_ge(S5(f"ya{b}"), t)
                            ins = pe.matmul(P[side][:, :], wh[h][:, :], wk[b], start=(h == 0), stop=(h == HEADS - 1))
                            ins.then_inc(S5(f"ya_free{b}"), 1)
                        pe.wait_ge(S5("ya_free1"), 4 * (n - 1) + 2 * side + 3)
                        pe.nop().then_inc(S5(name), 1)
                    norm_pe(pe, S5, n)
                supers(pe, body)

            @block.scalar
            def _(act):
                supers(act, lambda s, par, k, n: norm_act(act, S5, n))

        S5.done()

        S6 = Sems("k_")
        NEG, XW, HID, MX, FIN, Z0 = wk[0], wk[1], wk[3], FS[:, :], wk[5], junk[:, :]
        with nc.Block() as block:
            @block.gpsimd
            def _(pool):
                gather_rounds(pool, S6, [GA], [look_i], [table[3]])

            @block.vector
            def _(dve):
                pass_back(dve, S6)
                dve.wait_ge(S6("back_free0"), NS // 2 + 2)
                dve.wait_ge(S6("back_free1"), NS // 2 + 1)
                dve.memset(car[:, :], -BIG).then_inc(S6("carm"), 1)
                dve.wait_ge(S6("carm"), 1)
                dve.nop().then_inc(S6("back"), 1)

                def body(s, par, k, n):
                    dve.tensor_scalar(NEG, at(SAME, s), -1.0, BIG, A.add, A.mult).then_inc(S6("neg"), 1)
                    dve.wait_ge(S6("neg"), n)
                    dve.wait_ge(S6("message"), n)
                    seg_scan(dve, S6, n, P[5], MX, NEG, A.add, A.max)
                    dve.tensor_scalar(MX, MX, b2, None, A.add).then_inc(S6("b2"), 1)
                    dve.memset(Z0, 0.0).then_inc(S6("zero"), 1)
                    dve.wait_ge(S6("b2"), n)
                    dve.tensor_scalar(FIN, MX, -FMAX, FMAX, A.max, A.min).then_inc(S6("clipped"), 1)
                    dve.wait_ge(S6("clipped"), n)
                    dve.tensor_tensor(FIN.bitcast(I32), FIN, MX, A.is_equal).then_inc(S6("finite"), 1)
                    dve.wait_ge(S6("finite"), n)
                    dve.wait_ge(S6("zero"), n)
                    settle(dve, S6("settled"))
                    dve.copy_predicated(Z0, FIN.bitcast(I32), MX).then_inc(S6("out3"), 1)
                    dve.wait_ge(S6("out3"), n)
                    dve.tensor_tensor(U, Z0, at(XD, s), A.add).then_inc(S6("u"), 1)
                    norm_dve(dve, S6, s, n, keep=False)
                supers(dve, body)

            @block.tensor
            def _(pe):
                for par in range(2):
                    pe.sem_inc(S6(f"slot_free{par}"), 1)
                pe.wait_ge(S6("back"), 1)

                def body(s, par, k, n):
                    pe.wait_ge(S6(f"gathered{par}"), k * 128)
                    transpose4(pe, P[0], GA[:, par, :]).then_inc(S6("fm"), 1)
                    pe.wait_ge(S6("fm"), n)
                    pe.sem_inc(S6(f"slot_free{par}"), 1)
                    pe.matmul(P[1][:, :], w1d[:, :], at(XD, s), start=True, stop=False)
                    pe.wait_ge(S6("fm_kept"), n)
                    pe.matmul(P[1][:, :], w1s[:, :], XW, start=False, stop=True).then_inc(S6("hidden_mm"), 1)
                    pe.wait_ge(S6("hidden"), n)
                    pe.matmul(P[5][:, :], w2[:, :], HID, start=True, stop=True).then_inc(S6("message"), 1)
                    norm_pe(pe, S6, n)
                supers(pe, body)

            @block.scalar
            def _(act):
                supers(act, lambda s, par, k, n: keep_back(act, S6, s, par, n))
                act.sem_inc(S6("emb_free"), NS)

                def body(s, par, k, n):
                    act.wait_ge(S6("fm"), n)
                    act.activation(XW, P[0][:, :], ACT.Copy).then_inc(S6("fm_kept"), 1)
                    act.wait_ge(S6("hidden_mm"), n)
                    act.activation(HID, P[1][:, :], ACT.Relu, bias=b1).then_inc(S6("hidden"), 1)
                    norm_act(act, S6, n, at(XS, s))
                supers(act, body)

        S6.done()

        S7 = Sems("l_")
        with nc.Block() as block:
            @block.scalar
            def _(act):
                def body(s, par, k, n):
                    act.wait_ge(S7(f"free{par}"), k)
                    act.activation(GA[:, par, :], at(XS, s), ACT.Copy).then_inc(S7("rows"), 1)
                supers(act, body)

            @block.sync
            def _(sp):
                for par in range(2):
                    sp.sem_inc(S7(f"free{par}"), 1)

                def body(s, par, k, n):
                    sp.wait_ge(S7(f"scattered{par}"), k * 128)
                    sp.sem_inc(S7(f"free{par}"), 1)
                supers(sp, body)

            @block.gpsimd
            def _(pool):
                def body(s, par, k, n):
                    pool.wait_ge(S7("rows"), n)
                    pool.tensor_copy(win[:, par, 0:8], seg_i[:, bass.ds(s * 8, 8)]).then_inc(S7("window"), 1)
                    pool.wait_ge(S7("window"), n)
                    settle(pool, S7("settled"))
                    for j in range(8):
                        pool.indirect_dma_start(out, bass.IndirectOffsetOnAxis(ap=win[:, par, j:j + 1], axis=0),
                                                GA[:, par, j * D:(j + 1) * D], None, bounds_check=N - 1, oob_is_err=False
                                                ).then_inc(S7(f"scattered{par}"), 16)
                supers(pool, body)
                pool.wait_ge(S7("scattered0"), 128 * (NS // 2 + 1))
                pool.wait_ge(S7("scattered1"), 128 * (NS // 2))


def kernel(**inputs):
    import concourse.bacc as bacc
    from concourse.bass_utils import run_bass_kernel_spmd

    x = {k: np.ascontiguousarray(v) for k, v in inputs.items()}
    src, dst = x["src"], x["dst"]
    pad = EP - E
    src_p = np.concatenate([src, np.zeros(pad, np.int32)])
    dst_p = np.concatenate([np.full(1, -1, np.int32), dst, np.full(pad, N, np.int32), np.full(1, N + 1, np.int32)])

    def columns(v):
        return np.ascontiguousarray(v.reshape(NS, 2, 4, 128).transpose(3, 0, 2, 1).reshape(128, NS * 8))

    half = np.kron(np.eye(2, dtype=np.float32), np.ones((D, D), np.float32))
    eye = np.eye(128, dtype=np.float32)
    const = np.concatenate([eye, eye - half / D, half / D, half, np.kron(np.ones((2, 2), np.float32), np.eye(D, dtype=np.float32)),
                            np.ones((128, 128), np.float32)], axis=1).astype(np.float32)
    attr = np.zeros((2, EP), np.float32)
    attr[:, :E] = x["edge_attr_2"].T
    wa = x["L1_gnn_W_attn"][0]
    arrays = {
        "x": x["x"], "src_l": columns(src_p), "dst_l": columns(dst_p[1:EP + 1]), "next_l": columns(dst_p[2:EP + 2]),
        "dst_pad": dst_p, "attr": attr, "const": const,
        "proj": x["L0_gnn_proj_cosim"], "wffnT": x["L0_gnn_W_ffn"].T, "b_ffn": x["L0_gnn_b_ffn"],
        "wfcT": x["L1_gnn_W_fc"].T, "wfc": x["L1_gnn_W_fc"], "blkT": wa[:6 * D].reshape(6, D).T, "we": wa[6 * D:].reshape(2, 1),
        "wedge": x["L1_gnn_W_edge"], "we2nT": x["L1_gnn_W_e2n"].T, "wm1": x["L1_gnn_W_m1"], "wm2": x["L1_gnn_W_m2"],
        "w2l": x["L2_gnn_W"], "att": np.concatenate([x["L2_gnn_att_src"].ravel(), x["L2_gnn_att_dst"].ravel()]),
        "bias2": x["L2_gnn_bias"],
        "w1a": x["L3_gnn_W1"][:D], "w1b": x["L3_gnn_W1"][D:], "b1": x["L3_gnn_b1"], "w2": x["L3_gnn_W2"], "b2": x["L3_gnn_b2"],
    }
    nc = bacc.Bacc("TRN2", target_bir_lowering=False, num_devices=1)
    given, aps = {}, {}
    for name, v in arrays.items():
        v = np.ascontiguousarray(v)
        given[f"in_{name}"] = v
        aps[name] = nc.dram_tensor(f"in_{name}", v.shape, mybir.dt.from_np(v.dtype), kind="ExternalInput").ap()
    out = nc.dram_tensor("out_x", [N, D], F32, kind="ExternalOutput").ap()
    build(nc, aps, out)
    return run_bass_kernel_spmd(nc, [given], core_ids=[0]).results[0]["out_x"]
```

```python
import numpy as np
from contextlib import ExitStack
import concourse.bass as bass
from concourse import mybir

N, D, E = 100000, 64, 25000
SE = 1024
NS = (E + SE - 1) // SE
EP = NS * SE
LASTC = E - (NS - 1) * SE
HW = 512
NG = N // SE
RC = EP // 128
HEADS = 4
EPS = 1e-5
BIG = 3e38
FMAX = 3.4028234663852886e38
FAR = 1 << 20

F32, I32, U8 = mybir.dt.float32, mybir.dt.int32, mybir.dt.uint8
A = mybir.AluOpType
ACT = mybir.ActivationFunctionType
AX = mybir.AxisListType.X


def supers(eng, body):
    with eng.Fori(0, NS // 2) as i:
        body(2 * i, 0, i + 1, 2 * i + 1)
        body(2 * i + 1, 1, i + 1, 2 * i + 2)
    body(NS - 1, 0, NS // 2 + 1, NS)


def side_by_side(*streams):
    at = [[next(g), i, g] for i, g in enumerate(streams)]
    while at:
        first = min(at, key=lambda x: x[:2])
        try:
            first[0] = next(first[2])
        except StopIteration:
            at.remove(first)


def pairs(eng, *makers):
    with eng.Fori(0, NS // 2) as i:
        side_by_side(*(m(2 * i + par, par, i + 1) for par in range(2) for m in makers))
    side_by_side(*(m(NS - 1, 0, NS // 2 + 1) for m in makers))


def of(S, par):
    return lambda name: S(f"{name}{par}")


def settle(eng, sem):
    eng.sem_inc(sem, 1)


def per_row(t):
    return t.rearrange("p (j o) -> p j o", o=1).to_broadcast([128, 8, D])


def rows(t):
    return t.rearrange("p (j f) -> p j f", f=D)


def build(nc, a, out):
    ctx = ExitStack()
    with ctx:
        def sb(name, shape, dt=F32):
            return ctx.enter_context(nc.sbuf_tensor(name, shape, dt))

        def dram(name, shape, dt=F32):
            return nc.dram_tensor(name, shape, dt, kind="Internal").ap()

        class Sems:
            def __init__(self, prefix):
                self.prefix, self.made = prefix, {}

            def __call__(self, name):
                if name not in self.made:
                    self.made[name] = nc.alloc_semaphore(name=self.prefix + name)
                return self.made[name]

            def done(self):
                nc.clear_and_free_semaphores(list(self.made.values()))
                nc.all_engine_barrier()

        rank = dram("rank", [N, 1], I32)
        table = [dram(f"table{k}", [2 * EP, D]) for k in range(4)]
        logit1_d = dram("logit1_d", [EP])
        weight1_d = dram("weight1_d", [EP])
        logit2_d = dram("logit2_d", [3 * HEADS, EP])
        weight2_d = dram("weight2_d", [2 * HEADS, EP])

        XD = sb("XD", [128, NS * HW])
        XS = sb("XS", [128, NS * HW])
        SAME = sb("SAME", [128, NS * HW], U8)
        MORE = sb("MORE", [128, NS * HW], U8)
        src_i = sb("src_i", [128, 8 * NS], I32)
        dst_i = sb("dst_i", [128, 8 * NS], I32)
        seg_i = sb("seg_i", [128, 8 * NS], I32)
        row_i = sb("row_i", [128, 8 * NS], I32)
        look_i = sb("look_i", [128, 8 * NS], I32)
        t_i = sb("t_i", [128, 8 * NS], I32)
        win = sb("win", [128, 2, 24], I32)
        GA = sb("GA", [128, 2, HW])
        GB = sb("GB", [128, 2, HW])
        rank_t = sb("rank_t", [128, 8 * NS], I32)
        NW = 9
        work = sb("work", [128, 2 * NW * HW])
        W = [[work[:, (par * NW + i) * HW:(par * NW + i + 1) * HW] for i in range(NW)] for par in range(2)]
        wk = W[0]
        XN = sb("XN", [128, 2, HW])
        small = sb("small", [128, 2, 64])
        car = sb("car", [128, 1])
        stat = sb("stat", [128, 8, NS])
        red = sb("red", [128, 32])

        ident = sb("ident", [128, 128])
        ones = sb("ones", [128, 128])
        center = sb("center", [128, 128])
        average = sb("average", [128, 128])
        total = sb("total", [128, 128])
        fold = sb("fold", [128, 128])
        proj = sb("proj", [128, 128])
        wffn = sb("wffn", [128, 128])
        wfc = sb("wfc", [128, 128])
        chain = sb("chain", [128, 128])
        wh = [sb(f"wh{h}", [128, 128]) for h in range(HEADS)]
        w1d = sb("w1d", [128, 128])
        w1s = sb("w1s", [128, 128])
        w2 = sb("w2", [128, 128])
        eprj = sb("eprj", [128, 128])
        one_l = sb("one_l", [128, 6])
        two_l = sb("two_l", [128, 32])
        vec = sb("vec", [128, 16])
        P = [ctx.enter_context(nc.psum_tensor(f"P{i}", [128, HW], F32)) for i in range(8)]
        bff, relub, bias2, bias2c, b1, b2, eps_t, one_t = (vec[:, i:i + 1] for i in range(8))
        bias_row = sb("bias_row", [128, D])
        inv_scale, mu_s, mu_d, shift = (vec[:, i:i + 1] for i in range(8, 12))
        grad = sb("grad", [128, 4])
        row_same = sb("row_same", [128, RC])
        row_more = sb("row_more", [128, RC])
        row_neg = sb("row_neg", [128, RC])
        row_last = sb("row_last", [128, RC])
        ends = sb("ends", [128, 2 * HEADS])
        carry = sb("carry", [HEADS, 512])
        carry_in = sb("carry_in", [128, HEADS])

        S = Sems("su_")
        wl = GA[:, :, :].rearrange("p a c -> p (a c)")
        wl2 = GB[:, :, :].rearrange("p a c -> p (a c)")
        Wsb, Att, Wfc_n, Blk, Wed, We2, Wm, Asum = (wl[:, 0:256], wl[:, 256:768], wl[0:64, 768:896], wl[0:64, 900:906],
                                                    wl[0:2, 908:910], wl2[0:2, 0:64], wl2[:, 64:192], wl2[:, 192:320])
        Wmn = work[0:64, 2048:2304].rearrange("p (k c) -> p k c", k=2)
        W1a, IW, CW, we_t, Pr = wl2[:, 320:448], wl2[:, 448:576], wl2[:, 576:704], wl[0:2, 912:913], wl2[:, 704:960]

        sml = small[:, 0, :]
        with nc.Block() as block:
            blocks = [(proj, "proj"), (wffn, "wffnT"), (wfc, "wfcT"), (w1s, "w1b"), (w2, "w2"), (W1a, "w1a")]
            loads = [0]

            @block.sync
            def _(sp):
                def ld(dst, src):
                    sp.dma_start(dst, src).then_inc(S("load"), 16)
                    loads[0] += 16
                sp.wait_ge(S("zero"), 1)
                for h in range(2):
                    lo, hi = h * 64, h * 64 + 64
                    for t, name in blocks:
                        ld(t[lo:hi, lo:hi], a[name])
                    for k in range(HEADS):
                        ld(wh[k][lo:hi, lo:hi], a["w2l"][:, k * D:(k + 1) * D])
                    ld(Wsb[lo:hi, :], a["w2l"])
                    for i, name in enumerate(["b_ffn", "bias2", "b1", "b2"]):
                        ld(vec[lo:hi, (0, 2, 4, 5)[i]:(0, 2, 4, 5)[i] + 1], a[name].rearrange("(p o) -> p o", o=1))
                    ld(Wfc_n[:, h * 64:h * 64 + 64], a["wfc"])
                ld(Att, a["att"].rearrange("(o c) -> o c", o=1).to_broadcast([128, 512]))
                ld(bias_row[:, :], a["bias2"].rearrange("(o c) -> o c", o=1).to_broadcast([128, D]))
                ld(Blk, a["blkT"])
                ld(Wed, a["wedge"])
                ld(We2, a["we2nT"])
                ld(we_t, a["we"])
                for k in range(2):
                    for h in range(2):
                        ld(Wmn[:, k, h * 64:h * 64 + 64], a[f"wm{k + 1}"])
                for k, (t, off) in enumerate([(row_same, 0), (row_neg, 1), (row_more, 2)]):
                    ld(t[:, :].bitcast(I32), a["dst_pad"][off:off + EP].rearrange("(p c) -> p c", p=128))
                for i, t in enumerate([ident, center, average, total, fold, ones]):
                    ld(t[:, :], a["const"][:, i * 128:(i + 1) * 128])
                ld(src_i[:, :], a["src_l"])
                ld(dst_i[:, :], a["dst_l"])
                ld(seg_i[:, :], a["next_l"])
                sp.wait_ge(S("load"), loads[0])
                sp.sem_inc(S("loaded"), 1)
                sp.wait_ge(S("fill"), 2)
                sp.dma_start(rank.rearrange("(p c) o -> p (c o)", p=80), XS[0:80, 0:N // 80].bitcast(I32)).then_inc(S("init"), 16)
                sp.dma_start(table[0][EP:2 * EP, :].rearrange("(p c) f -> p (c f)", p=128), XD[:, :]).then_inc(S("init"), 16)
                sp.wait_ge(S("init"), 32)

            @block.gpsimd
            def _(pool):
                pool.iota(row_i[:, :].rearrange("p (s j) -> p s j", j=8), [[SE, NS], [1, 8]], base=0,
                          channel_multiplier=8).then_inc(S("iota"), 1)
                pool.memset(XS[0:80, 0:N // 80].bitcast(I32), -1).then_inc(S("fill"), 1)
                pool.memset(XD[:, :], 0.0).then_inc(S("fill"), 1)

            @block.vector
            def _(dve):
                step = [0]

                def link(ins):
                    step[0] += 1
                    ins.then_inc(S("dve"), 1)
                    dve.wait_ge(S("dve"), step[0])

                for t in [proj, wffn, wfc, w1s, w2, eprj, *wh]:
                    dve.memset(t[:, :], 0.0)
                for t in [one_l, two_l, car]:
                    dve.memset(t[:, :], 0.0)
                dve.memset(stat[:, :, :], 0.0)
                dve.memset(W1a, 0.0)
                link(dve.memset(eps_t, EPS))
                link(dve.memset(one_t, 1.0))
                dve.nop().then_inc(S("zero"), 1)
                dve.wait_ge(S("loaded"), 1)
                dve.wait_ge(S("iota"), 1)
                link(dve.tensor_tensor(t_i[:, :], dst_i[:, :], seg_i[:, :], A.is_equal))
                link(dve.scalar_tensor_tensor(seg_i[:, :], t_i[:, :], float(FAR), dst_i[:, :], A.mult, A.add))
                link(dve.tensor_scalar(dst_i[:, :], dst_i[:, :], float(N - 1), None, A.min))
                for t in (row_same, row_more):
                    link(dve.tensor_tensor(t[:, :], t[:, :].bitcast(I32), row_neg[:, :].bitcast(I32), A.is_equal))
                link(dve.tensor_scalar(row_neg[:, :], row_same[:, :], -1.0, BIG, A.add, A.mult))
                link(dve.tensor_scalar(row_last[:, :], row_more[:, :], 0.0, None, A.is_equal))
                link(dve.tensor_scalar(relub, bff, 0.0, None, A.max))
                link(dve.tensor_tensor(Asum[:, 0:64], Wsb[:, 0:64], Wsb[:, 64:128], A.add))
                link(dve.tensor_tensor(Asum[:, 64:128], Wsb[:, 128:192], Wsb[:, 192:256], A.add))
                link(dve.memset(Wm, 0.0))
                link(dve.tensor_tensor(Wm[0:64, 0:64], Asum[0:64, 0:64], Asum[0:64, 64:128], A.add))
                link(dve.tensor_tensor(Wm[64:128, 64:128], Asum[64:128, 0:64], Asum[64:128, 64:128], A.add))
                link(dve.scalar_tensor_tensor(IW, Wm, 1.0 / HEADS, ident[:, :], A.mult, A.add))
                for side in range(2):
                    link(dve.tensor_tensor(Pr, Wsb, Att[:, side * 256:(side + 1) * 256], A.mult))
                    link(dve.tensor_reduce(sml[:, side * 4:side * 4 + 4], Pr.rearrange("p (h d) -> p h d", h=HEADS), AX, A.add))
                link(dve.tensor_tensor(sml[:, 8:12], sml[:, 0:4], sml[:, 4:8], A.add))
                for h in range(2):
                    lo, hi = h * 64, h * 64 + 64
                    cols = lambda base: two_l[lo:hi, base + h:base + h + 7:2]
                    link(dve.tensor_copy(cols(0), sml[lo:hi, 0:4]))
                    link(dve.tensor_copy(cols(16), sml[lo:hi, 4:8]))
                    link(dve.tensor_copy(cols(24), sml[lo:hi, 8:12]))
                link(dve.tensor_tensor(w1d[:, :], W1a, w1s[:, :], A.subtract))
                dve.nop().then_inc(S("folded"), 1)
                dve.wait_ge(S("pe"), 1)
                link(dve.tensor_copy(CW, P[0][:, 0:128]))
                for h in range(2):
                    lo, hi = h * 64, h * 64 + 64
                    for c in range(2):
                        link(dve.tensor_copy(one_l[lo:hi, 2 * c + h:2 * c + h + 1], P[1][lo:hi, (0, 3)[c]:(0, 3)[c] + 1]))
                    link(dve.tensor_copy(eprj[lo:lo + 2, lo:hi], P[2][lo:lo + 2, 0:64]))
                    link(dve.tensor_copy(one_l[lo:lo + 2, 4 + h:5 + h], P[2][lo:lo + 2, 64:65]))
                link(dve.tensor_copy(bias2c, P[3][:, 0:1]))
                for k in range(2):
                    link(dve.tensor_copy(grad[:, k:k + 3:2], P[3][:, 4 + 2 * k:6 + 2 * k]))
                dve.nop().then_inc(S("cw"), 1)
                dve.wait_ge(S("pe"), 2)
                link(dve.tensor_copy(chain[:, :], P[4][:, 0:128]))
                link(dve.tensor_reduce(red[:, 0:1], bias_row[:, :], AX, A.add))
                link(dve.tensor_scalar(red[:, 1:2], red[:, 0:1], 1.0 / D, None, A.mult))
                link(dve.tensor_scalar(bias_row[:, :], bias_row[:, :], red[:, 1:2], None, A.subtract))

            @block.tensor
            def _(pe):
                pe.wait_ge(S("folded"), 1)
                pe.matmul(P[0][:, 0:128], center[:, :], IW, start=True, stop=True)
                pe.matmul(P[1][:, 0:6], Wfc_n, Blk, start=True, stop=True)
                for h in range(2):
                    pe.matmul(P[2][64 * h:64 * h + 2, 0:64], Wed, We2, start=True, stop=True)
                    pe.matmul(P[2][64 * h:64 * h + 2, 64:65], Wed, we_t, start=True, stop=True)
                pe.matmul(P[3][:, 0:1], center[:, :], bias2, start=True, stop=True)
                for k in range(2):
                    last = pe.matmul(P[3][:, 4 + 2 * k:6 + 2 * k], Wmn[:, k, :], Blk[:, 1 + k:5 + k:3], start=True, stop=True)
                last.then_inc(S("pe"), 1)
                pe.wait_ge(S("cw"), 1)
                pe.transpose(P[5][:, 0:128], CW, ident[:, :]).then_inc(S("pet"), 1)
                pe.wait_ge(S("cwt"), 1)
                pe.matmul(P[4][:, 0:128], wk[0][:, 0:128], center[:, :], start=True, stop=True).then_inc(S("pe"), 1)

            @block.scalar
            def _(act):
                act.wait_ge(S("pet"), 1)
                act.activation(wk[0][:, 0:128], P[5][:, 0:128], ACT.Copy).then_inc(S("cwt"), 1)

        S.done()

        def at(t, s):
            return t[:, bass.ds(s * HW, HW)]

        def rows_of(t, first):
            return t[bass.ds(first, SE), :].rearrange("(p j) f -> p (j f)", p=128)

        def gather_rounds(pool, S, look, table_k):
            def body(s, par, k, n):
                pool.wait_ge(S(f"slot_free{par}"), k)
                pool.tensor_copy(win[:, par, 0:8], look[:, bass.ds(s * 8, 8)]).then_inc(S("window"), 1)
                pool.wait_ge(S("window"), n)
                settle(pool, S("settled"))
                for j in range(8):
                    pool.indirect_dma_start(GA[:, par, j * D:(j + 1) * D], None, table_k,
                                            bass.IndirectOffsetOnAxis(ap=win[:, par, j:j + 1], axis=0)
                                            ).then_inc(S(f"gathered{par}"), 16)
            supers(pool, body)

        def transpose4(pe, dst, src):
            for q in range(4):
                ins = pe.transpose(dst[:, q * 128:(q + 1) * 128], src[:, q * 128:(q + 1) * 128], ident[:, :])
            return ins

        def seg_scan(dve, T, k, V, F, m, op0, op1):
            dve.tensor_tensor_scan(F[0:64, :], m[0:64, :], V[0:64, :], car[0:64, :], op0, op1).then_inc(T("scan0"), 1)
            dve.wait_ge(T("scan0"), k)
            dve.tensor_copy(car[64:128, :], F[0:64, HW - 1:HW]).then_inc(T("mid_carry"), 1)
            dve.wait_ge(T("mid_carry"), k)
            dve.tensor_tensor_scan(F[64:128, :], m[64:128, :], V[64:128, :], car[64:128, :], op0, op1).then_inc(T("scan1"), 1)
            dve.wait_ge(T("scan1"), k)
            dve.tensor_copy(car[0:64, :], F[64:128, HW - 1:HW]).then_inc(T("next_carry"), 1)
            dve.wait_ge(T("next_carry"), k)

        def norm_pe(pe, T, par, k, b, keep=True):
            U, EMB = W[par][4], W[par][6]
            yield b + 1
            pe.wait_ge(T("u"), k)
            for q in range(4):
                ins = pe.matmul(P[4 * par + 2][:, q * 128:(q + 1) * 128], U[:, q * 128:(q + 1) * 128], center[:, :],
                                start=True, stop=True)
            ins.then_inc(T("centred"), 1)
            yield b + 6
            pe.wait_ge(T("emb"), k)
            if keep:
                transpose4(pe, P[4 * par + 3], EMB).then_inc(T("x_fm"), 1)
                yield b + 8
                pe.wait_ge(T("kept"), k)

        def norm_act(act, T, par, k, b):
            yield b + 2
            act.wait_ge(T("centred"), k)
            act.activation(W[par][5], P[4 * par + 2][:, :], ACT.Square).then_inc(T("square"), 1)
            yield b + 4
            act.wait_ge(T("variance"), k)
            act.activation(small[:, par, 8:16], small[:, par, 0:8], ACT.Sqrt, scale=1.0 / D, bias=eps_t).then_inc(T("deviation"), 1)

        def norm_dve(dve, T, s, par, k, b, keep=True):
            SQ, EMB = W[par][5], W[par][6]
            yield b + 3
            dve.wait_ge(T("square"), k)
            dve.tensor_reduce(small[:, par, 0:8], rows(SQ), AX, A.add).then_inc(T("variance"), 1)
            yield b + 5
            dve.wait_ge(T("deviation"), k)
            dve.reciprocal(small[:, par, 16:24], small[:, par, 8:16]).then_inc(T("rstd"), 1)
            dve.wait_ge(T("rstd"), k)
            dve.wait_ge(T("emb_free"), k)
            dve.tensor_tensor(rows(EMB), rows(P[4 * par + 2][:, :]), per_row(small[:, par, 16:24]), A.mult).then_inc(T("emb"), 1)
            if keep:
                yield b + 7
                dve.wait_ge(T("x_fm"), k)
                dve.scalar_tensor_tensor(at(XD, s), at(MORE, s), 0.0, P[4 * par + 3][:, ::-1], A.is_equal, A.mult).then_inc(T("kept"), 1)

        def store_table(sp, T, table_k, s, par, k, b):
            yield b
            sp.wait_ge(T("emb"), k)
            sp.dma_start(rows_of(table_k, s * SE), W[par][6]).then_inc(T("stored"), 16)
            yield b + 3
            sp.wait_ge(T("stored"), k * 16)
            sp.sem_inc(T("emb_free"), 1)

        BACK = [W[0][5], W[1][5]]

        def pass_back(dve, S):
            dve.memset(car[:, :], 0.0).then_inc(S("car0"), 1)
            dve.wait_ge(S("car0"), 1)
            for par in range(2):
                dve.sem_inc(S(f"back_free{par}"), 1)

            def body(s, par, k, n):
                dve.wait_ge(S(f"back_free{par}"), k)
                settle(dve, S("settled"))
                B = BACK[par]
                for h in (1, 0):
                    lo, hi = 64 * h, 64 * h + 64
                    other = slice(64 - lo, 128 - lo)
                    x, more = (at(t, (NS - 1) - s)[lo:hi, :] for t in (XD, MORE))
                    dve.tensor_tensor_scan(B[lo:hi, ::-1], more, x, car[lo:hi, :], A.mult, A.add).then_inc(S(f"back{h}"), 1)
                    dve.wait_ge(S(f"back{h}"), n)
                    dve.tensor_copy(car[other, :], B[lo:hi, 0:1]).then_inc(S(f"back_carry{h}"), 1)
                    dve.wait_ge(S(f"back_carry{h}"), n)
            supers(dve, body)
            dve.wait_ge(S("back_free0"), NS // 2 + 2)
            dve.wait_ge(S("back_free1"), NS // 2 + 1)

        def keep_back(act, S, s, par, n):
            act.wait_ge(S("back_carry0"), n)
            act.activation(at(XD, (NS - 1) - s), BACK[par], ACT.Copy).then_inc(S(f"back_free{par}"), 1)

        def zero_carry(dve, S, value=0.0):
            dve.memset(car[:, :], value).then_inc(S("carry_start"), 1)
            dve.wait_ge(S("carry_start"), 1)

        def dense_pe(pe, T, par, c, b):
            VT = W[par][0]
            yield b + 2
            pe.wait_ge(T("vt"), c)
            for w, p in ((center, P[4 * par + 2]), (chain, P[4 * par + 3])):
                for q in range(4):
                    ins = pe.matmul(p[:, q * 128:(q + 1) * 128], VT[:, q * 128:(q + 1) * 128], w[:, :], start=True, stop=True)
                ins.then_inc(T("dense_mm"), 1)
            yield b + 9
            pe.wait_ge(T("y"), c)

        def sm(par, k):
            return small[:, par, k * 8:k * 8 + 8]

        def dense_act(act, T, par, c, b, m=None):
            DQ, Y = W[par][1], W[par][2]
            root = lambda dst, src, name: act.activation(sm(par, dst), sm(par, src), ACT.Sqrt, scale=1.0 / D, bias=eps_t).then_inc(T(name), 1)
            yield b + 3
            act.wait_ge(T("dense_mm"), 2 * c)
            act.activation(DQ, P[4 * par + 2][:, :], ACT.Square).then_inc(T("sq1"), 1)
            yield b + 5
            act.wait_ge(T("ss1"), c)
            root(1, 0, "sd1")
            yield b + 7
            act.wait_ge(T("ss2"), c)
            root(3, 2, "sd2")
            yield b + 9
            act.wait_ge(T("y"), c)
            act.activation(DQ, Y, ACT.Square).then_inc(T("sq2"), 1)
            yield b + 11
            act.wait_ge(T("ss3"), c)
            root(5, 4, "sd3")
            if m is not None:
                yield b + 13
                act.wait_ge(T("ss4"), m)
                root(7, 6, "sd4")

        def dense_dve(dve, T, par, c, b, m=None):
            DQ, Y, O1, O2, O3 = W[par][1], W[par][2], W[par][3], W[par][4], W[par][5]

            def twice(ss, sd, ss_next, a1, a2, a3, n2=c):
                dve.reciprocal(sd, sd).then_inc(T(a1), 1)
                dve.wait_ge(T(a1), c)
                dve.tensor_tensor(ss_next, ss, sd, A.mult).then_inc(T(a2), 1)
                dve.wait_ge(T(a2), n2)
                dve.tensor_tensor(ss_next, ss_next, sd, A.mult).then_inc(T(a3), 1)

            yield b + 4
            dve.wait_ge(T("sq1"), c)
            dve.tensor_reduce(sm(par, 0), rows(DQ), AX, A.add).then_inc(T("ss1"), 1)
            yield b + 6
            dve.wait_ge(T("sd1"), c)
            twice(sm(par, 0), sm(par, 1), sm(par, 2), "r1", "t2", "ss2")
            yield b + 8
            dve.wait_ge(T("sd2"), c)
            dve.reciprocal(sm(par, 3), sm(par, 3)).then_inc(T("r2"), 1)
            dve.wait_ge(T("r2"), c)
            dve.tensor_tensor(sm(par, 3), sm(par, 3), sm(par, 1), A.mult).then_inc(T("r12"), 1)
            dve.wait_ge(T("r12"), c)
            if m is None:
                dve.wait_ge(T("o_free"), c)
                dve.tensor_tensor(rows(O1), rows(P[4 * par + 2][:, :]), per_row(sm(par, 1)), A.mult)
                dve.tensor_tensor(rows(O2), rows(P[4 * par + 2][:, :]), per_row(sm(par, 3)), A.mult).then_inc(T("o12"), 1)
            dve.tensor_tensor(rows(Y), rows(P[4 * par + 3][:, :]), per_row(sm(par, 3)), A.mult).then_inc(T("y0"), 1)
            dve.wait_ge(T("y0"), c)
            dve.tensor_tensor(rows(Y), rows(Y), bias_row[:, :].rearrange("p (o f) -> p o f", o=1).to_broadcast([128, 8, D]),
                              A.add).then_inc(T("y"), 1)
            yield b + 10
            dve.wait_ge(T("sq2"), c)
            dve.tensor_reduce(sm(par, 4), rows(DQ), AX, A.add).then_inc(T("ss3"), 1)
            yield b + 12
            dve.wait_ge(T("sd3"), c)
            if m is None:
                dve.reciprocal(sm(par, 5), sm(par, 5)).then_inc(T("r3"), 1)
                dve.wait_ge(T("r3"), c)
                dve.tensor_tensor(rows(O3), rows(Y), per_row(sm(par, 5)), A.mult).then_inc(T("out_ready"), 1)
            else:
                twice(sm(par, 4), sm(par, 5), sm(par, 6), "r3", "t4", "ss4", m)
                yield b + 14
                dve.wait_ge(T("sd4"), m)
                dve.reciprocal(sm(par, 7), sm(par, 7)).then_inc(T("r4"), 1)
                dve.wait_ge(T("r4"), m)
                dve.tensor_tensor(sm(par, 7), sm(par, 7), sm(par, 5), A.mult).then_inc(T("r34"), 1)
                dve.wait_ge(T("r34"), m)
                dve.wait_ge(T("o_free"), c)
                dve.tensor_tensor(rows(O1), rows(Y), per_row(sm(par, 7)), A.mult).then_inc(T("out_ready"), 1)

        def node_pe(pe, T, par, c, m, b):
            yield b
            pe.wait_ge(T("xn"), m * 16)
            transpose4(pe, P[4 * par], XN[:, par, :]).then_inc(T("xt"), 1)
            pe.wait_ge(T("xt"), m)
            pe.sem_inc(T("xn_free"), 1)
            yield from dense_pe(pe, T, par, c, b)

        def node_act(act, T, par, c, m, b):
            yield b + 1
            act.wait_ge(T("xt"), m)
            act.activation(W[par][0], P[4 * par][:, :], ACT.Identity, bias=relub).then_inc(T("vt"), 1)
            yield from dense_act(act, T, par, c, b, m)

        def node_load(sp, T, par, m, b, first):
            yield b
            sp.wait_ge(T("xn_free"), m)
            sp.dma_start(XN[:, par, :], rows_of(a["x"], first)).then_inc(T("xn"), 16)

        def node_store(sp, T, par, c, m, b, first):
            yield b + 15
            sp.wait_ge(T("out_ready"), c)
            sp.dma_start(rows_of(out, first), W[par][3]).then_inc(T("stored_n"), 16)
            yield b + 18
            sp.wait_ge(T("stored_n"), m * 16)
            sp.sem_inc(T("o_free"), 1)

        def softmax_rows(block, S, logits, weights, K, slope, own):
            view = lambda i: work[:, i * 1024:i * 1024 + K * RC].rearrange("p (h c) -> p h c", h=K)
            L, T, R, X = (view(i) for i in range(4))
            LO, XO = (g[:, :, :].rearrange("p a c -> p (a c)")[:, 0:K * RC].rearrange("p (h c) -> p h c", h=K) for g in (GA, GB))
            all_ = lambda m: m[:, :].rearrange("p (o c) -> p o c", o=1).to_broadcast([128, K, RC])

            @block.sync
            def _(sp):
                for t, lo in ((L, 0), (T, K), (LO, 2 * K)) if own else ((L, 0),):
                    for h in range(K):
                        src = logits[lo + h, :] if own else logits
                        sp.dma_start(t[:, h, :], src.rearrange("(p c) -> p c", p=128)).then_inc(S("load"), 16)
                sp.wait_ge(S("weights"), 1)
                for t, lo in ((X, 0), (XO, K)) if own else ((X, 0),):
                    for h in range(K):
                        dst = weights[lo + h, :] if own else weights
                        sp.dma_start(dst.rearrange("(p c) -> p c", p=128), t[:, h, :]).then_inc(S("store"), 16)
                sp.wait_ge(S("store"), 16 * K * (1 + own))

            rounds = [0]

            @block.vector
            def _(dve):
                step = [0]

                def link(ins):
                    step[0] += 1
                    ins.then_inc(S("dve"), 1)
                    dve.wait_ge(S("dve"), step[0])

                def scan(src, dst, mask, op0, op1, start, down=False):
                    rounds[0] += 1
                    r = rounds[0]
                    d = (lambda x: x[:, ::-1]) if down else (lambda x: x)
                    for h in range(K):
                        link(dve.tensor_tensor_scan(d(dst[:, h, :]), d(mask[:, :]), d(src[:, h, :]), start, op0, op1))
                    edge = 0 if down else RC - 1
                    link(dve.tensor_copy(ends[:, 0:K], dst[:, :, edge]))
                    link(dve.tensor_reduce(red[:, 0:1], mask[:, :], AX, A.min))
                    link(dve.tensor_copy(ends[:, HEADS:HEADS + K], red[:, 0:1].to_broadcast([128, K])))
                    dve.nop().then_inc(S("ends"), 1)
                    dve.wait_ge(S("ends_row"), r)
                    link(dve.tensor_copy(carry[0:K, 0:256], P[0][0:K, 0:256]))
                    link(dve.memset(carry[0:K, 256:385], start))
                    into = carry[0:K, 256:384] if down else carry[0:K, 257:385]
                    link(dve.tensor_tensor_scan(d(into), d(carry[0:K, 128:256]), d(carry[0:K, 0:128]), start, op0, op1))
                    dve.nop().then_inc(S("carry"), 1)
                    dve.wait_ge(S("carry_in"), r)
                    link(dve.tensor_copy(carry_in[:, 0:K], P[1][:, 0:K]))
                    for h in range(K):
                        link(dve.tensor_tensor_scan(d(dst[:, h, :]), d(mask[:, :]), d(src[:, h, :]), carry_in[:, h:h + 1], op0, op1))

                def spread(t, dst):
                    link(dve.tensor_tensor(t, t, all_(row_last), A.mult))
                    scan(t, dst, row_more, A.mult, A.add, 0.0, down=True)

                dve.wait_ge(S("load"), 16 * K * (1 + 2 * own))
                if own:
                    link(dve.tensor_tensor(L, L, T, A.add))
                else:
                    link(dve.tensor_scalar(L, L, shift, None, A.add))
                link(dve.scalar_tensor_tensor(L, L, slope, L, A.mult, A.max))
                scan(L, T, row_neg, A.add, A.max, -BIG)
                spread(T, R)
                if own:
                    link(dve.scalar_tensor_tensor(LO, LO, slope, LO, A.mult, A.max))
                    link(dve.tensor_tensor(R, R, LO, A.max))
                    link(dve.tensor_tensor(LO, LO, R, A.subtract))
                link(dve.tensor_tensor(L, L, R, A.subtract))
                dve.nop().then_inc(S("shifted"), 1)
                dve.wait_ge(S("exp"), 1 + own)
                scan(X, T, row_same, A.mult, A.add, 0.0)
                spread(T, R)
                if own:
                    link(dve.tensor_tensor(R, R, XO, A.add))
                    link(dve.tensor_scalar(R, R, 1e-16, float(HEADS), A.add, A.mult))
                link(dve.reciprocal(R, R))
                link(dve.tensor_tensor(X, X, R, A.mult))
                if own:
                    link(dve.tensor_tensor(XO, XO, R, A.mult))
                dve.nop().then_inc(S("weights"), 1)

            @block.scalar
            def _(act):
                act.wait_ge(S("shifted"), 1)
                act.activation(X, L, ACT.Exp).then_inc(S("exp"), 1)
                if own:
                    act.activation(XO, LO, ACT.Exp).then_inc(S("exp"), 1)

            @block.tensor
            def _(pe):
                for r, down in enumerate((False, True, False, True)):
                    pe.wait_ge(S("ends"), r + 1)
                    pe.transpose(P[0][0:K, 0:128], ends[:, 0:K], ident[:, :])
                    pe.transpose(P[0][0:K, 128:256], ends[:, HEADS:HEADS + K], ident[:, :]).then_inc(S("ends_row"), 1)
                    pe.wait_ge(S("carry"), r + 1)
                    src = carry[0:K, 257:385] if down else carry[0:K, 256:384]
                    pe.transpose(P[1][:, 0:K], src, ident[0:K, 0:K]).then_inc(S("carry_in"), 1)


        NA_ = 48
        NB = NG + 1 - NA_
        SM = Sems("m_")
        with nc.Block() as block:
            cols = work[:, 7 * HW:7 * HW + HW + 2].bitcast(I32)

            @block.gpsimd
            def _(pool):
                def scatter(s, par, k, n):
                    pool.tensor_copy(win[:, par, 0:8], seg_i[:, bass.ds(s * 8, 8)]).then_inc(SM("window"), 1)
                    pool.tensor_copy(win[:, par, 8:16], row_i[:, bass.ds(s * 8, 8)]).then_inc(SM("window"), 1)
                    pool.wait_ge(SM("window"), n * 2)
                    settle(pool, SM("settled"))
                    for j in range(8):
                        pool.indirect_dma_start(rank, bass.IndirectOffsetOnAxis(ap=win[:, par, j:j + 1], axis=0),
                                                win[:, par, 8 + j:9 + j], None, bounds_check=N - 1, oob_is_err=False
                                                ).then_inc(SM(f"scattered{par}"), 16)

                with pool.Fori(0, NS // 2) as i:
                    scatter(2 * i, 0, i + 1, 2 * i + 1)
                    scatter(2 * i + 1, 1, i + 1, 2 * i + 2)
                    pool.wait_ge(SM("scattered0"), 128 * (i + 1))
                    pool.wait_ge(SM("scattered1"), 128 * (i + 1))
                scatter(NS - 1, 0, NS // 2 + 1, NS)
                pool.wait_ge(SM("scattered0"), 128 * (NS // 2 + 1))

            def loops(eng, node, mask=None):
                def body(i, firsts):
                    gens = [node(of(SM, par), par, i + 1, firsts[par]) for par in range(2)]
                    side_by_side(*gens, *([mask(i)] if mask else []))
                with eng.Fori(0, NB // 2 - 1) as i:
                    body(i, [(NA_ + 2 * i + par) * SE for par in range(2)])
                body(NB // 2 - 1, [(NG - 1) * SE, N - SE])

            @block.sync
            def _(sp):
                def node(T, par, k, first):
                    yield from node_load(sp, T, par, k, 0, first)
                    yield from node_store(sp, T, par, k, k, 0, first)

                def mask(i):
                    yield 0
                    sp.wait_ge(SM("cols_free"), i + 1)
                    for h in range(2):
                        sp.dma_start(cols[64 * h:64 * h + 64, :],
                                     a["dst_pad"][bass.ds(i * SE + h * HW, HW + 2)].rearrange("(o c) -> o c", o=1)
                                     .to_broadcast([64, HW + 2])).then_inc(SM("cols"), 16)
                with sp.Fori(0, NB // 2 - 1) as i:
                    side_by_side(*(node(of(SM, par), par, i + 1, (NA_ + 2 * i + par) * SE) for par in range(2)), mask(i))
                k = NB // 2
                side_by_side(node(of(SM, 0), 0, k, (NG - 1) * SE), node_load(sp, of(SM, 1), 1, k, 0, N - SE), mask(k - 1))
                side_by_side(node_store(sp, of(SM, 1), 1, k, k, 0, N - SE))

            @block.tensor
            def _(pe):
                for par in range(2):
                    pe.sem_inc(SM(f"xn_free{par}"), 1)
                loops(pe, lambda T, par, k, first: node_pe(pe, T, par, k, k, 0))

            @block.scalar
            def _(act):
                loops(act, lambda T, par, k, first: node_act(act, T, par, k, k, 0))

            @block.vector
            def _(dve):
                dve.sem_inc(SM("cols_free"), 1)
                for par in range(2):
                    dve.sem_inc(SM(f"o_free{par}"), 1)

                def mask(i):
                    yield 3
                    dve.wait_ge(SM("cols"), i * 32 + 32)
                    dve.tensor_tensor(at(SAME, i), cols[:, 1:HW + 1], cols[:, 0:HW], A.is_equal)
                    dve.tensor_tensor(at(MORE, i), cols[:, HW:0:-1], cols[:, HW + 1:1:-1], A.is_equal).then_inc(SM("mask"), 1)
                    yield 11
                    dve.wait_ge(SM("mask"), i + 1)
                    dve.sem_inc(SM("cols_free"), 1)
                loops(dve, lambda T, par, k, first: dense_dve(dve, T, par, k, 0, k), mask)
        SM.done()

        SA = Sems("a_")
        with nc.Block() as block:
            @block.gpsimd
            def _(pool):
                def body(s, par, k, n):
                    pool.wait_ge(SA(f"slot_free{par}"), k)
                    pool.wait_ge(SA(f"rank_kept{par}"), k)
                    pool.tensor_copy(win[:, par, 0:8], src_i[:, bass.ds(s * 8, 8)]).then_inc(SA("window"), 1)
                    pool.tensor_copy(win[:, par, 8:16], dst_i[:, bass.ds(s * 8, 8)]).then_inc(SA("window"), 1)
                    pool.wait_ge(SA("window"), n * 2)
                    settle(pool, SA("settled"))
                    for b, (buf, t) in enumerate(((GA, a["x"]), (GB, a["x"]), (None, rank))):
                        for j in range(8):
                            col = (b % 2) * 8 + j
                            dst = buf[:, par, j * D:(j + 1) * D] if buf is not None else win[:, par, 16 + j:17 + j]
                            pool.indirect_dma_start(dst, None, t, bass.IndirectOffsetOnAxis(ap=win[:, par, col:col + 1], axis=0)
                                                    ).then_inc(SA(f"gathered{par}"), 16)
                supers(pool, body)

            def streams(eng, edge, node):
                def body(s, par, k, tail=False):
                    T = of(SA, par)
                    per = 3
                    yield edge(T, s, par, k, per * (k - 1) + 1)
                    for j in range(0 if tail else 2):
                        yield node(T, par, per * (k - 1) + 2 + j, 2 * (k - 1) + j + 1, 16 + 16 * j, (2 * s + j) * SE)
                with eng.Fori(0, NS // 2) as i:
                    side_by_side(*(g for par in range(2) for g in body(2 * i + par, par, i + 1)))
                side_by_side(*body(NS - 1, 0, NS // 2 + 1, True))

            @block.tensor
            def _(pe):
                for par in range(2):
                    pe.sem_inc(SA(f"slot_free{par}"), 1)
                    pe.sem_inc(SA(f"xn_free{par}"), 1)

                def edge(T, s, par, k, c):
                    yield 0
                    pe.wait_ge(T("gathered"), k * 384)
                    transpose4(pe, P[4 * par], GA[:, par, :])
                    transpose4(pe, P[4 * par + 1], GB[:, par, :]).then_inc(T("ends_fm"), 1)
                    dense = dense_pe(pe, T, par, c, 0)
                    yield next(dense)
                    next(dense)
                    pe.wait_ge(T("ends_fm"), k)
                    pe.sem_inc(T("slot_free"), 1)
                    yield 3
                    pe.wait_ge(T("scan1"), k)
                    pe.wait_ge(T("sum_d"), k)
                    transpose4(pe, P[4 * par + 1], W[par][7]).then_inc(T("x_em"), 1)
                    yield 9
                    pe.wait_ge(T("emb"), k)
                    for _ in dense:
                        pass
                streams(pe, edge, lambda T, par, c, m, b, first: node_pe(pe, T, par, c, m, b))

            @block.scalar
            def _(act):
                def edge(T, s, par, k, c):
                    bank = P[4 * par][:, :], P[4 * par + 1][:, :]
                    hi, n_cols = (64, LASTC) if isinstance(s, int) else (128, HW)
                    yield 1
                    act.wait_ge(T("ends_fm"), k)
                    act.activation(at(XS, s), bank[0], ACT.Copy)
                    act.activation(at(XD, s), bank[1], ACT.Copy).then_inc(T("ends"), 1)
                    act.activation(W[par][0], bank[0], ACT.Identity, bias=relub).then_inc(T("vt"), 1)
                    act.activation(W[par][1][0:hi, 0:n_cols], bank[0][0:hi, 0:n_cols], ACT.Square,
                                   accum_out=stat[0:hi, 0, bass.ds(s, 1)]).then_inc(T("sum_s"), 1)
                    act.wait_ge(T("sum_s"), k)
                    act.activation(W[par][1][0:hi, 0:n_cols], bank[1][0:hi, 0:n_cols], ACT.Square,
                                   accum_out=stat[0:hi, 1, bass.ds(s, 1)]).then_inc(T("sum_d"), 1)
                    dense = dense_act(act, T, par, c, 0)
                    act.wait_ge(T("sum_d"), k)
                    step = next(dense)
                    yield step
                    step = next(dense)
                    yield 4
                    act.wait_ge(T("x_em"), k)
                    act.wait_ge(T("emb_free"), k)
                    act.activation(W[par][6], bank[1], ACT.Copy).then_inc(T("emb"), 1)
                    yield step
                    yield from dense
                streams(act, edge, lambda T, par, c, m, b, first: node_act(act, T, par, c, m, b))

            @block.vector
            def _(dve):
                for par in range(2):
                    for name in ("o_free", "rank_kept"):
                        dve.sem_inc(SA(f"{name}{par}"), 1)
                zero_carry(dve, SA)

                def edge(T, s, par, k, c):
                    V, F = W[par][8], W[par][7]
                    yield 2
                    dve.wait_ge(T("ends"), k)
                    dve.tensor_tensor(V, at(XS, s), at(XD, s), A.subtract).then_inc(T("v"), 1)
                    dve.tensor_copy(rank_t[:, bass.ds(s * 8, 8)], win[:, par, 16:24]).then_inc(T("rank_copied"), 1)
                    dve.wait_ge(T("v"), k)
                    seg_scan(dve, T, k, V, F, at(SAME, s), A.mult, A.add)
                    dve.wait_ge(T("rank_copied"), k)
                    dve.sem_inc(T("rank_kept"), 1)
                    yield from dense_dve(dve, T, par, c, 0)
                streams(dve, edge, lambda T, par, c, m, b, first: dense_dve(dve, T, par, c, b, m))

            @block.sync
            def _(sp):
                for par in range(2):
                    sp.sem_inc(SA(f"emb_free{par}"), 1)

                def edge(T, s, par, k, c):
                    yield from store_table(sp, T, table[0], s, par, k, 5)
                    yield 13
                    sp.wait_ge(T("out_ready"), c)
                    for i in range(3):
                        sp.dma_start(rows_of(table[i + 1], s * SE + EP), W[par][3 + i]).then_inc(T("stored_o"), 16)
                    yield 19
                    sp.wait_ge(T("stored_o"), k * 48)
                    sp.sem_inc(T("o_free"), 1)

                def node(T, par, c, m, b, first):
                    yield from node_load(sp, T, par, m, b - 10, first)
                    yield from node_store(sp, T, par, c, m, b, first)
                streams(sp, edge, node)
        SA.done()

        SB = Sems("b_")
        with nc.Block() as block:
            @block.vector
            def _(dve):
                step = [0]

                def link(ins):
                    step[0] += 1
                    ins.then_inc(SB("dve"), 1)
                    dve.wait_ge(SB("dve"), step[0])

                link(dve.tensor_scalar(t_i[:, :], row_i[:, :], float(EP + 1), None, A.add))
                link(dve.scalar_tensor_tensor(look_i[:, :], rank_t[:, :], 0.0, t_i[:, :], A.is_lt, A.mult))
                link(dve.tensor_tensor(t_i[:, :], look_i[:, :], rank_t[:, :], A.add))
                link(dve.tensor_copy(look_i[:, :], t_i[:, :]))
                link(dve.tensor_reduce(red[:, 0:2], stat[:, 0:2, :], AX, A.add))
                dve.nop().then_inc(SB("sums"), 1)
                dve.wait_ge(SB("norms"), 1)
                link(dve.tensor_tensor(red[:, 4:5], red[:, 2:3], red[:, 3:4], A.mult))
                link(dve.tensor_scalar(red[:, 5:6], red[:, 4:5], 1e-6, None, A.add))
                link(dve.reciprocal(inv_scale, red[:, 5:6]))
                link(dve.memset(car[:, :], 0.0))

            @block.tensor
            def _(pe):
                pe.wait_ge(SB("sums"), 1)
                pe.matmul(P[0][:, 0:2], ones[:, :], red[:, 0:2], start=True, stop=True).then_inc(SB("all"), 1)

            @block.scalar
            def _(act):
                act.wait_ge(SB("all"), 1)
                act.activation(red[:, 2:4], P[0][:, 0:2], ACT.Sqrt).then_inc(SB("norms"), 1)

        SB.done()

        S0 = Sems("c_")
        with nc.Block() as block:
            @block.gpsimd
            def _(pool):
                gather_rounds(pool, S0, look_i, table[0])

            @block.vector
            def _(dve):
                def stream(s, par, k):
                    T = of(S0, par)
                    PR, GT, V, F, OUT0 = (W[par][i] for i in (0, 2, 8, 7, 3))
                    yield 0
                    dve.tensor_tensor(PR, at(XS, s), at(XD, s), A.mult).then_inc(T("product"), 1)
                    yield 4
                    dve.wait_ge(T("logit"), k)
                    dve.tensor_scalar(GT, P[4 * par + 2][:, :], -5.0, 5.0, A.max, A.min).then_inc(T("clipped"), 1)
                    yield 6
                    dve.wait_ge(T("gate"), k)
                    dve.wait_ge(T("sums_fm"), k)
                    dve.tensor_tensor(V, P[4 * par][:, :], GT, A.mult).then_inc(T("v"), 1)
                    dve.wait_ge(T("v"), k)
                    seg_scan(dve, T, k, V, F, at(SAME, s), A.mult, A.add)
                    yield 9
                    dve.wait_ge(T("ffn"), k)
                    dve.tensor_tensor(W[par][4], at(XD, s), OUT0, A.add).then_inc(T("u"), 1)
                    yield from norm_dve(dve, T, s, par, k, 9)
                pairs(dve, stream)

            @block.tensor
            def _(pe):
                for par in range(2):
                    pe.sem_inc(S0(f"slot_free{par}"), 1)

                def stream(s, par, k):
                    T = of(S0, par)
                    bank = [P[4 * par + i][:, :] for i in range(4)]
                    yield 1
                    pe.wait_ge(T("product"), k)
                    pe.matmul(bank[1], proj[:, :], W[par][0], start=True, stop=True).then_inc(T("cos"), 1)
                    yield 3
                    pe.wait_ge(T("relu"), k)
                    pe.matmul(bank[2], total[:, :], W[par][1], start=True, stop=True).then_inc(T("logit"), 1)
                    yield 5
                    pe.wait_ge(T("gathered"), k * 128)
                    transpose4(pe, bank[0], GA[:, par, :]).then_inc(T("sums_fm"), 1)
                    pe.wait_ge(T("sums_fm"), k)
                    pe.sem_inc(T("slot_free"), 1)
                    yield 7
                    pe.wait_ge(T("scan1"), k)
                    pe.matmul(bank[1], wffn[:, :], W[par][7], start=True, stop=True).then_inc(T("ffn_mm"), 1)
                    yield from norm_pe(pe, T, par, k, 9)
                pairs(pe, stream)

            @block.scalar
            def _(act):
                def stream(s, par, k):
                    T = of(S0, par)
                    bank1 = P[4 * par + 1][:, :]
                    yield 2
                    act.wait_ge(T("cos"), k)
                    act.activation(W[par][1], bank1, ACT.Relu, scale=inv_scale).then_inc(T("relu"), 1)
                    yield 5
                    act.wait_ge(T("clipped"), k)
                    act.activation(W[par][2], W[par][2], ACT.Exp).then_inc(T("gate"), 1)
                    yield 8
                    act.wait_ge(T("ffn_mm"), k)
                    act.activation(W[par][3], bank1, ACT.Relu, bias=bff).then_inc(T("ffn"), 1)
                    yield from norm_act(act, T, par, k, 9)
                pairs(act, stream)

            @block.sync
            def _(sp):
                for par in range(2):
                    sp.sem_inc(S0(f"emb_free{par}"), 1)
                pairs(sp, lambda s, par, k: store_table(sp, of(S0, par), table[1], s, par, k, 15))
        S0.done()

        S1 = Sems("d_")
        with nc.Block() as block:
            @block.gpsimd
            def _(pool):
                gather_rounds(pool, S1, look_i, table[1])

            @block.vector
            def _(dve):
                pass_back(dve, S1)

                def sums(s, par, k, n):
                    hi, c = (64, LASTC) if isinstance(s, int) else (128, HW)
                    dve.tensor_reduce(stat[0:hi, 3, bass.ds(s, 1)], at(XD, s)[0:hi, 0:c], AX, A.add)
                supers(dve, sums)

            @block.tensor
            def _(pe):
                for par in range(2):
                    pe.sem_inc(S1(f"slot_free{par}"), 1)
                    pe.sem_inc(S1(f"fm_kept{par}"), 1)

                def body(s, par, k, n):
                    pe.wait_ge(S1(f"gathered{par}"), k * 128)
                    pe.wait_ge(S1(f"fm_kept{par}"), k)
                    transpose4(pe, P[par], GA[:, par, :]).then_inc(S1(f"fm{par}"), 1)
                    pe.wait_ge(S1(f"fm{par}"), k)
                    pe.sem_inc(S1(f"slot_free{par}"), 1)
                supers(pe, body)

            @block.scalar
            def _(act):
                def body(s, par, k, n):
                    keep_back(act, S1, s, par, n)
                    act.wait_ge(S1(f"fm{par}"), k)
                    hi, c = (64, LASTC) if isinstance(s, int) else (128, HW)
                    act.activation(W[par][0][0:hi, 0:c], P[par][0:hi, 0:c], ACT.Copy,
                                   accum_out=stat[0:hi, 2, bass.ds(s, 1)])
                    act.activation(at(XS, s), P[par][:, :], ACT.Copy).then_inc(S1(f"fm_kept{par}"), 1)
                supers(act, body)
        S1.done()

        def load_attributes(sp, T, s, par):
            for h in range(2):
                sp.dma_start(W[par][1][64 * h:64 * h + 2, :], a["attr"][:, bass.ds(s * SE + h * HW, HW)]).then_inc(T("eat"), 16)

        def load_weights(sp, sem, w, t, s):
            for h in range(2):
                sp.dma_start(t[64 * h:64 * h + 64, :], w[bass.ds(s * SE + h * HW, HW)].rearrange("(o c) -> o c", o=1)
                             .to_broadcast([64, HW])).then_inc(sem, 16)

        S2 = Sems("e_")
        with nc.Block() as block:
            @block.vector
            def _(dve):
                step = [0]

                def link(ins):
                    step[0] += 1
                    ins.then_inc(S2("dve"), 1)
                    dve.wait_ge(S2("dve"), step[0])

                for par in range(2):
                    link(dve.memset(W[par][1], 0.0))
                    dve.sem_inc(S2(f"eat_free{par}"), 1)
                link(dve.tensor_reduce(red[:, 0:2], stat[:, 2:4, :], AX, A.add))
                dve.nop().then_inc(S2("sums"), 1)
                dve.wait_ge(S2("folded"), 1)
                link(dve.tensor_copy(red[:, 2:4], P[0][:, 0:2]))
                dve.nop().then_inc(S2("means"), 1)
                dve.wait_ge(S2("mu"), 1)
                link(dve.tensor_scalar(vec[:, 9:11], P[1][:, 0:2], -1.0 / E, None, A.mult))
                dve.nop().then_inc(S2("mu_ready"), 1)

                def stream(s, par, k):
                    T = of(S2, par)
                    hi, c = (64, LASTC) if isinstance(s, int) else (128, HW)
                    yield 2
                    for side, mu in enumerate((mu_s, mu_d)):
                        dve.wait_ge(T(f"square{side}"), k)
                        dve.scalar_tensor_tensor(W[par][5 + side][0:hi, 0:c], P[4 * par + side][0:hi, 0:c], mu[0:hi, :],
                                                 W[par][3 + side][0:hi, 0:c], A.add, A.mult,
                                                 accum_out=stat[0:hi, 5 + 2 * side, bass.ds(s, 1)]).then_inc(T(f"cube{side}"), 1)
                pairs(dve, stream)
                for par in range(2):
                    dve.wait_ge(S2(f"cube1{par}"), NS // 2 + 1 - par)
                    dve.wait_ge(S2(f"square1{par}"), NS // 2 + 1 - par)
                link(dve.tensor_reduce(red[:, 4:8], stat[:, 4:8, :], AX, A.add))
                dve.nop().then_inc(S2("moment_sums"), 1)
                dve.wait_ge(S2("moments"), 1)
                m = red[:, 8:12]
                link(dve.tensor_scalar(m, P[0][:, 4:8], 1.0 / E, None, A.mult))
                link(dve.scalar_tensor_tensor(red[:, 12:16], m, -1.0, m, A.mult, A.max))
                dve.nop().then_inc(S2("abs"), 1)
                link(dve.tensor_scalar(red[:, 16:20], m, 0.0, None, A.is_gt))
                link(dve.tensor_scalar(red[:, 20:24], m, 0.0, None, A.is_lt))
                link(dve.tensor_tensor(red[:, 16:20], red[:, 16:20], red[:, 20:24], A.subtract))
                dve.wait_ge(S2("root"), 1)
                link(dve.tensor_tensor(red[:, 16:20], red[:, 16:20], red[:, 24:28], A.mult))
                link(dve.tensor_tensor(red[:, 16:20], red[:, 16:20], grad[:, :], A.mult))
                link(dve.tensor_reduce(red[:, 28:29], red[:, 16:20], AX, A.add))
                dve.nop().then_inc(S2("weighted"), 1)
                dve.wait_ge(S2("shifted"), 1)
                link(dve.tensor_copy(shift, P[0][:, 8:9]))

            @block.gpsimd
            def _(pool):
                pool.memset(small[:, 0, 0:4:2], 0.5).then_inc(S2("exponents"), 1)
                pool.memset(small[:, 0, 1:4:2], 1.0 / 3.0).then_inc(S2("exponents"), 1)
                pool.wait_ge(S2("exponents"), 2)
                pool.wait_ge(S2("abs"), 1)
                pool.tensor_tensor(red[:, 24:28], red[:, 12:16], small[:, 0, 0:4], A.pow).then_inc(S2("root"), 1)

            @block.tensor
            def _(pe):
                pe.wait_ge(S2("sums"), 1)
                pe.matmul(P[0][:, 0:2], fold[:, :], red[:, 0:2], start=True, stop=True).then_inc(S2("folded"), 1)
                pe.wait_ge(S2("means"), 1)
                pe.matmul(P[1][:, 0:2], wfc[:, :], red[:, 2:4], start=True, stop=True).then_inc(S2("mu"), 1)
                pe.wait_ge(S2("mu_ready"), 1)

                def stream(s, par, k):
                    T = of(S2, par)
                    bank = [P[4 * par + i] for i in range(3)]
                    yield 0
                    pe.matmul(bank[0][:, :], wfc[:, :], at(XS, s), start=True, stop=True).then_inc(T("z"), 1)
                    pe.matmul(bank[1][:, :], wfc[:, :], at(XD, s), start=True, stop=True).then_inc(T("z"), 1)
                    pe.matmul(bank[2][0:2, :], one_l[:, 0:2], at(XS, s), start=True, stop=False)
                    pe.matmul(bank[2][0:2, :], one_l[:, 2:4], at(XD, s), start=False, stop=False)
                    pe.wait_ge(T("eat"), k * 32)
                    pe.matmul(bank[2][0:2, :], one_l[:, 4:6], W[par][1], start=False, stop=True).then_inc(T("logit"), 1)
                    yield 3
                    pe.wait_ge(T("logit"), k)
                    pe.sem_inc(T("eat_free"), 1)
                    pe.wait_ge(T("cube1"), k)
                    pe.wait_ge(T("row"), k)
                pairs(pe, stream)
                pe.wait_ge(S2("moment_sums"), 1)
                pe.matmul(P[0][:, 4:8], fold[:, :], red[:, 4:8], start=True, stop=True).then_inc(S2("moments"), 1)
                pe.wait_ge(S2("weighted"), 1)
                pe.matmul(P[0][:, 8:9], total[:, :], red[:, 28:29], start=True, stop=True).then_inc(S2("shifted"), 1)

            @block.scalar
            def _(act):
                def stream(s, par, k):
                    T = of(S2, par)
                    hi, c = (64, LASTC) if isinstance(s, int) else (128, HW)
                    yield 1
                    act.wait_ge(T("z"), 2 * k)
                    for side, mu in enumerate((mu_s, mu_d)):
                        act.activation(W[par][3 + side][0:hi, 0:c], P[4 * par + side][0:hi, 0:c], ACT.Square, bias=mu[0:hi, :],
                                       accum_out=stat[0:hi, 4 + 2 * side, bass.ds(s, 1)]).then_inc(T(f"square{side}"), 1)
                    yield 2
                    act.wait_ge(T("logit"), k)
                    act.wait_ge(T("row_free"), k)
                    act.activation(W[par][2][0:2, :], P[4 * par + 2][0:2, :], ACT.Copy).then_inc(T("row"), 1)
                pairs(act, stream)

            @block.sync
            def _(sp):
                for par in range(2):
                    sp.sem_inc(S2(f"row_free{par}"), 1)

                def stream(s, par, k):
                    T = of(S2, par)
                    yield -1
                    sp.wait_ge(T("eat_free"), k)
                    load_attributes(sp, T, s, par)
                    yield 3
                    sp.wait_ge(T("row"), k)
                    sp.dma_start(logit1_d[bass.ds(s * SE, SE)].rearrange("(a c) -> a c", a=2), W[par][2][0:2, :]).then_inc(T("stored"), 16)
                    yield 5
                    sp.wait_ge(T("stored"), k * 16)
                    sp.sem_inc(T("row_free"), 1)
                pairs(sp, stream)
        S2.done()

        SF = Sems("f_")
        with nc.Block() as block:
            softmax_rows(block, SF, logit1_d, weight1_d, 1, 0.01, False)
        SF.done()

        S3 = Sems("g_")
        with nc.Block() as block:
            @block.sync
            def _(sp):
                for par in range(2):
                    sp.sem_inc(S3(f"emb_free{par}"), 1)

                def stream(s, par, k):
                    T = of(S3, par)
                    yield -1
                    sp.wait_ge(T("in_free"), k)
                    load_attributes(sp, T, s, par)
                    load_weights(sp, T("weights"), weight1_d, W[par][0], s)
                    yield from store_table(sp, T, table[2], s, par, k, 8)
                pairs(sp, stream)

            @block.tensor
            def _(pe):
                pe.wait_ge(S3("start"), 1)

                def stream(s, par, k):
                    T = of(S3, par)
                    yield 1
                    pe.matmul(P[4 * par][:, :], wfc[:, :], at(XS, s), start=True, stop=False)
                    pe.wait_ge(T("eat"), k * 32)
                    pe.matmul(P[4 * par][:, :], eprj[:, :], W[par][1], start=False, stop=True).then_inc(T("message"), 1)
                    yield from norm_pe(pe, T, par, k, 2)
                pairs(pe, stream)

            @block.vector
            def _(dve):
                for par in range(2):
                    dve.memset(W[par][1], 0.0).then_inc(S3("attr0"), 1)
                dve.wait_ge(S3("attr0"), 2)
                for par in range(2):
                    dve.sem_inc(S3(f"in_free{par}"), 1)
                dve.sem_inc(S3("start"), 1)
                zero_carry(dve, S3)

                def stream(s, par, k):
                    T = of(S3, par)
                    V, F = W[par][8], W[par][7]
                    yield 2
                    dve.wait_ge(T("message"), k)
                    dve.wait_ge(T("weights"), k * 32)
                    dve.tensor_tensor(V, P[4 * par][:, :], W[par][0], A.mult).then_inc(T("v"), 1)
                    dve.wait_ge(T("v"), k)
                    dve.sem_inc(T("in_free"), 1)
                    seg_scan(dve, T, k, V, F, at(SAME, s), A.mult, A.add)
                    dve.tensor_tensor(W[par][4], at(XD, s), F, A.add).then_inc(T("u"), 1)
                    yield from norm_dve(dve, T, s, par, k, 2)
                pairs(dve, stream)

            @block.scalar
            def _(act):
                pairs(act, lambda s, par, k: norm_act(act, of(S3, par), par, k, 2))
        S3.done()

        S4 = Sems("h_")
        with nc.Block() as block:
            @block.gpsimd
            def _(pool):
                gather_rounds(pool, S4, look_i, table[2])

            @block.vector
            def _(dve):
                pass_back(dve, S4)

            @block.tensor
            def _(pe):
                for par in range(2):
                    pe.sem_inc(S4(f"slot_free{par}"), 1)
                    pe.sem_inc(S4(f"read{par}"), 1)

                def body(s, par, k, n):
                    bank = P[4 * par:4 * par + 3]
                    pe.wait_ge(S4(f"read{par}"), k)
                    pe.wait_ge(S4(f"back_free{par}"), k + 1)
                    pe.matmul(bank[1][0:16, :], two_l[:, 16:32], at(XD, (NS - 1) - s), start=True, stop=True).then_inc(S4(f"dst_part{par}"), 1)
                    pe.wait_ge(S4(f"gathered{par}"), k * 128)
                    transpose4(pe, bank[0], GA[:, par, :]).then_inc(S4(f"fm{par}"), 1)
                    pe.wait_ge(S4(f"fm{par}"), k)
                    pe.sem_inc(S4(f"slot_free{par}"), 1)
                    pe.wait_ge(S4(f"fm_kept{par}"), k)
                    pe.matmul(bank[2][0:8, :], two_l[:, 0:8], at(XS, s), start=True, stop=True).then_inc(S4(f"src_part{par}"), 1)
                supers(pe, body)

            @block.scalar
            def _(act):
                def body(s, par, k, n):
                    keep_back(act, S4, s, par, n)
                    act.wait_ge(S4(f"fm{par}"), k)
                    act.activation(at(XS, s), P[4 * par][:, :], ACT.Copy).then_inc(S4(f"fm_kept{par}"), 1)
                    act.wait_ge(S4(f"row_free{par}"), k)
                    act.wait_ge(S4(f"dst_part{par}"), k)
                    act.activation(W[par][1][0:16, :], P[4 * par + 1][0:16, :], ACT.Copy)
                    act.wait_ge(S4(f"src_part{par}"), k)
                    act.activation(W[par][2][0:8, :], P[4 * par + 2][0:8, :], ACT.Copy).then_inc(S4(f"read{par}"), 1)
                supers(act, body)

            @block.sync
            def _(sp):
                for par in range(2):
                    sp.sem_inc(S4(f"row_free{par}"), 1)

                def stream(s, par, k):
                    T = of(S4, par)
                    yield 0
                    sp.wait_ge(T("read"), k + 1)
                    for h in range(2):
                        sp.dma_start(logit2_d[0:HEADS, bass.ds(s * SE + h * HW, HW)], W[par][2][h:8:2, :]).then_inc(T("stored"), 16)
                        sp.dma_start(logit2_d[HEADS:3 * HEADS, bass.ds(((NS - 1) - s) * SE + h * HW, HW)], W[par][1][h:16:2, :]).then_inc(T("stored"), 16)
                    yield 1
                    sp.wait_ge(T("stored"), k * 64)
                    sp.sem_inc(T("row_free"), 1)
                pairs(sp, stream)
        S4.done()

        SI = Sems("i_")
        with nc.Block() as block:
            softmax_rows(block, SI, logit2_d, weight2_d, HEADS, 0.2, True)
        SI.done()

        S5 = Sems("j_")
        HB = [[GA[:, par, :], GB[:, par, :], XN[:, par, :], W[par][8]] for par in range(2)]
        with nc.Block() as block:
            @block.sync
            def _(sp):
                for par in range(2):
                    sp.sem_inc(S5(f"emb_free{par}"), 1)
                    sp.sem_inc(S5(f"first{par}"), 1)

                def stream(s, par, k):
                    T = of(S5, par)
                    for side in range(2):
                        yield (-1, 1)[side]
                        sp.wait_ge(T("weights_free"), 2 * (k - 1) + side + 1)
                        for h in range(HEADS):
                            load_weights(sp, T("weights"), weight2_d[side * HEADS + h, :], HB[par][h], s)
                    yield from store_table(sp, T, table[3], s, par, k, 12)
                pairs(sp, stream)

            @block.vector
            def _(dve):
                for par in range(2):
                    dve.sem_inc(S5(f"weights_free{par}"), 1)
                zero_carry(dve, S5)

                def stream(s, par, k):
                    T = of(S5, par)
                    F, V = W[par][7], W[par][5]
                    for side, x in enumerate((XS, XD)):
                        yield (1, 4)[side]
                        if side == 1:
                            dve.wait_ge(T("message"), k)
                        dve.wait_ge(T("weights"), (2 * (k - 1) + side + 1) * 32 * HEADS)
                        for h in range(HEADS):
                            ins = dve.tensor_tensor(W[par][h], at(x, s), HB[par][h], A.mult)
                        ins.then_inc(T("scaled"), 1)
                        dve.wait_ge(T("scaled"), 2 * (k - 1) + side + 1)
                        dve.sem_inc(T("weights_free"), 1)
                    yield 6
                    seg_scan(dve, T, k, P[4 * par], F, at(SAME, s), A.mult, A.add)
                    dve.wait_ge(T("self"), k)
                    dve.scalar_tensor_tensor(V, P[4 * par + 1][:, :], bias2, F, A.add, A.add).then_inc(T("v"), 1)
                    dve.wait_ge(T("v"), k)
                    dve.tensor_tensor(W[par][4], V, at(XD, s), A.add).then_inc(T("u"), 1)
                    yield from norm_dve(dve, T, s, par, k, 6)
                pairs(dve, stream)

            @block.tensor
            def _(pe):
                def stream(s, par, k):
                    T = of(S5, par)
                    for side, name in ((0, "message"), (1, "self")):
                        yield (2, 5)[side]
                        pe.wait_ge(T("scaled"), 2 * (k - 1) + side + 1)
                        for h in range(HEADS):
                            ins = pe.matmul(P[4 * par + side][:, :], wh[h][:, :], W[par][h], start=(h == 0), stop=(h == HEADS - 1))
                        ins.then_inc(T(name), 1)
                    yield from norm_pe(pe, T, par, k, 6)
                pairs(pe, stream)

            @block.scalar
            def _(act):
                pairs(act, lambda s, par, k: norm_act(act, of(S5, par), par, k, 6))
        S5.done()

        S8 = Sems("p_")
        with nc.Block() as block:
            @block.vector
            def _(dve):
                pass_back(dve, S8)

            @block.scalar
            def _(act):
                supers(act, lambda s, par, k, n: keep_back(act, S8, s, par, n))
        S8.done()

        S6 = Sems("k_")
        with nc.Block() as block:
            @block.gpsimd
            def _(pool):
                def gather(s, par, k):
                    pool.wait_ge(S6(f"slot_free{par}"), k)
                    pool.tensor_copy(win[:, par, 0:8], look_i[:, bass.ds(s * 8, 8)]).then_inc(S6(f"window{par}"), 1)
                    pool.wait_ge(S6(f"window{par}"), k)
                    settle(pool, S6("settled"))
                    for j in range(8):
                        pool.indirect_dma_start(GA[:, par, j * D:(j + 1) * D], None, table[3],
                                                bass.IndirectOffsetOnAxis(ap=win[:, par, j:j + 1], axis=0)
                                                ).then_inc(S6(f"gathered{par}"), 16)

                def scatter(s, par, k):
                    pool.wait_ge(S6(f"emb{par}"), k)
                    pool.tensor_copy(win[:, par, 8:16], seg_i[:, bass.ds(s * 8, 8)]).then_inc(S6(f"seg_window{par}"), 1)
                    pool.wait_ge(S6(f"seg_window{par}"), k)
                    settle(pool, S6("settled"))
                    for j in range(8):
                        pool.indirect_dma_start(out, bass.IndirectOffsetOnAxis(ap=win[:, par, 8 + j:9 + j], axis=0),
                                                W[par][6][:, j * D:(j + 1) * D], None, bounds_check=N - 1, oob_is_err=False
                                                ).then_inc(S6(f"scattered{par}"), 16)

                gather(0, 0, 1)
                gather(1, 1, 1)
                with pool.Fori(0, NS // 2 - 1) as i:
                    for par in range(2):
                        gather(2 * i + 2 + par, par, i + 2)
                    for par in range(2):
                        scatter(2 * i + par, par, i + 1)
                gather(NS - 1, 0, NS // 2 + 1)
                scatter(NS - 3, 0, NS // 2)
                scatter(NS - 2, 1, NS // 2)
                scatter(NS - 1, 0, NS // 2 + 1)
                pool.wait_ge(S6("scattered0"), 128 * (NS // 2 + 1))
                pool.wait_ge(S6("scattered1"), 128 * (NS // 2))

            @block.sync
            def _(sp):
                for par in range(2):
                    sp.sem_inc(S6(f"emb_free{par}"), 1)

                def stream(s, par, k):
                    yield 0
                    sp.wait_ge(S6(f"scattered{par}"), k * 128)
                    sp.sem_inc(S6(f"emb_free{par}"), 1)
                pairs(sp, stream)

            @block.vector
            def _(dve):
                zero_carry(dve, S6, -BIG)

                def stream(s, par, k):
                    T = of(S6, par)
                    NEG, FIN, Z0, MX = (W[par][i] for i in (0, 3, 8, 7))
                    yield 0
                    dve.tensor_scalar(NEG, at(SAME, s), -1.0, BIG, A.add, A.mult)
                    dve.memset(Z0, 0.0).then_inc(T("neg"), 1)
                    yield 5
                    dve.wait_ge(T("neg"), k)
                    dve.wait_ge(T("message"), k)
                    seg_scan(dve, T, k, P[4 * par], MX, NEG, A.add, A.max)
                    dve.tensor_scalar(MX, MX, b2, None, A.add).then_inc(T("b2"), 1)
                    dve.wait_ge(T("b2"), k)
                    dve.tensor_scalar(FIN, MX, -FMAX, FMAX, A.max, A.min).then_inc(T("clipped"), 1)
                    dve.wait_ge(T("clipped"), k)
                    dve.tensor_tensor(FIN.bitcast(I32), FIN, MX, A.is_equal).then_inc(T("finite"), 1)
                    dve.wait_ge(T("finite"), k)
                    settle(dve, S6("settled_dve"))
                    dve.copy_predicated(Z0, FIN.bitcast(I32), MX).then_inc(T("out3"), 1)
                    dve.wait_ge(T("out3"), k)
                    dve.tensor_tensor(W[par][4], Z0, at(XD, s), A.add).then_inc(T("u"), 1)
                    yield from norm_dve(dve, T, s, par, k, 5, keep=False)
                pairs(dve, stream)

            @block.tensor
            def _(pe):
                for par in range(2):
                    pe.sem_inc(S6(f"slot_free{par}"), 1)

                def stream(s, par, k):
                    T = of(S6, par)
                    bank = [P[4 * par + i][:, :] for i in range(2)]
                    yield 0
                    pe.wait_ge(T("gathered"), k * 128)
                    transpose4(pe, bank[0], GA[:, par, :]).then_inc(T("fm"), 1)
                    pe.matmul(bank[1], w1d[:, :], at(XD, s), start=True, stop=False)
                    pe.wait_ge(T("fm"), k)
                    pe.sem_inc(T("slot_free"), 1)
                    yield 2
                    pe.wait_ge(T("fm_kept"), k)
                    pe.matmul(bank[1], w1s[:, :], W[par][1], start=False, stop=True).then_inc(T("hidden_mm"), 1)
                    yield 4
                    pe.wait_ge(T("hidden"), k)
                    pe.matmul(bank[0], w2[:, :], W[par][2], start=True, stop=True).then_inc(T("message"), 1)
                    yield from norm_pe(pe, T, par, k, 5, keep=False)
                pairs(pe, stream)

            @block.scalar
            def _(act):
                def stream(s, par, k):
                    T = of(S6, par)
                    yield 1
                    act.wait_ge(T("fm"), k)
                    act.activation(W[par][1], P[4 * par][:, :], ACT.Copy).then_inc(T("fm_kept"), 1)
                    yield 3
                    act.wait_ge(T("hidden_mm"), k)
                    act.activation(W[par][2], P[4 * par + 1][:, :], ACT.Relu, bias=b1).then_inc(T("hidden"), 1)
                    yield from norm_act(act, T, par, k, 5)
                pairs(act, stream)


def kernel(**inputs):
    import concourse.bacc as bacc
    from concourse.bass_utils import run_bass_kernel_spmd

    x = {k: np.ascontiguousarray(v) for k, v in inputs.items()}
    src, dst = x["src"], x["dst"]
    pad = EP - E
    src_p = np.concatenate([src, np.zeros(pad, np.int32)])
    dst_p = np.concatenate([np.full(1, -1, np.int32), dst, np.full(pad, N, np.int32), np.full(1, N + 1, np.int32)])

    def columns(v):
        return np.ascontiguousarray(v.reshape(NS, 2, 4, 128).transpose(3, 0, 2, 1).reshape(128, NS * 8))

    half = np.kron(np.eye(2, dtype=np.float32), np.ones((D, D), np.float32))
    eye = np.eye(128, dtype=np.float32)
    const = np.concatenate([eye, eye - half / D, half / D, half, np.kron(np.ones((2, 2), np.float32), np.eye(D, dtype=np.float32)),
                            np.ones((128, 128), np.float32)], axis=1).astype(np.float32)
    attr = np.zeros((2, EP), np.float32)
    attr[:, :E] = x["edge_attr_2"].T
    wa = x["L1_gnn_W_attn"][0]
    arrays = {
        "x": x["x"], "src_l": columns(src_p), "dst_l": columns(dst_p[1:EP + 1]), "next_l": columns(dst_p[2:EP + 2]),
        "dst_pad": dst_p, "attr": attr, "const": const,
        "proj": x["L0_gnn_proj_cosim"], "wffnT": x["L0_gnn_W_ffn"].T, "b_ffn": x["L0_gnn_b_ffn"],
        "wfcT": x["L1_gnn_W_fc"].T, "wfc": x["L1_gnn_W_fc"], "blkT": wa[:6 * D].reshape(6, D).T, "we": wa[6 * D:].reshape(2, 1),
        "wedge": x["L1_gnn_W_edge"], "we2nT": x["L1_gnn_W_e2n"].T, "wm1": x["L1_gnn_W_m1"], "wm2": x["L1_gnn_W_m2"],
        "w2l": x["L2_gnn_W"], "att": np.concatenate([x["L2_gnn_att_src"].ravel(), x["L2_gnn_att_dst"].ravel()]),
        "bias2": x["L2_gnn_bias"],
        "w1a": x["L3_gnn_W1"][:D], "w1b": x["L3_gnn_W1"][D:], "b1": x["L3_gnn_b1"], "w2": x["L3_gnn_W2"], "b2": x["L3_gnn_b2"],
    }
    nc = bacc.Bacc("TRN2", target_bir_lowering=False, num_devices=1)
    given, aps = {}, {}
    for name, v in arrays.items():
        v = np.ascontiguousarray(v)
        given[f"in_{name}"] = v
        aps[name] = nc.dram_tensor(f"in_{name}", v.shape, mybir.dt.from_np(v.dtype), kind="ExternalInput").ap()
    out = nc.dram_tensor("out_x", [N, D], F32, kind="ExternalOutput").ap()
    build(nc, aps, out)
    return run_bass_kernel_spmd(nc, [given], core_ids=[0]).results[0]["out_x"]
```

```python
import numpy as np
from contextlib import ExitStack
from functools import partial
import concourse.bass as bass
from concourse import mybir

N, D, E = 100000, 64, 25000
SE = 1024
NS = (E + SE - 1) // SE
EP = NS * SE
LASTC = E - (NS - 1) * SE
HW = 512
NG = N // SE
RC = EP // 128
HEADS = 4
EPS = 1e-5
BIG = 3e38
FMAX = 3.4028234663852886e38
PARTS = 3
FAR = 1 << 20

F32, I32, U8, BF16 = mybir.dt.float32, mybir.dt.int32, mybir.dt.uint8, mybir.dt.bfloat16
A = mybir.AluOpType
ACT = mybir.ActivationFunctionType
AX = mybir.AxisListType.X


def supers(eng, body):
    with eng.Fori(0, NS // 2) as i:
        body(2 * i, 0, i + 1, 2 * i + 1)
        body(2 * i + 1, 1, i + 1, 2 * i + 2)
    body(NS - 1, 0, NS // 2 + 1, NS)


def merge(*streams):
    at = [[next(g), i, g] for i, g in enumerate(streams)]
    while at:
        first = min(at, key=lambda x: x[:2])
        yield first[0]
        try:
            first[0] = next(first[2])
        except StopIteration:
            at.remove(first)


def side_by_side(*streams):
    for _ in merge(*streams):
        pass


def pairs(eng, *makers):
    with eng.Fori(0, NS // 2) as i:
        side_by_side(*(m(2 * i + par, par, i + 1) for par in range(2) for m in makers))
    side_by_side(*(m(NS - 1, 0, NS // 2 + 1) for m in makers))


def together(*parts):
    return lambda T, s, par, k: merge(*(part(T, s, par, k) for part in parts))


def pipelined(eng, S, *stages):
    def slot(first, i):
        going = []
        for d, stage in reversed(list(enumerate(stages))):
            s = first - d
            if s >= 0 and (i is not None or s < NS):
                at_s, turn = (s, 0) if i is None else (2 * i + s, i)
                if stage is not None:
                    going.append(stage(of(S, s % 2), at_s, s % 2, turn + (s // 2 + 1)))
        side_by_side(*going)

    lead = len(stages) // 2 * 2
    turns = (NS - lead) // 2
    for t in range(lead):
        slot(t, None)
    with eng.Fori(0, turns) as i:
        slot(lead, i)
        slot(lead + 1, i)
    for t in range(lead + 2 * turns, NS + len(stages) - 1):
        slot(t, None)


def of(S, par):
    return lambda name: S(f"{name}{par}")


def settle(eng, sem):
    eng.sem_inc(sem, 1)


def per_row(t):
    return t.rearrange("p (j o) -> p j o", o=1).to_broadcast([128, 8, D])


def rows(t):
    return t.rearrange("p (j f) -> p j f", f=D)


def build(nc, a, out):
    ctx = ExitStack()
    with ctx:
        def sb(name, shape, dt=F32):
            return ctx.enter_context(nc.sbuf_tensor(name, shape, dt))

        def dram(name, shape, dt=F32):
            return nc.dram_tensor(name, shape, dt, kind="Internal").ap()

        class Sems:
            def __init__(self, prefix):
                self.prefix, self.made = prefix, {}

            def __call__(self, name):
                if name not in self.made:
                    self.made[name] = nc.alloc_semaphore(name=self.prefix + name)
                return self.made[name]

            def done(self):
                nc.clear_and_free_semaphores(list(self.made.values()))
                nc.all_engine_barrier()

        rank = dram("rank", [N, 1], I32)
        table = [dram(f"table{k}", [2 * EP, D]) for k in range(4)]
        logit1_d = dram("logit1_d", [EP])
        weight1_d = dram("weight1_d", [PARTS, EP], BF16)
        logit2_d = dram("logit2_d", [3 * HEADS, EP])
        weight2_d = dram("weight2_d", [PARTS * 2 * HEADS, EP], BF16)

        XD = sb("XD", [128, NS * HW])
        XS = sb("XS", [128, NS * HW])
        SAME = sb("SAME", [128, NS * HW], U8)
        MORE = sb("MORE", [128, NS * HW], U8)
        src_i = sb("src_i", [128, 8 * NS], I32)
        dst_i = sb("dst_i", [128, 8 * NS], I32)
        seg_i = sb("seg_i", [128, 8 * NS], I32)
        row_i = sb("row_i", [128, 8 * NS], I32)
        look_i = sb("look_i", [128, 8 * NS], I32)
        t_i = sb("t_i", [128, 8 * NS], I32)
        win = sb("win", [128, 2, 24], I32)
        GA = sb("GA", [128, 2, HW])
        GB = sb("GB", [128, 2, HW])
        rank_t = sb("rank_t", [128, 8 * NS], I32)
        NW = 9
        work = sb("work", [128, 2 * NW * HW])
        W = [[work[:, (par * NW + i) * HW:(par * NW + i + 1) * HW] for i in range(NW)] for par in range(2)]
        wk = W[0]
        XN = sb("XN", [128, 2, HW])
        small = sb("small", [128, 2, 64])
        car = sb("car", [128, 1])
        stat = sb("stat", [128, 8, NS])
        red = sb("red", [128, 32])

        ident = sb("ident", [128, 128])
        ones = sb("ones", [128, 128])
        center = sb("center", [128, 128])
        total = sb("total", [128, 128])
        fold = sb("fold", [128, 128])
        proj = sb("proj", [128, 128])
        wffn = sb("wffn", [128, 128])
        wfc = sb("wfc", [128, 128])
        chain = sb("chain", [128, 128])
        wh = [sb(f"wh{h}", [128, 128]) for h in range(HEADS)]
        w1d = sb("w1d", [128, 128])
        w1s = sb("w1s", [128, 128])
        w2 = sb("w2", [128, 128])
        eprj = sb("eprj", [128, 128])
        one_l = sb("one_l", [128, 6])
        two_l = sb("two_l", [128, 32])
        vec = sb("vec", [128, 16])
        XNS = [XN[:, par, :] for par in range(2)]
        SMALL = [small[:, par, :] for par in range(2)]
        P = [ctx.enter_context(nc.psum_tensor(f"P{i}", [128, HW], F32)) for i in range(8)]
        BN = [[P[4 * par][:, :], P[4 * par + 2][:, :], P[4 * par + 3][:, :]] for par in range(2)]
        bff, relub, bias2, b1, b2, eps_t = (vec[:, i:i + 1] for i in (0, 1, 2, 4, 5, 6))
        spread = sb("spread", [PARTS * 4 * HEADS, (2 * HEADS + 1) * 128], BF16)
        spread_g = lambda g: spread[:, g * 128:(g + 1) * 128]
        spread_all = spread[0:2 * PARTS, 2 * HEADS * 128:(2 * HEADS + 1) * 128]
        weight_rows = [GA[0:PARTS * 4 * HEADS, par, 0:HW // 2].bitcast(BF16) for par in range(2)]
        bias_row = sb("bias_row", [128, D])
        inv_scale, mu_s, mu_d, shift = (vec[:, i:i + 1] for i in range(8, 12))
        grad = sb("grad", [128, 4])
        row_same = sb("row_same", [128, RC])
        row_more = sb("row_more", [128, RC])
        row_neg = sb("row_neg", [128, RC])
        row_last = sb("row_last", [128, RC])
        ends = sb("ends", [128, 2 * HEADS])
        carry = sb("carry", [HEADS, 512])
        carry_in = sb("carry_in", [128, HEADS])

        S = Sems("su_")
        wl = GA[:, :, :].rearrange("p a c -> p (a c)")
        wl2 = GB[:, :, :].rearrange("p a c -> p (a c)")
        Wsb, Att, Wfc_n, Blk, Wed, We2, Wm, Asum = (wl[:, 0:256], wl[:, 256:768], wl[0:64, 768:896], wl[0:64, 900:906],
                                                    wl[0:2, 908:910], wl2[0:2, 0:64], wl2[:, 64:192], wl2[:, 192:320])
        Wmn = work[0:64, 2048:2304].rearrange("p (k c) -> p k c", k=2)
        W1a, IW, CW, we_t, Pr = wl2[:, 320:448], wl2[:, 448:576], wl2[:, 576:704], wl[0:2, 912:913], wl2[:, 704:960]

        sml = small[:, 0, :]
        with nc.Block() as block:
            blocks = [(proj, "proj"), (wffn, "wffnT"), (wfc, "wfcT"), (w1s, "w1b"), (w2, "w2"), (W1a, "w1a")]
            loads = [0]

            @block.sync
            def _(sp):
                def ld(dst, src):
                    sp.dma_start(dst, src).then_inc(S("load"), 16)
                    loads[0] += 16
                sp.wait_ge(S("zero"), 1)
                for h in range(2):
                    lo, hi = h * 64, h * 64 + 64
                    for t, name in blocks:
                        ld(t[lo:hi, lo:hi], a[name])
                    for k in range(HEADS):
                        ld(wh[k][lo:hi, lo:hi], a["w2l"][:, k * D:(k + 1) * D])
                    ld(Wsb[lo:hi, :], a["w2l"])
                    for i, name in enumerate(["b_ffn", "bias2", "b1", "b2"]):
                        ld(vec[lo:hi, (0, 2, 4, 5)[i]:(0, 2, 4, 5)[i] + 1], a[name].rearrange("(p o) -> p o", o=1))
                    ld(Wfc_n[:, h * 64:h * 64 + 64], a["wfc"])
                ld(Att, a["att"].rearrange("(o c) -> o c", o=1).to_broadcast([128, 512]))
                ld(bias_row[:, :], a["bias2"].rearrange("(o c) -> o c", o=1).to_broadcast([128, D]))
                ld(Blk, a["blkT"])
                ld(Wed, a["wedge"])
                ld(We2, a["we2nT"])
                ld(we_t, a["we"])
                for k in range(2):
                    for h in range(2):
                        ld(Wmn[:, k, h * 64:h * 64 + 64], a[f"wm{k + 1}"])
                for k, (t, off) in enumerate([(row_same, 0), (row_neg, 1), (row_more, 2)]):
                    ld(t[:, :].bitcast(I32), a["dst_pad"][off:off + EP].rearrange("(p c) -> p c", p=128))
                for i, t in enumerate([ident, center, total, fold, ones]):
                    ld(t[:, :], a["const"][:, i * 128:(i + 1) * 128])
                ld(work[0:PARTS * 4 * HEADS, 2560:2560 + (2 * HEADS + 1) * 128], a["spread"])
                ld(src_i[:, :], a["src_l"])
                ld(dst_i[:, :], a["dst_l"])
                ld(seg_i[:, :], a["next_l"])
                sp.wait_ge(S("load"), loads[0])
                sp.sem_inc(S("loaded"), 1)
                sp.wait_ge(S("fill"), 2)
                sp.dma_start(rank.rearrange("(p c) o -> p (c o)", p=80), XS[0:80, 0:N // 80].bitcast(I32)).then_inc(S("init"), 16)
                sp.dma_start(table[0][EP:2 * EP, :].rearrange("(p c) f -> p (c f)", p=128), XD[:, :]).then_inc(S("init"), 16)
                sp.wait_ge(S("init"), 32)

            @block.gpsimd
            def _(pool):
                pool.iota(row_i[:, :].rearrange("p (s j) -> p s j", j=8), [[SE, NS], [1, 8]], base=0,
                          channel_multiplier=8).then_inc(S("iota"), 1)
                pool.memset(XS[0:80, 0:N // 80].bitcast(I32), -1).then_inc(S("fill"), 1)
                pool.memset(XD[:, :], 0.0).then_inc(S("fill"), 1)

            @block.vector
            def _(dve):
                step = [0]

                def link(ins):
                    step[0] += 1
                    ins.then_inc(S("dve"), 1)
                    dve.wait_ge(S("dve"), step[0])

                for t in [proj, wffn, wfc, w1s, w2, eprj, *wh]:
                    dve.memset(t[:, :], 0.0)
                for t in [one_l, two_l, car]:
                    dve.memset(t[:, :], 0.0)
                dve.memset(stat[:, :, :], 0.0)
                dve.memset(W1a, 0.0)
                link(dve.memset(eps_t, EPS))
                dve.nop().then_inc(S("zero"), 1)
                dve.wait_ge(S("loaded"), 1)
                dve.wait_ge(S("iota"), 1)
                dve.tensor_copy(spread[:, :], work[0:PARTS * 4 * HEADS, 2560:2560 + (2 * HEADS + 1) * 128])
                link(dve.tensor_tensor(t_i[:, :], dst_i[:, :], seg_i[:, :], A.is_equal))
                link(dve.scalar_tensor_tensor(seg_i[:, :], t_i[:, :], float(FAR), dst_i[:, :], A.mult, A.add))
                link(dve.tensor_scalar(dst_i[:, :], dst_i[:, :], float(N - 1), None, A.min))
                for t in (row_same, row_more):
                    link(dve.tensor_tensor(t[:, :], t[:, :].bitcast(I32), row_neg[:, :].bitcast(I32), A.is_equal))
                link(dve.tensor_scalar(row_neg[:, :], row_same[:, :], -1.0, BIG, A.add, A.mult))
                link(dve.tensor_scalar(row_last[:, :], row_more[:, :], 0.0, None, A.is_equal))
                link(dve.tensor_scalar(relub, bff, 0.0, None, A.max))
                link(dve.tensor_tensor(Asum[:, 0:64], Wsb[:, 0:64], Wsb[:, 64:128], A.add))
                link(dve.tensor_tensor(Asum[:, 64:128], Wsb[:, 128:192], Wsb[:, 192:256], A.add))
                link(dve.memset(Wm, 0.0))
                link(dve.tensor_tensor(Wm[0:64, 0:64], Asum[0:64, 0:64], Asum[0:64, 64:128], A.add))
                link(dve.tensor_tensor(Wm[64:128, 64:128], Asum[64:128, 0:64], Asum[64:128, 64:128], A.add))
                link(dve.scalar_tensor_tensor(IW, Wm, 1.0 / HEADS, ident[:, :], A.mult, A.add))
                for side in range(2):
                    link(dve.tensor_tensor(Pr, Wsb, Att[:, side * 256:(side + 1) * 256], A.mult))
                    link(dve.tensor_reduce(sml[:, side * 4:side * 4 + 4], Pr.rearrange("p (h d) -> p h d", h=HEADS), AX, A.add))
                link(dve.tensor_tensor(sml[:, 8:12], sml[:, 0:4], sml[:, 4:8], A.add))
                for h in range(2):
                    lo, hi = h * 64, h * 64 + 64
                    cols = lambda base: two_l[lo:hi, base + h:base + h + 7:2]
                    link(dve.tensor_copy(cols(0), sml[lo:hi, 0:4]))
                    link(dve.tensor_copy(cols(16), sml[lo:hi, 4:8]))
                    link(dve.tensor_copy(cols(24), sml[lo:hi, 8:12]))
                link(dve.tensor_tensor(w1d[:, :], W1a, w1s[:, :], A.subtract))
                dve.nop().then_inc(S("folded"), 1)
                dve.wait_ge(S("pe"), 1)
                link(dve.tensor_copy(CW, P[0][:, 0:128]))
                for h in range(2):
                    lo, hi = h * 64, h * 64 + 64
                    for c in range(2):
                        link(dve.tensor_copy(one_l[lo:hi, 2 * c + h:2 * c + h + 1], P[1][lo:hi, (0, 3)[c]:(0, 3)[c] + 1]))
                    link(dve.tensor_copy(eprj[lo:lo + 2, lo:hi], P[2][lo:lo + 2, 0:64]))
                    link(dve.tensor_copy(one_l[lo:lo + 2, 4 + h:5 + h], P[2][lo:lo + 2, 64:65]))
                for k in range(2):
                    link(dve.tensor_copy(grad[:, k:k + 3:2], P[3][:, 4 + 2 * k:6 + 2 * k]))
                dve.nop().then_inc(S("cw"), 1)
                dve.wait_ge(S("pe"), 2)
                link(dve.tensor_copy(chain[:, :], P[4][:, 0:128]))
                link(dve.tensor_reduce(red[:, 0:1], bias_row[:, :], AX, A.add))
                link(dve.tensor_scalar(red[:, 1:2], red[:, 0:1], 1.0 / D, None, A.mult))
                link(dve.tensor_scalar(bias_row[:, :], bias_row[:, :], red[:, 1:2], None, A.subtract))

            @block.tensor
            def _(pe):
                pe.wait_ge(S("folded"), 1)
                pe.matmul(P[0][:, 0:128], center[:, :], IW, start=True, stop=True)
                pe.matmul(P[1][:, 0:6], Wfc_n, Blk, start=True, stop=True)
                for h in range(2):
                    pe.matmul(P[2][64 * h:64 * h + 2, 0:64], Wed, We2, start=True, stop=True)
                    pe.matmul(P[2][64 * h:64 * h + 2, 64:65], Wed, we_t, start=True, stop=True)
                for k in range(2):
                    last = pe.matmul(P[3][:, 4 + 2 * k:6 + 2 * k], Wmn[:, k, :], Blk[:, 1 + k:5 + k:3], start=True, stop=True)
                last.then_inc(S("pe"), 1)
                pe.wait_ge(S("cw"), 1)
                pe.transpose(P[5][:, 0:128], CW, ident[:, :]).then_inc(S("pet"), 1)
                pe.wait_ge(S("cwt"), 1)
                pe.matmul(P[4][:, 0:128], wk[0][:, 0:128], center[:, :], start=True, stop=True).then_inc(S("pe"), 1)

            @block.scalar
            def _(act):
                act.wait_ge(S("pet"), 1)
                act.activation(wk[0][:, 0:128], P[5][:, 0:128], ACT.Copy).then_inc(S("cwt"), 1)

        S.done()

        def at(t, s):
            return t[:, bass.ds(s * HW, HW)]

        def rows_of(t, first):
            return t[bass.ds(first, SE), :].rearrange("(p j) f -> p (j f)", p=128)

        def gather_rounds(pool, S, look, table_k):
            def body(s, par, k, n):
                pool.wait_ge(S(f"slot_free{par}"), k)
                pool.tensor_copy(win[:, par, 0:8], look[:, bass.ds(s * 8, 8)]).then_inc(S("window"), 1)
                pool.wait_ge(S("window"), n)
                settle(pool, S("settled"))
                for j in range(8):
                    pool.indirect_dma_start(GA[:, par, j * D:(j + 1) * D], None, table_k,
                                            bass.IndirectOffsetOnAxis(ap=win[:, par, j:j + 1], axis=0)
                                            ).then_inc(S(f"gathered{par}"), 16)
            supers(pool, body)

        def transpose4(pe, dst, src):
            for q in range(4):
                ins = pe.transpose(dst[:, q * 128:(q + 1) * 128], src[:, q * 128:(q + 1) * 128], ident[:, :])
            return ins

        def seg_scan(dve, T, k, V, F, m, op0, op1):
            dve.tensor_tensor_scan(F[0:64, :], m[0:64, :], V[0:64, :], car[0:64, :], op0, op1).then_inc(T("scan0"), 1)
            dve.wait_ge(T("scan0"), k)
            dve.tensor_copy(car[64:128, :], F[0:64, HW - 1:HW]).then_inc(T("mid_carry"), 1)
            dve.wait_ge(T("mid_carry"), k)
            dve.tensor_tensor_scan(F[64:128, :], m[64:128, :], V[64:128, :], car[64:128, :], op0, op1).then_inc(T("scan1"), 1)
            dve.wait_ge(T("scan1"), k)
            dve.tensor_copy(car[0:64, :], F[64:128, HW - 1:HW]).then_inc(T("next_carry"), 1)
            dve.wait_ge(T("next_carry"), k)

        def norm_pe(pe, T, s, par, k):
            yield 0
            pe.wait_ge(T("u"), k)
            for q in range(4):
                ins = pe.matmul(P[4 * par + 2][:, q * 128:(q + 1) * 128], W[par][4][:, q * 128:(q + 1) * 128], center[:, :],
                                start=True, stop=True)
            ins.then_inc(T("centred"), 1)

        def back_pe(pe, T, s, par, k):
            yield 0
            pe.wait_ge(T("emb"), k)
            pe.wait_ge(T("kept"), k)
            transpose4(pe, P[4 * par + 3], W[par][6]).then_inc(T("x_fm"), 1)

        def keeping(dve, S):
            for par in range(2):
                dve.sem_inc(S(f"kept{par}"), 1)

        def norm_act(act, T, s, par, k):
            yield 1
            act.wait_ge(T("centred"), k)
            act.activation(W[par][5], P[4 * par + 2][:, :], ACT.Square).then_inc(T("square"), 1)
            yield 3
            act.wait_ge(T("variance"), k)
            act.activation(small[:, par, 8:16], small[:, par, 0:8], ACT.Sqrt, scale=1.0 / D, bias=eps_t).then_inc(T("deviation"), 1)

        def norm_dve(dve, T, s, par, k, free="stored", count=None):
            yield 2
            dve.wait_ge(T("square"), k)
            dve.tensor_reduce(small[:, par, 0:8], rows(W[par][5]), AX, A.add).then_inc(T("variance"), 1)
            yield 4
            dve.wait_ge(T("deviation"), k)
            dve.reciprocal(small[:, par, 16:24], small[:, par, 8:16]).then_inc(T("rstd"), 1)
            dve.wait_ge(T("rstd"), k)
            count = 16 * k if count is None else count
            if not isinstance(count, int) or count > 0:
                dve.wait_ge(T(free), count)
            dve.tensor_tensor(rows(W[par][6]), rows(P[4 * par + 2][:, :]), per_row(small[:, par, 16:24]), A.mult).then_inc(T("emb"), 1)

        def back_dve(dve, T, s, par, k):
            yield 1
            dve.wait_ge(T("x_fm"), k)
            dve.scalar_tensor_tensor(at(XD, s), at(MORE, s), 0.0, P[4 * par + 3][:, ::-1], A.is_equal, A.mult).then_inc(T("kept"), 1)

        def store_table(sp, T, table_k, s, par, k, step=0):
            yield step
            sp.wait_ge(T("emb"), k)
            sp.dma_start(rows_of(table_k, s * SE), W[par][6]).then_inc(T("stored"), 16)

        def storing(sp, S):
            for par in range(2):
                sp.sem_inc(S(f"stored{par}"), 16)

        def all_stored(sp, S):
            sp.wait_ge(S("stored0"), 16 * (NS // 2 + 2))
            sp.wait_ge(S("stored1"), 16 * (NS // 2 + 1))

        BACK = [W[0][5], W[1][5]]

        def pass_back(dve, S, run=None):
            dve.memset(car[:, :], 0.0).then_inc(S("car0"), 1)
            dve.wait_ge(S("car0"), 1)
            for par in range(2):
                dve.sem_inc(S(f"back_free{par}"), 1)

            def body(s, par, k, n):
                dve.wait_ge(S(f"back_free{par}"), k)
                settle(dve, S("settled"))
                B = BACK[par]
                for h in (1, 0):
                    lo, hi = 64 * h, 64 * h + 64
                    other = slice(64 - lo, 128 - lo)
                    x, more = (at(t, (NS - 1) - s)[lo:hi, :] for t in (XD, MORE))
                    dve.tensor_tensor_scan(B[lo:hi, ::-1], more, x, car[lo:hi, :], A.mult, A.add).then_inc(S(f"back{h}"), 1)
                    dve.wait_ge(S(f"back{h}"), n)
                    dve.tensor_copy(car[other, :], B[lo:hi, 0:1]).then_inc(S(f"back_carry{h}"), 1)
                    dve.wait_ge(S(f"back_carry{h}"), n)
            if run is None:
                supers(dve, body)
            else:
                def stage(T, s, par, k):
                    yield 0
                    body(s, par, k, 2 * k - 1 + par)
                run(stage)
            dve.wait_ge(S("back_free0"), NS // 2 + 2)
            dve.wait_ge(S("back_free1"), NS // 2 + 1)

        def keep_back(act, S, s, par, n):
            act.wait_ge(S("back_carry0"), n)
            act.activation(at(XD, (NS - 1) - s), BACK[par], ACT.Copy).then_inc(S(f"back_free{par}"), 1)

        def zero_carry(dve, S, value=0.0):
            dve.memset(car[:, :], value).then_inc(S("carry_start"), 1)
            dve.wait_ge(S("carry_start"), 1)

        def dense_pe1(pe, T, par, c, b):
            VT = W[par][0]
            yield b + 2
            pe.wait_ge(T("vt"), c)
            for w, p in ((center, BN[par][1]), (chain, BN[par][2])):
                for q in range(4):
                    ins = pe.matmul(p[:, q * 128:(q + 1) * 128], VT[:, q * 128:(q + 1) * 128], w[:, :], start=True, stop=True)
                ins.then_inc(T("dense_mm"), 1)

        def dense_pe3(pe, T, par, c, b):
            yield b + 9
            pe.wait_ge(T("y"), c)

        def dense_pe(pe, T, par, c, b):
            yield from dense_pe1(pe, T, par, c, b)
            yield from dense_pe3(pe, T, par, c, b)

        def sm(par, k):
            return SMALL[par][:, k * 8:k * 8 + 8]

        def root(act, T, par, dst, src, name):
            act.activation(sm(par, dst), sm(par, src), ACT.Sqrt, scale=1.0 / D, bias=eps_t).then_inc(T(name), 1)

        def dense_act1(act, T, par, c, b):
            yield b + 3
            act.wait_ge(T("dense_mm"), 2 * c)
            act.activation(W[par][1], BN[par][1], ACT.Square).then_inc(T("sq1"), 1)

        def dense_act2(act, T, par, c, b):
            yield b + 5
            act.wait_ge(T("ss1"), c)
            root(act, T, par, 1, 0, "sd1")
            yield b + 7
            act.wait_ge(T("ss2"), c)
            root(act, T, par, 3, 2, "sd2")

        def dense_act3(act, T, par, c, b, m=None, squares=1):
            yield b + 9
            act.wait_ge(T("y"), c)
            act.activation(W[par][squares], W[par][2], ACT.Square).then_inc(T("sq2"), 1)
            yield b + 11
            act.wait_ge(T("ss3"), c)
            root(act, T, par, 5, 4, "sd3")
            if m is not None:
                yield b + 13
                act.wait_ge(T("ss4"), m)
                root(act, T, par, 7, 6, "sd4")

        def dense_act(act, T, par, c, b, m=None):
            yield from dense_act1(act, T, par, c, b)
            yield from dense_act2(act, T, par, c, b)
            yield from dense_act3(act, T, par, c, b, m)

        def twice(dve, T, par, ss, c, names, n):
            dve.reciprocal(sm(par, ss + 1), sm(par, ss + 1)).then_inc(T(names[0]), 1)
            dve.wait_ge(T(names[0]), c)
            dve.tensor_tensor(sm(par, ss + 2), sm(par, ss), sm(par, ss + 1), A.mult).then_inc(T(names[1]), 1)
            dve.wait_ge(T(names[1]), n)
            dve.tensor_tensor(sm(par, ss + 2), sm(par, ss + 2), sm(par, ss + 1), A.mult).then_inc(T(names[2]), 1)

        def dense_dve2(dve, T, par, c, b, free=None):
            Y = W[par][2]
            yield b + 4
            dve.wait_ge(T("sq1"), c)
            dve.tensor_reduce(sm(par, 0), rows(W[par][1]), AX, A.add).then_inc(T("ss1"), 1)
            yield b + 6
            dve.wait_ge(T("sd1"), c)
            twice(dve, T, par, 0, c, ("r1", "t2", "ss2"), c)
            yield b + 8
            dve.wait_ge(T("sd2"), c)
            dve.reciprocal(sm(par, 3), sm(par, 3)).then_inc(T("r2"), 1)
            dve.wait_ge(T("r2"), c)
            dve.tensor_tensor(sm(par, 3), sm(par, 3), sm(par, 1), A.mult).then_inc(T("r12"), 1)
            dve.wait_ge(T("r12"), c)
            if free is not None:
                dve.wait_ge(T("out_stored"), free)
                dve.tensor_tensor(rows(W[par][3]), rows(BN[par][1]), per_row(sm(par, 1)), A.mult)
                dve.tensor_tensor(rows(W[par][4]), rows(BN[par][1]), per_row(sm(par, 3)), A.mult).then_inc(T("o12"), 1)
            dve.tensor_tensor(rows(Y), rows(BN[par][2]), per_row(sm(par, 3)), A.mult).then_inc(T("y0"), 1)
            dve.wait_ge(T("y0"), c)
            dve.tensor_tensor(rows(Y), rows(Y), bias_row[:, :].rearrange("p (o f) -> p o f", o=1).to_broadcast([128, 8, D]),
                              A.add).then_inc(T("y"), 1)

        def dense_dve3(dve, T, par, c, b, free=None, m=None, squares=1):
            Y = W[par][2]
            yield b + 10
            dve.wait_ge(T("sq2"), c)
            dve.tensor_reduce(sm(par, 4), rows(W[par][squares]), AX, A.add).then_inc(T("ss3"), 1)
            yield b + 12
            dve.wait_ge(T("sd3"), c)
            if m is None:
                dve.reciprocal(sm(par, 5), sm(par, 5)).then_inc(T("r3"), 1)
                dve.wait_ge(T("r3"), c)
                dve.tensor_tensor(rows(W[par][5]), rows(Y), per_row(sm(par, 5)), A.mult).then_inc(T("out_ready"), 1)
            else:
                twice(dve, T, par, 4, c, ("r3", "t4", "ss4"), m)
                yield b + 14
                dve.wait_ge(T("sd4"), m)
                dve.reciprocal(sm(par, 7), sm(par, 7)).then_inc(T("r4"), 1)
                dve.wait_ge(T("r4"), m)
                dve.tensor_tensor(sm(par, 7), sm(par, 7), sm(par, 5), A.mult).then_inc(T("r34"), 1)
                dve.wait_ge(T("r34"), m)
                dve.wait_ge(T("out_stored"), free)
                dve.tensor_tensor(rows(W[par][3]), rows(Y), per_row(sm(par, 7)), A.mult).then_inc(T("out_ready"), 1)

        def dense_dve(dve, T, par, c, b, free, m=None):
            yield from dense_dve2(dve, T, par, c, b, free if m is None else None)
            yield from dense_dve3(dve, T, par, c, b, free, m)

        def node_pe1(pe, T, par, c, m, b):
            yield b
            pe.wait_ge(T("xn"), m * 16)
            transpose4(pe, BN[par][0], XNS[par]).then_inc(T("xt"), 1)
            pe.wait_ge(T("xt"), m)
            pe.sem_inc(T("xn_free"), 1)
            yield from dense_pe1(pe, T, par, c, b)

        def node_pe(pe, T, par, c, m, b):
            yield from node_pe1(pe, T, par, c, m, b)
            yield from dense_pe3(pe, T, par, c, b)

        def node_act1(act, T, par, c, m, b):
            yield b + 1
            act.wait_ge(T("xt"), m)
            act.activation(W[par][0], BN[par][0], ACT.Identity, bias=relub).then_inc(T("vt"), 1)
            yield from dense_act1(act, T, par, c, b)

        def node_act(act, T, par, c, m, b):
            yield from node_act1(act, T, par, c, m, b)
            yield from dense_act2(act, T, par, c, b)
            yield from dense_act3(act, T, par, c, b, m)

        def node_load(sp, T, par, m, b, first):
            yield b
            sp.wait_ge(T("xn_free"), m)
            sp.dma_start(XNS[par], rows_of(a["x"], first)).then_inc(T("xn"), 16)

        def node_store(sp, T, par, c, b, first):
            yield b + 15
            sp.wait_ge(T("out_ready"), c)
            sp.dma_start(rows_of(out, first), W[par][3]).then_inc(T("out_stored"), 16)

        NA_ = NG + 1 - 2 * NS

        def is_last(s, base):
            return isinstance(s, int) and base + s == NG

        def first_of(s, base):
            return N - SE if is_last(s, base) else (s + base) * SE

        def nodes_sync(sp, S, base, own=None):
            def load(T, s, par, k):
                yield from node_load(sp, T, par, k, 0, first_of(s, base))

            def store(T, s, par, k):
                if is_last(s, base):
                    yield 6
                    sp.wait_ge(S(f"out_stored{1 - par}"), 16 * (NS // 2 + 1))
                yield from node_store(sp, T, par, k, -9, first_of(s, base))
            for par in range(2):
                sp.sem_inc(S(f"out_stored{par}"), 16)
            pipelined(sp, S, together(load, own) if own else load, None, None, store)
            for par in range(2):
                sp.wait_ge(S(f"out_stored{par}"), 16 * (NS // 2 + 2 - par))

        def nodes_tensor(pe, S, own=None):
            for par in range(2):
                pe.sem_inc(S(f"xn_free{par}"), 1)
            node = lambda T, s, par, k: node_pe1(pe, T, par, k, k, 0)
            pipelined(pe, S, None, together(node, own) if own else node, None, lambda T, s, par, k: dense_pe3(pe, T, par, k, -9))

        def nodes_scalar(act, S, own=None):
            node = lambda T, s, par, k: node_act1(act, T, par, k, k, 0)
            pipelined(act, S, None, together(node, own) if own else node,
                      lambda T, s, par, k: dense_act2(act, T, par, k, -4),
                      lambda T, s, par, k: dense_act3(act, T, par, k, -9, k, 4))

        def nodes_vector(dve, S, own=None):
            pipelined(dve, S, None, own, lambda T, s, par, k: dense_dve2(dve, T, par, k, -4),
                      lambda T, s, par, k: dense_dve3(dve, T, par, k, -9, 16 * k, k, 4))

        def softmax_rows(block, S, logits, weights, K, slope, own):
            view = lambda i: work[:, i * 1024:i * 1024 + K * RC].rearrange("p (h c) -> p h c", h=K)
            L, T, R, X = (view(i) for i in range(4))
            LO, XO = (g[:, :, :].rearrange("p a c -> p (a c)")[:, 0:K * RC].rearrange("p (h c) -> p h c", h=K) for g in (GA, GB))
            half = [work[:, 4096 + i * 512:4096 + i * 512 + K * RC // 2].bitcast(BF16) for i in range(PARTS * (1 + own))]
            rest = work[:, 4096 + 6 * 512:4096 + 6 * 512 + K * RC]
            all_ = lambda m: m[:, :].rearrange("p (o c) -> p o c", o=1).to_broadcast([128, K, RC])

            @block.sync
            def _(sp):
                for t, lo in ((L, 0), (T, K), (LO, 2 * K)) if own else ((L, 0),):
                    for h in range(K):
                        src = logits[lo + h, :] if own else logits
                        sp.dma_start(t[:, h, :], src.rearrange("(p c) -> p c", p=128)).then_inc(S("load"), 16)
                sp.wait_ge(S("weights"), 1)
                for side in range(1 + own):
                    for part in range(PARTS):
                        for h in range(K):
                            row = (part * (1 + own) + side) * K + h
                            sp.dma_start(weights[row, :].rearrange("(p c) -> p c", p=128),
                                         half[side * PARTS + part][:, h * RC:(h + 1) * RC]).then_inc(S("store"), 16)
                sp.wait_ge(S("store"), 16 * K * PARTS * (1 + own))

            rounds = [0]

            @block.vector
            def _(dve):
                step = [0]

                def link(ins):
                    step[0] += 1
                    ins.then_inc(S("dve"), 1)
                    dve.wait_ge(S("dve"), step[0])

                def scan(src, dst, mask, op0, op1, start, down=False):
                    rounds[0] += 1
                    r = rounds[0]
                    d = (lambda x: x[:, ::-1]) if down else (lambda x: x)
                    for h in range(K):
                        link(dve.tensor_tensor_scan(d(dst[:, h, :]), d(mask[:, :]), d(src[:, h, :]), start, op0, op1))
                    edge = 0 if down else RC - 1
                    link(dve.tensor_copy(ends[:, 0:K], dst[:, :, edge]))
                    link(dve.tensor_reduce(red[:, 0:1], mask[:, :], AX, A.min))
                    link(dve.tensor_copy(ends[:, HEADS:HEADS + K], red[:, 0:1].to_broadcast([128, K])))
                    dve.nop().then_inc(S("ends"), 1)
                    dve.wait_ge(S("ends_row"), r)
                    link(dve.tensor_copy(carry[0:K, 0:256], P[0][0:K, 0:256]))
                    link(dve.memset(carry[0:K, 256:385], start))
                    into = carry[0:K, 256:384] if down else carry[0:K, 257:385]
                    link(dve.tensor_tensor_scan(d(into), d(carry[0:K, 128:256]), d(carry[0:K, 0:128]), start, op0, op1))
                    dve.nop().then_inc(S("carry"), 1)
                    dve.wait_ge(S("carry_in"), r)
                    link(dve.tensor_copy(carry_in[:, 0:K], P[1][:, 0:K]))
                    for h in range(K):
                        link(dve.tensor_tensor_scan(d(dst[:, h, :]), d(mask[:, :]), d(src[:, h, :]), carry_in[:, h:h + 1], op0, op1))

                def spread(t, dst):
                    link(dve.tensor_tensor(t, t, all_(row_last), A.mult))
                    scan(t, dst, row_more, A.mult, A.add, 0.0, down=True)

                dve.wait_ge(S("load"), 16 * K * (1 + 2 * own))
                if own:
                    link(dve.tensor_tensor(L, L, T, A.add))
                else:
                    link(dve.tensor_scalar(L, L, shift, None, A.add))
                link(dve.scalar_tensor_tensor(L, L, slope, L, A.mult, A.max))
                scan(L, T, row_neg, A.add, A.max, -BIG)
                spread(T, R)
                if own:
                    link(dve.scalar_tensor_tensor(LO, LO, slope, LO, A.mult, A.max))
                    link(dve.tensor_tensor(R, R, LO, A.max))
                    link(dve.tensor_tensor(LO, LO, R, A.subtract))
                link(dve.tensor_tensor(L, L, R, A.subtract))
                dve.nop().then_inc(S("shifted"), 1)
                dve.wait_ge(S("exp"), 1 + own)
                scan(X, T, row_same, A.mult, A.add, 0.0)
                spread(T, R)
                if own:
                    link(dve.tensor_tensor(R, R, XO, A.add))
                    link(dve.tensor_scalar(R, R, 1e-16, float(HEADS), A.add, A.mult))
                link(dve.reciprocal(R, R))
                link(dve.tensor_tensor(X, X, R, A.mult))
                if own:
                    link(dve.tensor_tensor(XO, XO, R, A.mult))
                for side, w in enumerate((X, XO)[:1 + own]):
                    flat = w.rearrange("p h c -> p (h c)")
                    for part in range(PARTS):
                        link(dve.tensor_copy(half[side * PARTS + part], flat if part == 0 else rest))
                        if part < PARTS - 1:
                            link(dve.tensor_tensor(rest, flat if part == 0 else rest, half[side * PARTS + part], A.subtract))
                dve.nop().then_inc(S("weights"), 1)

            @block.scalar
            def _(act):
                act.wait_ge(S("shifted"), 1)
                act.activation(X, L, ACT.Exp).then_inc(S("exp"), 1)
                if own:
                    act.activation(XO, LO, ACT.Exp).then_inc(S("exp"), 1)

            @block.tensor
            def _(pe):
                for r, down in enumerate((False, True, False, True)):
                    pe.wait_ge(S("ends"), r + 1)
                    pe.transpose(P[0][0:K, 0:128], ends[:, 0:K], ident[:, :])
                    pe.transpose(P[0][0:K, 128:256], ends[:, HEADS:HEADS + K], ident[:, :]).then_inc(S("ends_row"), 1)
                    pe.wait_ge(S("carry"), r + 1)
                    src = carry[0:K, 257:385] if down else carry[0:K, 256:384]
                    pe.transpose(P[1][:, 0:K], src, ident[0:K, 0:K]).then_inc(S("carry_in"), 1)


        SM = Sems("m_")
        with nc.Block() as block:
            cols = [work[:, (par * NW + 7) * HW:(par * NW + 8) * HW + 2].bitcast(I32) for par in range(2)]

            @block.gpsimd
            def _(pool):
                def scatter(s, par, k, n, wait=True):
                    if wait:
                        pool.wait_ge(SM(f"scattered{par}"), 128 * (k - 1))
                    pool.tensor_copy(win[:, par, 0:8], seg_i[:, bass.ds(s * 8, 8)]).then_inc(SM("window"), 1)
                    pool.tensor_copy(win[:, par, 8:16], row_i[:, bass.ds(s * 8, 8)]).then_inc(SM("window"), 1)
                    pool.wait_ge(SM("window"), n * 2)
                    settle(pool, SM("settled"))
                    for j in range(8):
                        pool.indirect_dma_start(rank, bass.IndirectOffsetOnAxis(ap=win[:, par, j:j + 1], axis=0),
                                                win[:, par, 8 + j:9 + j], None, bounds_check=N - 1, oob_is_err=False
                                                ).then_inc(SM(f"scattered{par}"), 16)

                for par in range(2):
                    scatter(par, par, 1, par + 1, wait=False)
                with pool.Fori(0, NS // 2 - 1) as i:
                    for par in range(2):
                        scatter(2 * i + 2 + par, par, i + 2, 2 * i + 3 + par)
                scatter(NS - 1, 0, NS // 2 + 1, NS)
                pool.wait_ge(SM("scattered0"), 128 * (NS // 2 + 1))
                pool.wait_ge(SM("scattered1"), 128 * (NS // 2))

            @block.sync
            def _(sp):
                def mask_load(T, s, par, k):
                    yield 0
                    sp.wait_ge(T("cols_free"), k)
                    for h in range(2):
                        sp.dma_start(cols[par][64 * h:64 * h + 64, :],
                                     a["dst_pad"][bass.ds(s * SE + h * HW, HW + 2)].rearrange("(o c) -> o c", o=1)
                                     .to_broadcast([64, HW + 2])).then_inc(T("cols"), 16)
                nodes_sync(sp, SM, NA_, mask_load)

            @block.tensor
            def _(pe):
                nodes_tensor(pe, SM)

            @block.scalar
            def _(act):
                nodes_scalar(act, SM)

            @block.vector
            def _(dve):
                for par in range(2):
                    dve.sem_inc(SM(f"cols_free{par}"), 1)

                def mask(T, s, par, k):
                    yield 0
                    dve.wait_ge(T("cols"), k * 32)
                    dve.tensor_tensor(at(SAME, s), cols[par][:, 1:HW + 1], cols[par][:, 0:HW], A.is_equal)
                    dve.tensor_tensor(at(MORE, s), cols[par][:, HW:0:-1], cols[par][:, HW + 1:1:-1], A.is_equal).then_inc(T("mask"), 1)
                    yield 5
                    dve.wait_ge(T("mask"), k)
                    dve.sem_inc(T("cols_free"), 1)
                nodes_vector(dve, SM, mask)
        SM.done()

        SA = Sems("a_")
        with nc.Block() as block:
            @block.gpsimd
            def _(pool):
                def body(s, par, k, n):
                    pool.wait_ge(SA(f"slot_free{par}"), k)
                    pool.wait_ge(SA(f"rank_kept{par}"), k)
                    pool.tensor_copy(win[:, par, 0:8], src_i[:, bass.ds(s * 8, 8)]).then_inc(SA("window"), 1)
                    pool.tensor_copy(win[:, par, 8:16], dst_i[:, bass.ds(s * 8, 8)]).then_inc(SA("window"), 1)
                    pool.wait_ge(SA("window"), n * 2)
                    settle(pool, SA("settled"))
                    for b, (buf, t) in enumerate(((GA, a["x"]), (GB, a["x"]), (None, rank))):
                        for j in range(8):
                            col = (b % 2) * 8 + j
                            dst = buf[:, par, j * D:(j + 1) * D] if buf is not None else win[:, par, 16 + j:17 + j]
                            pool.indirect_dma_start(dst, None, t, bass.IndirectOffsetOnAxis(ap=win[:, par, col:col + 1], axis=0)
                                                    ).then_inc(SA(f"gathered{par}"), 16)
                supers(pool, body)

            def streams(eng, edge, node):
                def body(s, par, k, tail=False):
                    T = of(SA, par)
                    per = 3
                    yield edge(T, s, par, k, per * (k - 1) + 1)
                    for j in range(0 if tail else 2):
                        yield node(T, par, k, j, per * (k - 1) + 2 + j, 2 * (k - 1) + j + 1, 16 + 16 * j, (2 * s + j) * SE)
                with eng.Fori(0, NS // 2) as i:
                    side_by_side(*(g for par in range(2) for g in body(2 * i + par, par, i + 1)))
                side_by_side(*body(NS - 1, 0, NS // 2 + 1, True))

            @block.tensor
            def _(pe):
                for par in range(2):
                    pe.sem_inc(SA(f"slot_free{par}"), 1)
                    pe.sem_inc(SA(f"xn_free{par}"), 1)

                def edge(T, s, par, k, c):
                    yield 0
                    pe.wait_ge(T("gathered"), k * 384)
                    transpose4(pe, P[4 * par], GA[:, par, :])
                    transpose4(pe, P[4 * par + 1], GB[:, par, :]).then_inc(T("ends_fm"), 1)
                    dense = dense_pe(pe, T, par, c, 0)
                    yield next(dense)
                    next(dense)
                    pe.wait_ge(T("ends_fm"), k)
                    pe.sem_inc(T("slot_free"), 1)
                    yield 3
                    pe.wait_ge(T("scan1"), k)
                    pe.wait_ge(T("sum_d"), k)
                    transpose4(pe, P[4 * par + 1], W[par][7]).then_inc(T("x_em"), 1)
                    yield 9
                    pe.wait_ge(T("emb"), k)
                    for _ in dense:
                        pass
                streams(pe, edge, lambda T, par, k, j, c, m, b, first: node_pe(pe, T, par, c, m, b))

            @block.scalar
            def _(act):
                def edge(T, s, par, k, c):
                    bank = P[4 * par][:, :], P[4 * par + 1][:, :]
                    hi, n_cols = (64, LASTC) if isinstance(s, int) else (128, HW)
                    yield 1
                    act.wait_ge(T("ends_fm"), k)
                    act.activation(at(XS, s), bank[0], ACT.Copy)
                    act.activation(at(XD, s), bank[1], ACT.Copy).then_inc(T("ends"), 1)
                    act.activation(W[par][0], bank[0], ACT.Identity, bias=relub).then_inc(T("vt"), 1)
                    act.activation(W[par][1][0:hi, 0:n_cols], bank[0][0:hi, 0:n_cols], ACT.Square,
                                   accum_out=stat[0:hi, 0, bass.ds(s, 1)]).then_inc(T("sum_s"), 1)
                    act.wait_ge(T("sum_s"), k)
                    act.activation(W[par][1][0:hi, 0:n_cols], bank[1][0:hi, 0:n_cols], ACT.Square,
                                   accum_out=stat[0:hi, 1, bass.ds(s, 1)]).then_inc(T("sum_d"), 1)
                    dense = dense_act(act, T, par, c, 0)
                    act.wait_ge(T("sum_d"), k)
                    step = next(dense)
                    yield step
                    step = next(dense)
                    yield 4
                    act.wait_ge(T("x_em"), k)
                    act.wait_ge(T("stored"), 16 * k)
                    act.activation(W[par][6], bank[1], ACT.Copy).then_inc(T("emb"), 1)
                    yield step
                    yield from dense
                streams(act, edge, lambda T, par, k, j, c, m, b, first: node_act(act, T, par, c, m, b))

            @block.vector
            def _(dve):
                for par in range(2):
                    dve.sem_inc(SA(f"rank_kept{par}"), 1)
                zero_carry(dve, SA)

                def edge(T, s, par, k, c):
                    V, F = W[par][8], W[par][7]
                    yield 2
                    dve.wait_ge(T("ends"), k)
                    dve.tensor_tensor(V, at(XS, s), at(XD, s), A.subtract).then_inc(T("v"), 1)
                    dve.tensor_copy(rank_t[:, bass.ds(s * 8, 8)], win[:, par, 16:24]).then_inc(T("rank_copied"), 1)
                    dve.wait_ge(T("v"), k)
                    seg_scan(dve, T, k, V, F, at(SAME, s), A.mult, A.add)
                    dve.wait_ge(T("rank_copied"), k)
                    dve.sem_inc(T("rank_kept"), 1)
                    yield from dense_dve(dve, T, par, c, 0, 80 * k)
                streams(dve, edge, lambda T, par, k, j, c, m, b, first: dense_dve(dve, T, par, c, b, 80 * k + 48 + 16 * j, m))

            @block.sync
            def _(sp):
                for par in range(2):
                    sp.sem_inc(SA(f"out_stored{par}"), 80)
                storing(sp, SA)

                def edge(T, s, par, k, c):
                    yield from store_table(sp, T, table[0], s, par, k, 5)
                    yield 13
                    sp.wait_ge(T("out_ready"), c)
                    for i in range(3):
                        sp.dma_start(rows_of(table[i + 1], s * SE + EP), W[par][3 + i]).then_inc(T("out_stored"), 16)

                def node(T, par, k, j, c, m, b, first):
                    yield from node_load(sp, T, par, m, b - 10, first)
                    yield from node_store(sp, T, par, c, b, first)
                streams(sp, edge, node)
                all_stored(sp, SA)
                sp.wait_ge(SA("out_stored0"), 80 * (NS // 2 + 1) + 48)
                sp.wait_ge(SA("out_stored1"), 80 * (NS // 2 + 1))
        SA.done()

        SB = Sems("b_")
        with nc.Block() as block:
            @block.vector
            def _(dve):
                step = [0]

                def link(ins):
                    step[0] += 1
                    ins.then_inc(SB("dve"), 1)
                    dve.wait_ge(SB("dve"), step[0])

                link(dve.tensor_scalar(t_i[:, :], row_i[:, :], float(EP + 1), None, A.add))
                link(dve.scalar_tensor_tensor(look_i[:, :], rank_t[:, :], 0.0, t_i[:, :], A.is_lt, A.mult))
                link(dve.tensor_tensor(t_i[:, :], look_i[:, :], rank_t[:, :], A.add))
                link(dve.tensor_copy(look_i[:, :], t_i[:, :]))
                link(dve.tensor_reduce(red[:, 0:2], stat[:, 0:2, :], AX, A.add))
                dve.nop().then_inc(SB("sums"), 1)
                dve.wait_ge(SB("norms"), 1)
                link(dve.tensor_tensor(red[:, 4:5], red[:, 2:3], red[:, 3:4], A.mult))
                link(dve.tensor_scalar(red[:, 5:6], red[:, 4:5], 1e-6, None, A.add))
                link(dve.reciprocal(inv_scale, red[:, 5:6]))
                link(dve.memset(car[:, :], 0.0))

            @block.tensor
            def _(pe):
                pe.wait_ge(SB("sums"), 1)
                pe.matmul(P[0][:, 0:2], ones[:, :], red[:, 0:2], start=True, stop=True).then_inc(SB("all"), 1)

            @block.scalar
            def _(act):
                act.wait_ge(SB("all"), 1)
                act.activation(red[:, 2:4], P[0][:, 0:2], ACT.Sqrt).then_inc(SB("norms"), 1)

        SB.done()

        S0 = Sems("c_")
        with nc.Block() as block:
            @block.gpsimd
            def _(pool):
                gather_rounds(pool, S0, look_i, table[0])

            @block.vector
            def _(dve):
                def gate(T, s, par, k):
                    yield 0
                    dve.tensor_tensor(W[par][0], at(XS, s), at(XD, s), A.mult).then_inc(T("product"), 1)
                    yield 4
                    dve.wait_ge(T("logit"), k)
                    dve.tensor_scalar(W[par][2], P[4 * par + 1][:, :], -5.0, 5.0, A.max, A.min).then_inc(T("clipped"), 1)

                def sums(T, s, par, k):
                    V, F = W[par][8], W[par][7]
                    yield 1
                    dve.wait_ge(T("gate"), k)
                    dve.wait_ge(T("sums_fm"), k)
                    dve.tensor_tensor(V, P[4 * par][:, :], W[par][2], A.mult).then_inc(T("v"), 1)
                    dve.wait_ge(T("v"), k)
                    seg_scan(dve, T, k, V, F, at(SAME, s), A.mult, A.add)
                    yield 4
                    dve.wait_ge(T("ffn"), k)
                    dve.tensor_tensor(W[par][4], at(XD, s), W[par][3], A.add).then_inc(T("u"), 1)
                keeping(dve, S0)
                pipelined(dve, S0, gate, sums, partial(norm_dve, dve), partial(back_dve, dve))

            @block.tensor
            def _(pe):
                for par in range(2):
                    pe.sem_inc(S0(f"slot_free{par}"), 1)

                def gate(T, s, par, k):
                    bank = P[4 * par + 1][:, :]
                    yield 1
                    pe.wait_ge(T("product"), k)
                    pe.matmul(bank, proj[:, :], W[par][0], start=True, stop=True).then_inc(T("cos"), 1)
                    yield 3
                    pe.wait_ge(T("relu"), k)
                    pe.matmul(bank, total[:, :], W[par][1], start=True, stop=True).then_inc(T("logit"), 1)

                def sums(T, s, par, k):
                    bank = P[4 * par][:, :]
                    yield 0
                    pe.wait_ge(T("gathered"), k * 128)
                    transpose4(pe, bank, GA[:, par, :]).then_inc(T("sums_fm"), 1)
                    pe.wait_ge(T("sums_fm"), k)
                    pe.sem_inc(T("slot_free"), 1)
                    yield 2
                    pe.wait_ge(T("scan1"), k)
                    pe.matmul(bank, wffn[:, :], W[par][7], start=True, stop=True).then_inc(T("ffn_mm"), 1)
                pipelined(pe, S0, gate, sums, partial(norm_pe, pe), partial(back_pe, pe))

            @block.scalar
            def _(act):
                def gate(T, s, par, k):
                    yield 2
                    act.wait_ge(T("cos"), k)
                    act.activation(W[par][1], P[4 * par + 1][:, :], ACT.Relu, scale=inv_scale).then_inc(T("relu"), 1)
                    yield 5
                    act.wait_ge(T("clipped"), k)
                    act.activation(W[par][2], W[par][2], ACT.Exp).then_inc(T("gate"), 1)

                def sums(T, s, par, k):
                    yield 3
                    act.wait_ge(T("ffn_mm"), k)
                    act.activation(W[par][3], P[4 * par][:, :], ACT.Relu, bias=bff).then_inc(T("ffn"), 1)
                pipelined(act, S0, gate, sums, partial(norm_act, act))

            @block.sync
            def _(sp):
                storing(sp, S0)
                pipelined(sp, S0, None, None, lambda T, s, par, k: store_table(sp, T, table[1], s, par, k, 6))
                all_stored(sp, S0)
        S0.done()

        S1 = Sems("d_")
        with nc.Block() as block:
            @block.gpsimd
            def _(pool):
                gather_rounds(pool, S1, look_i, table[1])

            @block.vector
            def _(dve):
                pass_back(dve, S1, lambda stage: nodes_vector(dve, S1, stage))

            @block.tensor
            def _(pe):
                for par in range(2):
                    pe.sem_inc(S1(f"slot_free{par}"), 1)
                    pe.sem_inc(S1(f"fm_kept{par}"), 1)

                def states(T, s, par, k):
                    yield 3
                    pe.wait_ge(T("gathered"), k * 128)
                    pe.wait_ge(T("fm_kept"), k)
                    transpose4(pe, P[4 * par + 1], GA[:, par, :]).then_inc(T("fm"), 1)
                    pe.wait_ge(T("fm"), k)
                    pe.sem_inc(T("slot_free"), 1)
                nodes_tensor(pe, S1, states)

            @block.scalar
            def _(act):
                def states(T, s, par, k):
                    yield 2
                    r_ = (NS - 1) - s
                    act.wait_ge(S1("back_carry0"), 2 * k - 1 + par)
                    hi, c = (64, LASTC) if isinstance(s, int) and s == 0 else (128, HW)
                    act.activation(W[par][8][0:hi, 0:c], BACK[par][0:hi, 0:c], ACT.Copy, accum_out=stat[0:hi, 3, bass.ds(r_, 1)])
                    act.activation(at(XD, r_), BACK[par], ACT.Copy).then_inc(T("back_free"), 1)
                    yield 5
                    act.wait_ge(T("fm"), k)
                    hi, c = (64, LASTC) if isinstance(s, int) and s == NS - 1 else (128, HW)
                    bank = P[4 * par + 1]
                    act.activation(W[par][7][0:hi, 0:c], bank[0:hi, 0:c], ACT.Copy, accum_out=stat[0:hi, 2, bass.ds(s, 1)])
                    act.activation(at(XS, s), bank[:, :], ACT.Copy).then_inc(T("fm_kept"), 1)
                nodes_scalar(act, S1, states)

            @block.sync
            def _(sp):
                nodes_sync(sp, S1, NA_ + NS)
        S1.done()

        def load_attributes(sp, T, s, par):
            for h in range(2):
                sp.dma_start(W[par][1][64 * h:64 * h + 2, :], a["attr"][:, bass.ds(s * SE + h * HW, HW)]).then_inc(T("eat"), 16)

        def load_weights(sp, T, w, par, s):
            for h in range(2):
                sp.dma_start(weight_rows[par][h:2 * w.shape[0]:2, :], w[:, bass.ds(s * SE + h * HW, HW)]).then_inc(T("weights"), 16)

        S2 = Sems("e_")
        with nc.Block() as block:
            @block.vector
            def _(dve):
                step = [0]

                def link(ins):
                    step[0] += 1
                    ins.then_inc(S2("dve"), 1)
                    dve.wait_ge(S2("dve"), step[0])

                for par in range(2):
                    link(dve.memset(W[par][1], 0.0))
                    dve.sem_inc(S2(f"eat_free{par}"), 1)
                link(dve.tensor_reduce(red[:, 0:2], stat[:, 2:4, :], AX, A.add))
                dve.nop().then_inc(S2("sums"), 1)
                dve.wait_ge(S2("folded"), 1)
                link(dve.tensor_copy(red[:, 2:4], P[0][:, 0:2]))
                dve.nop().then_inc(S2("means"), 1)
                dve.wait_ge(S2("mu"), 1)
                link(dve.tensor_scalar(vec[:, 9:11], P[1][:, 0:2], -1.0 / E, None, A.mult))
                dve.nop().then_inc(S2("mu_ready"), 1)

                def stream(s, par, k):
                    T = of(S2, par)
                    hi, c = (64, LASTC) if isinstance(s, int) else (128, HW)
                    yield 2
                    for side, mu in enumerate((mu_s, mu_d)):
                        dve.wait_ge(T(f"square{side}"), k)
                        dve.scalar_tensor_tensor(W[par][5 + side][0:hi, 0:c], P[4 * par + side][0:hi, 0:c], mu[0:hi, :],
                                                 W[par][3 + side][0:hi, 0:c], A.add, A.mult,
                                                 accum_out=stat[0:hi, 5 + 2 * side, bass.ds(s, 1)]).then_inc(T(f"cube{side}"), 1)
                pairs(dve, stream)
                for par in range(2):
                    dve.wait_ge(S2(f"cube1{par}"), NS // 2 + 1 - par)
                    dve.wait_ge(S2(f"square1{par}"), NS // 2 + 1 - par)
                link(dve.tensor_reduce(red[:, 4:8], stat[:, 4:8, :], AX, A.add))
                dve.nop().then_inc(S2("moment_sums"), 1)
                dve.wait_ge(S2("moments"), 1)
                m = red[:, 8:12]
                link(dve.tensor_scalar(m, P[0][:, 4:8], 1.0 / E, None, A.mult))
                link(dve.scalar_tensor_tensor(red[:, 12:16], m, -1.0, m, A.mult, A.max))
                dve.nop().then_inc(S2("abs"), 1)
                link(dve.tensor_scalar(red[:, 16:20], m, 0.0, None, A.is_gt))
                link(dve.tensor_scalar(red[:, 20:24], m, 0.0, None, A.is_lt))
                link(dve.tensor_tensor(red[:, 16:20], red[:, 16:20], red[:, 20:24], A.subtract))
                dve.wait_ge(S2("root"), 1)
                link(dve.tensor_tensor(red[:, 16:20], red[:, 16:20], red[:, 24:28], A.mult))
                link(dve.tensor_tensor(red[:, 16:20], red[:, 16:20], grad[:, :], A.mult))
                link(dve.tensor_reduce(red[:, 28:29], red[:, 16:20], AX, A.add))
                dve.nop().then_inc(S2("weighted"), 1)
                dve.wait_ge(S2("shifted"), 1)
                link(dve.tensor_copy(shift, P[0][:, 8:9]))

            @block.gpsimd
            def _(pool):
                pool.memset(small[:, 0, 0:4:2], 0.5).then_inc(S2("exponents"), 1)
                pool.memset(small[:, 0, 1:4:2], 1.0 / 3.0).then_inc(S2("exponents"), 1)
                pool.wait_ge(S2("exponents"), 2)
                pool.wait_ge(S2("abs"), 1)
                pool.tensor_tensor(red[:, 24:28], red[:, 12:16], small[:, 0, 0:4], A.pow).then_inc(S2("root"), 1)

            @block.tensor
            def _(pe):
                pe.wait_ge(S2("sums"), 1)
                pe.matmul(P[0][:, 0:2], fold[:, :], red[:, 0:2], start=True, stop=True).then_inc(S2("folded"), 1)
                pe.wait_ge(S2("means"), 1)
                pe.matmul(P[1][:, 0:2], wfc[:, :], red[:, 2:4], start=True, stop=True).then_inc(S2("mu"), 1)
                pe.wait_ge(S2("mu_ready"), 1)

                def stream(s, par, k):
                    T = of(S2, par)
                    bank = [P[4 * par + i] for i in range(3)]
                    yield 0
                    pe.matmul(bank[0][:, :], wfc[:, :], at(XS, s), start=True, stop=True).then_inc(T("z"), 1)
                    pe.matmul(bank[1][:, :], wfc[:, :], at(XD, s), start=True, stop=True).then_inc(T("z"), 1)
                    pe.matmul(bank[2][0:2, :], one_l[:, 0:2], at(XS, s), start=True, stop=False)
                    pe.matmul(bank[2][0:2, :], one_l[:, 2:4], at(XD, s), start=False, stop=False)
                    pe.wait_ge(T("eat"), k * 32)
                    pe.matmul(bank[2][0:2, :], one_l[:, 4:6], W[par][1], start=False, stop=True).then_inc(T("logit"), 1)
                    yield 3
                    pe.wait_ge(T("logit"), k)
                    pe.sem_inc(T("eat_free"), 1)
                    pe.wait_ge(T("cube1"), k)
                    pe.wait_ge(T("row"), k)
                pairs(pe, stream)
                pe.wait_ge(S2("moment_sums"), 1)
                pe.matmul(P[0][:, 4:8], fold[:, :], red[:, 4:8], start=True, stop=True).then_inc(S2("moments"), 1)
                pe.wait_ge(S2("weighted"), 1)
                pe.matmul(P[0][:, 8:9], total[:, :], red[:, 28:29], start=True, stop=True).then_inc(S2("shifted"), 1)

            @block.scalar
            def _(act):
                def stream(s, par, k):
                    T = of(S2, par)
                    hi, c = (64, LASTC) if isinstance(s, int) else (128, HW)
                    yield 1
                    act.wait_ge(T("z"), 2 * k)
                    for side, mu in enumerate((mu_s, mu_d)):
                        act.activation(W[par][3 + side][0:hi, 0:c], P[4 * par + side][0:hi, 0:c], ACT.Square, bias=mu[0:hi, :],
                                       accum_out=stat[0:hi, 4 + 2 * side, bass.ds(s, 1)]).then_inc(T(f"square{side}"), 1)
                    yield 2
                    act.wait_ge(T("logit"), k)
                    act.wait_ge(T("row_free"), k)
                    act.activation(W[par][2][0:2, :], P[4 * par + 2][0:2, :], ACT.Copy).then_inc(T("row"), 1)
                pairs(act, stream)

            @block.sync
            def _(sp):
                for par in range(2):
                    sp.sem_inc(S2(f"row_free{par}"), 1)

                def stream(s, par, k):
                    T = of(S2, par)
                    yield -1
                    sp.wait_ge(T("eat_free"), k)
                    load_attributes(sp, T, s, par)
                    yield 3
                    sp.wait_ge(T("row"), k)
                    sp.dma_start(logit1_d[bass.ds(s * SE, SE)].rearrange("(a c) -> a c", a=2), W[par][2][0:2, :]).then_inc(T("stored"), 16)
                    yield 5
                    sp.wait_ge(T("stored"), k * 16)
                    sp.sem_inc(T("row_free"), 1)
                pairs(sp, stream)
        S2.done()

        SF = Sems("f_")
        with nc.Block() as block:
            softmax_rows(block, SF, logit1_d, weight1_d, 1, 0.01, False)
        SF.done()

        S3 = Sems("g_")
        with nc.Block() as block:
            @block.sync
            def _(sp):
                storing(sp, S3)

                def load(T, s, par, k):
                    yield 0
                    sp.wait_ge(T("in_free"), k)
                    load_attributes(sp, T, s, par)
                    load_weights(sp, T, weight1_d, par, s)
                pipelined(sp, S3, load, None, lambda T, s, par, k: store_table(sp, T, table[2], s, par, k, 6))
                all_stored(sp, S3)

            @block.tensor
            def _(pe):
                pe.wait_ge(S3("start"), 1)

                def message(T, s, par, k):
                    yield 0
                    pe.matmul(P[4 * par][:, :], wfc[:, :], at(XS, s), start=True, stop=False)
                    pe.wait_ge(T("eat"), k * 32)
                    pe.wait_ge(T("weights"), k * 32)
                    pe.matmul(P[4 * par + 1][:, :], spread_all, weight_rows[par][0:2 * PARTS, :], start=True, stop=True).then_inc(T("weights_fm"), 1)
                    pe.matmul(P[4 * par][:, :], eprj[:, :], W[par][1], start=False, stop=True).then_inc(T("message"), 1)
                pipelined(pe, S3, None, message, partial(norm_pe, pe), partial(back_pe, pe))

            @block.vector
            def _(dve):
                for par in range(2):
                    dve.memset(W[par][1], 0.0).then_inc(S3("attr0"), 1)
                dve.wait_ge(S3("attr0"), 2)
                for par in range(2):
                    dve.sem_inc(S3(f"in_free{par}"), 1)
                dve.sem_inc(S3("start"), 1)
                zero_carry(dve, S3)

                def message(T, s, par, k):
                    V, F = W[par][8], W[par][7]
                    yield 3
                    dve.wait_ge(T("weights_kept"), k)
                    dve.wait_ge(T("message"), k)
                    dve.tensor_tensor(V, P[4 * par][:, :], W[par][0], A.mult).then_inc(T("v"), 1)
                    dve.wait_ge(T("v"), k)
                    dve.sem_inc(T("in_free"), 1)
                    seg_scan(dve, T, k, V, F, at(SAME, s), A.mult, A.add)
                    dve.tensor_tensor(W[par][4], at(XD, s), F, A.add).then_inc(T("u"), 1)
                keeping(dve, S3)
                pipelined(dve, S3, None, message, partial(norm_dve, dve), partial(back_dve, dve))

            @block.scalar
            def _(act):
                def message(T, s, par, k):
                    yield 1
                    act.wait_ge(T("weights_fm"), k)
                    act.activation(W[par][0], P[4 * par + 1][:, :], ACT.Copy).then_inc(T("weights_kept"), 1)
                pipelined(act, S3, None, message, partial(norm_act, act))
        S3.done()

        S4 = Sems("h_")
        with nc.Block() as block:
            @block.gpsimd
            def _(pool):
                gather_rounds(pool, S4, look_i, table[2])

            @block.vector
            def _(dve):
                pass_back(dve, S4)

            @block.tensor
            def _(pe):
                for par in range(2):
                    pe.sem_inc(S4(f"slot_free{par}"), 1)
                    pe.sem_inc(S4(f"read{par}"), 1)

                def body(s, par, k, n):
                    bank = P[4 * par:4 * par + 3]
                    pe.wait_ge(S4(f"read{par}"), k)
                    pe.wait_ge(S4(f"back_free{par}"), k + 1)
                    pe.matmul(bank[1][0:16, :], two_l[:, 16:32], at(XD, (NS - 1) - s), start=True, stop=True).then_inc(S4(f"dst_part{par}"), 1)
                    pe.wait_ge(S4(f"gathered{par}"), k * 128)
                    transpose4(pe, bank[0], GA[:, par, :]).then_inc(S4(f"fm{par}"), 1)
                    pe.wait_ge(S4(f"fm{par}"), k)
                    pe.sem_inc(S4(f"slot_free{par}"), 1)
                    pe.wait_ge(S4(f"fm_kept{par}"), k)
                    pe.matmul(bank[2][0:8, :], two_l[:, 0:8], at(XS, s), start=True, stop=True).then_inc(S4(f"src_part{par}"), 1)
                supers(pe, body)

            @block.scalar
            def _(act):
                def body(s, par, k, n):
                    keep_back(act, S4, s, par, n)
                    act.wait_ge(S4(f"fm{par}"), k)
                    act.activation(at(XS, s), P[4 * par][:, :], ACT.Copy).then_inc(S4(f"fm_kept{par}"), 1)
                    act.wait_ge(S4(f"row_free{par}"), k)
                    act.wait_ge(S4(f"dst_part{par}"), k)
                    act.activation(W[par][1][0:16, :], P[4 * par + 1][0:16, :], ACT.Copy)
                    act.wait_ge(S4(f"src_part{par}"), k)
                    act.activation(W[par][2][0:8, :], P[4 * par + 2][0:8, :], ACT.Copy).then_inc(S4(f"read{par}"), 1)
                supers(act, body)

            @block.sync
            def _(sp):
                for par in range(2):
                    sp.sem_inc(S4(f"row_free{par}"), 1)

                def stream(s, par, k):
                    T = of(S4, par)
                    yield 0
                    sp.wait_ge(T("read"), k + 1)
                    for h in range(2):
                        sp.dma_start(logit2_d[0:HEADS, bass.ds(s * SE + h * HW, HW)], W[par][2][h:8:2, :]).then_inc(T("stored"), 16)
                        sp.dma_start(logit2_d[HEADS:3 * HEADS, bass.ds(((NS - 1) - s) * SE + h * HW, HW)], W[par][1][h:16:2, :]).then_inc(T("stored"), 16)
                    yield 1
                    sp.wait_ge(T("stored"), k * 64)
                    sp.sem_inc(T("row_free"), 1)
                pairs(sp, stream)
        S4.done()

        SI = Sems("i_")
        with nc.Block() as block:
            softmax_rows(block, SI, logit2_d, weight2_d, HEADS, 0.2, True)
        SI.done()

        S5 = Sems("j_")
        WB = lambda par, g: P[4 * par + (1, 2, 1, 2, 3, 2, 3, 2)[g]][:, :]
        with nc.Block() as block:
            @block.sync
            def _(sp):
                storing(sp, S5)

                def load(T, s, par, k):
                    yield 0
                    sp.wait_ge(T("weights_free"), k)
                    load_weights(sp, T, weight2_d, par, s)
                pipelined(sp, S5, load, None, lambda T, s, par, k: store_table(sp, T, table[3], s, par, k, 6))
                all_stored(sp, S5)

            @block.vector
            def _(dve):
                zero_carry(dve, S5)

                def message(T, s, par, k):
                    F, V = W[par][7], W[par][8]
                    for g in range(2 * HEADS):
                        yield (1, 1, 1, 3, 3, 3, 5, 5)[g]
                        dve.wait_ge(T("weights_fm"), 2 * HEADS * (k - 1) + g + 1)
                        if g >= HEADS:
                            dve.wait_ge(T("head_sum"), 2 * HEADS * (k - 1) + g - HEADS + 1)
                        x = XS if g < HEADS else XD
                        dve.tensor_tensor(W[par][g % HEADS], at(x, s), WB(par, g), A.mult).then_inc(T("scaled"), 1)
                    seg_scan(dve, T, k, P[4 * par], F, at(SAME, s), A.mult, A.add)
                    dve.wait_ge(T("head_sum"), 2 * HEADS * k)
                    dve.scalar_tensor_tensor(V, P[4 * par + 1][:, :], bias2, F, A.add, A.add).then_inc(T("v"), 1)
                    dve.wait_ge(T("v"), k)
                    dve.tensor_tensor(W[par][4], V, at(XD, s), A.add).then_inc(T("u"), 1)
                keeping(dve, S5)
                pipelined(dve, S5, None, message, partial(norm_dve, dve), partial(back_dve, dve))

            @block.tensor
            def _(pe):
                for par in range(2):
                    pe.sem_inc(S5(f"weights_free{par}"), 1)

                def message(T, s, par, k):
                    base = 2 * HEADS * (k - 1)

                    def weights(g):
                        if g == 4:
                            pe.wait_ge(T("kept"), k)
                        pe.matmul(WB(par, g), spread_g(g), weight_rows[par], start=True, stop=True).then_inc(T("weights_fm"), 1)

                    yield 0
                    pe.wait_ge(T("weights"), k * 32)
                    weights(0)
                    weights(1)
                    for g in range(2 * HEADS):
                        yield (2, 2, 2, 4, 4, 4, 6, 6)[g]
                        pe.wait_ge(T("scaled"), base + g + 1)
                        if g + 2 < 2 * HEADS:
                            weights(g + 2)
                        pe.matmul(P[4 * par + g // HEADS][:, :], wh[g % HEADS][:, :], W[par][g % HEADS],
                                  start=(g % HEADS == 0), stop=(g % HEADS == HEADS - 1)).then_inc(T("head_sum"), 1)
                    pe.wait_ge(T("weights_fm"), base + 2 * HEADS)
                    pe.sem_inc(T("weights_free"), 1)
                pipelined(pe, S5, None, message, partial(norm_pe, pe), partial(back_pe, pe))

            @block.scalar
            def _(act):
                pipelined(act, S5, None, None, partial(norm_act, act))
        S5.done()

        S8 = Sems("p_")
        with nc.Block() as block:
            @block.vector
            def _(dve):
                pass_back(dve, S8)

            @block.scalar
            def _(act):
                supers(act, lambda s, par, k, n: keep_back(act, S8, s, par, n))
        S8.done()

        S6 = Sems("k_")
        with nc.Block() as block:
            @block.gpsimd
            def _(pool):
                def gather(s, par, k):
                    pool.wait_ge(S6(f"slot_free{par}"), k)
                    pool.tensor_copy(win[:, par, 0:8], look_i[:, bass.ds(s * 8, 8)]).then_inc(S6(f"window{par}"), 1)
                    pool.wait_ge(S6(f"window{par}"), k)
                    settle(pool, S6("settled"))
                    for j in range(8):
                        pool.indirect_dma_start(GA[:, par, j * D:(j + 1) * D], None, table[3],
                                                bass.IndirectOffsetOnAxis(ap=win[:, par, j:j + 1], axis=0)
                                                ).then_inc(S6(f"gathered{par}"), 16)

                def scatter(s, par, k):
                    pool.wait_ge(S6(f"emb{par}"), k)
                    pool.tensor_copy(win[:, par, 8:16], seg_i[:, bass.ds(s * 8, 8)]).then_inc(S6(f"seg_window{par}"), 1)
                    pool.wait_ge(S6(f"seg_window{par}"), k)
                    settle(pool, S6("settled"))
                    for j in range(8):
                        pool.indirect_dma_start(out, bass.IndirectOffsetOnAxis(ap=win[:, par, 8 + j:9 + j], axis=0),
                                                W[par][6][:, j * D:(j + 1) * D], None, bounds_check=N - 1, oob_is_err=False
                                                ).then_inc(S6(f"scattered{par}"), 16)

                gather(0, 0, 1)
                gather(1, 1, 1)
                with pool.Fori(0, NS // 2 - 1) as i:
                    for par in range(2):
                        gather(2 * i + 2 + par, par, i + 2)
                    for par in range(2):
                        scatter(2 * i + par, par, i + 1)
                gather(NS - 1, 0, NS // 2 + 1)
                scatter(NS - 3, 0, NS // 2)
                scatter(NS - 2, 1, NS // 2)
                scatter(NS - 1, 0, NS // 2 + 1)
                pool.wait_ge(S6("scattered0"), 128 * (NS // 2 + 1))
                pool.wait_ge(S6("scattered1"), 128 * (NS // 2))

            @block.vector
            def _(dve):
                zero_carry(dve, S6, -BIG)

                def stream(T, s, par, k):
                    NEG, FIN, Z0, MX = (W[par][i] for i in (0, 3, 8, 7))
                    yield 0
                    dve.tensor_scalar(NEG, at(SAME, s), -1.0, BIG, A.add, A.mult)
                    dve.memset(Z0, 0.0).then_inc(T("neg"), 1)
                    yield 5
                    dve.wait_ge(T("neg"), k)
                    dve.wait_ge(T("message"), k)
                    seg_scan(dve, T, k, P[4 * par], MX, NEG, A.add, A.max)
                    dve.tensor_scalar(MX, MX, b2, None, A.add).then_inc(T("b2"), 1)
                    dve.wait_ge(T("b2"), k)
                    dve.tensor_scalar(FIN, MX, -FMAX, FMAX, A.max, A.min).then_inc(T("clipped"), 1)
                    dve.wait_ge(T("clipped"), k)
                    dve.tensor_tensor(FIN.bitcast(I32), FIN, MX, A.is_equal).then_inc(T("finite"), 1)
                    dve.wait_ge(T("finite"), k)
                    settle(dve, S6("settled_dve"))
                    dve.copy_predicated(Z0, FIN.bitcast(I32), MX).then_inc(T("out3"), 1)
                    dve.wait_ge(T("out3"), k)
                    dve.tensor_tensor(W[par][4], Z0, at(XD, s), A.add).then_inc(T("u"), 1)
                pipelined(dve, S6, stream, lambda T, s, par, k: norm_dve(
                    dve, T, s, par, k, "scattered", 0 if isinstance(s, int) and s < 2 else 128 * (k - 1)), None, None)

            @block.tensor
            def _(pe):
                for par in range(2):
                    pe.sem_inc(S6(f"slot_free{par}"), 1)

                def stream(T, s, par, k):
                    bank = [P[4 * par + i][:, :] for i in range(2)]
                    yield 0
                    pe.wait_ge(T("gathered"), k * 128)
                    transpose4(pe, bank[0], GA[:, par, :]).then_inc(T("fm"), 1)
                    pe.matmul(bank[1], w1d[:, :], at(XD, s), start=True, stop=False)
                    pe.wait_ge(T("fm"), k)
                    pe.sem_inc(T("slot_free"), 1)
                    yield 2
                    pe.wait_ge(T("fm_kept"), k)
                    pe.matmul(bank[1], w1s[:, :], W[par][1], start=False, stop=True).then_inc(T("hidden_mm"), 1)
                    yield 4
                    pe.wait_ge(T("hidden"), k)
                    pe.matmul(bank[0], w2[:, :], W[par][2], start=True, stop=True).then_inc(T("message"), 1)
                def emb(T, s, par, k):
                    yield 0
                    pe.wait_ge(T("emb"), k)
                pipelined(pe, S6, stream, partial(norm_pe, pe), emb)

            @block.scalar
            def _(act):
                def stream(T, s, par, k):
                    yield 1
                    act.wait_ge(T("fm"), k)
                    act.activation(W[par][1], P[4 * par][:, :], ACT.Copy).then_inc(T("fm_kept"), 1)
                    yield 3
                    act.wait_ge(T("hidden_mm"), k)
                    act.activation(W[par][2], P[4 * par + 1][:, :], ACT.Relu, bias=b1).then_inc(T("hidden"), 1)
                pipelined(act, S6, stream, partial(norm_act, act))


def kernel(**inputs):
    import concourse.bacc as bacc
    from concourse.bass_utils import run_bass_kernel_spmd

    x = {k: np.ascontiguousarray(v) for k, v in inputs.items()}
    src, dst = x["src"], x["dst"]
    pad = EP - E
    src_p = np.concatenate([src, np.zeros(pad, np.int32)])
    dst_p = np.concatenate([np.full(1, -1, np.int32), dst, np.full(pad, N, np.int32), np.full(1, N + 1, np.int32)])

    def columns(v):
        return np.ascontiguousarray(v.reshape(NS, 2, 4, 128).transpose(3, 0, 2, 1).reshape(128, NS * 8))

    half = np.kron(np.eye(2, dtype=np.float32), np.ones((D, D), np.float32))
    eye = np.eye(128, dtype=np.float32)
    const = np.concatenate([eye, eye - half / D, half, np.kron(np.ones((2, 2), np.float32), np.eye(D, dtype=np.float32)),
                            np.ones((128, 128), np.float32)], axis=1).astype(np.float32)
    row = np.arange(PARTS * 4 * HEADS)[:, None]
    to_half = row % 2 == np.arange(128)[None] // D
    spread = np.concatenate([to_half & (row // 2 % (2 * HEADS) == g) for g in range(2 * HEADS)] + [to_half], axis=1)
    attr = np.zeros((2, EP), np.float32)
    attr[:, :E] = x["edge_attr_2"].T
    wa = x["L1_gnn_W_attn"][0]
    arrays = {
        "x": x["x"], "src_l": columns(src_p), "dst_l": columns(dst_p[1:EP + 1]), "next_l": columns(dst_p[2:EP + 2]),
        "dst_pad": dst_p, "attr": attr, "const": const, "spread": spread.astype(np.float32),
        "proj": x["L0_gnn_proj_cosim"], "wffnT": x["L0_gnn_W_ffn"].T, "b_ffn": x["L0_gnn_b_ffn"],
        "wfcT": x["L1_gnn_W_fc"].T, "wfc": x["L1_gnn_W_fc"], "blkT": wa[:6 * D].reshape(6, D).T, "we": wa[6 * D:].reshape(2, 1),
        "wedge": x["L1_gnn_W_edge"], "we2nT": x["L1_gnn_W_e2n"].T, "wm1": x["L1_gnn_W_m1"], "wm2": x["L1_gnn_W_m2"],
        "w2l": x["L2_gnn_W"], "att": np.concatenate([x["L2_gnn_att_src"].ravel(), x["L2_gnn_att_dst"].ravel()]),
        "bias2": x["L2_gnn_bias"],
        "w1a": x["L3_gnn_W1"][:D], "w1b": x["L3_gnn_W1"][D:], "b1": x["L3_gnn_b1"], "w2": x["L3_gnn_W2"], "b2": x["L3_gnn_b2"],
    }
    nc = bacc.Bacc("TRN2", target_bir_lowering=False, num_devices=1)
    given, aps = {}, {}
    for name, v in arrays.items():
        v = np.ascontiguousarray(v)
        given[f"in_{name}"] = v
        aps[name] = nc.dram_tensor(f"in_{name}", v.shape, mybir.dt.from_np(v.dtype), kind="ExternalInput").ap()
    out = nc.dram_tensor("out_x", [N, D], F32, kind="ExternalOutput").ap()
    build(nc, aps, out)
    return run_bass_kernel_spmd(nc, [given], core_ids=[0]).results[0]["out_x"]
```
